# Optimizing a Trainium2 kernel written in Bass

```python
import numpy as np
import jax
import jax.numpy as jnp

def _softmax(x, axis=-1):
    return jax.nn.softmax(x, axis=axis)

def _gelu(x):
    return jax.nn.gelu(x, approximate=True)

def _silu(x):
    return jax.nn.silu(x)

def _sigmoid(x):
    return jax.nn.sigmoid(x)

def _layernorm(x, axis=-1, eps=1e-05):
    m = jnp.mean(x, axis=axis, keepdims=True)
    v = jnp.var(x, axis=axis, keepdims=True)
    return (x - m) / jnp.sqrt(v + eps)

def _scatter_add(tgt, idx, src, axis=0):
    return tgt.at[idx].add(src)

def _segment_sum(src, seg, n):
    return jax.ops.segment_sum(src, seg, n)
kernel_name = 'mk_xattn_ffn_d2_seqx_r4_332004'

def setup_inputs(seed: int=0):
    np.random.seed(seed)
    _w = jnp.asarray

    def _rec_inputs():
        import jax
        import jax.numpy as jnp
        _rk = jax.random.key(seed)
        x = -0.0002928 + 1 * jax.random.normal(jax.random.fold_in(_rk, 1), (2, 512, 256), jnp.float32)
        _lenS = 512 - jax.random.randint(jax.random.fold_in(_rk, 7), (2,), 0, max(1, 512 // 4) + 1, jnp.int32)
        _lenS2 = 1024 - jax.random.randint(jax.random.fold_in(_rk, 8), (2,), 0, max(1, 1024 // 4) + 1, jnp.int32)
        _ctx_1024P = jax.random.normal(jax.random.fold_in(_rk, 11), (2, 16, 256), jnp.float32)
        _ctx_1024c = jax.random.dirichlet(jax.random.fold_in(_rk, 511), 0.3 * jnp.ones((16,), jnp.float32), (2, 1024))
        _ctx_1024t = jnp.einsum('bsk,bkd->bsd', _ctx_1024c, _ctx_1024P)
        _ctx_1024t = _ctx_1024t * jax.lax.rsqrt(jnp.mean(jnp.square(_ctx_1024t)) + 1e-12) * 0.953939
        ctx_1024 = -1.39393e-06 + 0.999914 * (_ctx_1024t + 0.3 * jax.random.normal(jax.random.fold_in(_rk, 611), (2, 1024, 256), jnp.float32))
        _validS = jnp.arange(512)[None, :] < _lenS[:, None]
        _validS2 = jnp.arange(1024)[None, :] < _lenS2[:, None]
        _causal = jnp.tril(jnp.ones((512, 512), dtype=bool))
        mask_1x1xSxS2_ik0 = jnp.where(jnp.broadcast_to(_validS2[0:1, None, None, :], (1, 1, 512, 1024)), 0, 1).astype(jnp.int32)
        mask_BxSxS2_bk0 = jnp.logical_not(jnp.broadcast_to(_validS2[:, None, :], (2, 512, 1024)))
        return (x, ctx_1024, mask_1x1xSxS2_ik0, mask_BxSxS2_bk0)
    x, ctx_1024, mask_1x1xSxS2_ik0, mask_BxSxS2_bk0 = _rec_inputs()

    def _L0_xattn_setup():
        import jax, jax.numpy as jnp
        import numpy as np
        D_MODEL = 256
        NUM_HEADS = 16
        HEAD_DIM = D_MODEL // NUM_HEADS
        B, S = (2, 512)
        key = jax.random.key(seed)
        ks = jax.random.split(key, 12)
        s = 0.02
        inp = {'Q': jax.random.normal(ks[0], (B, S, D_MODEL), jnp.float32), 'K': jax.random.normal(ks[1], (B, S, D_MODEL), jnp.float32), 'V': jax.random.normal(ks[2], (B, S, D_MODEL), jnp.float32), 'mask': jnp.tril(jnp.ones((S, S), jnp.int32))[None, None, :, :], 'Wq': jax.random.normal(ks[3], (D_MODEL, D_MODEL), jnp.float32) * s, 'bq': jnp.zeros((D_MODEL,), jnp.float32), 'Wk': jax.random.normal(ks[4], (D_MODEL, D_MODEL), jnp.float32) * s, 'bk': jnp.zeros((D_MODEL,), jnp.float32), 'Wv': jax.random.normal(ks[5], (D_MODEL, D_MODEL), jnp.float32) * s, 'bv': jnp.zeros((D_MODEL,), jnp.float32), 'Wo': jax.random.normal(ks[6], (D_MODEL, D_MODEL), jnp.float32) * s, 'bo': jnp.zeros((D_MODEL,), jnp.float32)}
        return inp
    _L0_xattn_all = _L0_xattn_setup()
    _L0_xattn_in = {k: v for k, v in _L0_xattn_all.items() if k in ('Wq', 'bq', 'Wk', 'bk', 'Wv', 'bv', 'Wo', 'bo')}
    del _L0_xattn_all

    def _L0_ffn_setup():
        import jax, jax.numpy as jnp
        import numpy as np
        B, T, E, C, H, G = (2, 512, 8, 256, 512, 16)
        key = jax.random.key(seed)
        ks = jax.random.split(key, 7)
        return {'hidden_states': jax.random.normal(ks[0], (B, T, C), jnp.float32), 'w_red': jax.random.normal(ks[1], (C, G), jnp.float32) * 0.02, 'wg': jax.random.normal(ks[2], (E, G), jnp.float32), 'W1': jax.random.normal(ks[3], (E, C, H), jnp.float32) * 0.02, 'b1': jax.random.normal(ks[4], (E, H), jnp.float32) * 0.02, 'W2': jax.random.normal(ks[5], (E, H, C), jnp.float32) * 0.02, 'b2': jax.random.normal(ks[6], (E, C), jnp.float32) * 0.02}
    _L0_ffn_all = _L0_ffn_setup()
    _L0_ffn_in = {k: v for k, v in _L0_ffn_all.items() if k in ('w_red', 'wg', 'W1', 'b1', 'W2', 'b2')}
    del _L0_ffn_all

    def _L1_xattn_setup():
        import jax, jax.numpy as jnp
        import numpy as np
        EPS = 1e-05
        NEG_BIAS = -1000000000.0
        N_HEADS = 16

        def layer_norm(x, gamma, beta):
            mu = jnp.mean(x, axis=-1, keepdims=True)
            var = jnp.mean(jnp.square(x - mu), axis=-1, keepdims=True)
            return (x - mu) * jax.lax.rsqrt(var + EPS) * gamma + beta

        def split_heads(x, n_heads):
            b, s, d = x.shape
            return x.reshape(b, s, n_heads, d // n_heads).transpose(0, 2, 1, 3)
        key = jax.random.key(seed)
        ks = jax.random.split(key, 12)
        B, S, D = (2, 512, 256)
        inp = {'query_antecedent': jax.random.normal(ks[0], (B, S, D), jnp.float32), 'key_antecedent': jax.random.normal(ks[1], (B, S, D), jnp.float32), 'value_antecedent': jax.random.normal(ks[2], (B, S, D), jnp.float32), 'mask': jnp.tril(jnp.ones((S, S), jnp.bool_))[None].repeat(B, axis=0), 'Wq': jax.random.normal(ks[3], (D, D), jnp.float32) * (1.0 / np.sqrt(D)), 'Wk': jax.random.normal(ks[4], (D, D), jnp.float32) * (1.0 / np.sqrt(D)), 'Wv': jax.random.normal(ks[5], (D, D), jnp.float32) * (1.0 / np.sqrt(D)), 'gq': jnp.ones((D,), jnp.float32), 'bq': jnp.zeros((D,), jnp.float32), 'gk': jnp.ones((D,), jnp.float32), 'bk': jnp.zeros((D,), jnp.float32), 'gv': jnp.ones((D,), jnp.float32), 'bv': jnp.zeros((D,), jnp.float32)}
        return inp
    _L1_xattn_all = _L1_xattn_setup()
    _L1_xattn_in = {k: v for k, v in _L1_xattn_all.items() if k in ('Wq', 'Wk', 'Wv', 'gq', 'bq', 'gk', 'bk', 'gv', 'bv')}
    del _L1_xattn_all

    def _L1_ffn_setup():
        import jax, jax.numpy as jnp
        import numpy as np
        H, I, E_ROUTED, TOP_K = (256, 704, 7, 2)
        B, S = (4, 512)

        def _expert(h, g, u, d):
            return jnp.einsum('...i,hi->...h', jax.nn.silu(h @ g.T) * (h @ u.T), d)
        key = jax.random.key(seed)
        ks = jax.random.split(key, 10)
        sc = 0.02
        return {'x': jax.random.normal(ks[0], (B, S, H), dtype=jnp.float32), 'sg': jax.random.normal(ks[1], (I, H), dtype=jnp.float32) * sc, 'su': jax.random.normal(ks[2], (I, H), dtype=jnp.float32) * sc, 'sd': jax.random.normal(ks[3], (H, I), dtype=jnp.float32) * sc, 'rg': jax.random.normal(ks[4], (E_ROUTED, I, H), dtype=jnp.float32) * sc, 'ru': jax.random.normal(ks[5], (E_ROUTED, I, H), dtype=jnp.float32) * sc, 'rd': jax.random.normal(ks[6], (E_ROUTED, H, I), dtype=jnp.float32) * sc, 'wr': jax.random.normal(ks[7], (E_ROUTED, H), dtype=jnp.float32) * sc, 'rb': jnp.zeros((E_ROUTED,), dtype=jnp.float32)}
    _L1_ffn_all = _L1_ffn_setup()
    _L1_ffn_in = {k: v for k, v in _L1_ffn_all.items() if k in ('sg', 'su', 'sd', 'rg', 'ru', 'rd', 'wr', 'rb')}
    del _L1_ffn_all
    return {'x': x, 'ctx_1024': ctx_1024, 'mask_1x1xSxS2_ik0': mask_1x1xSxS2_ik0, 'mask_BxSxS2_bk0': mask_BxSxS2_bk0, 'L0_xattn_Wq': _L0_xattn_in['Wq'], 'L0_xattn_bq': _L0_xattn_in['bq'], 'L0_xattn_Wk': _L0_xattn_in['Wk'], 'L0_xattn_bk': _L0_xattn_in['bk'], 'L0_xattn_Wv': _L0_xattn_in['Wv'], 'L0_xattn_bv': _L0_xattn_in['bv'], 'L0_xattn_Wo': _L0_xattn_in['Wo'], 'L0_xattn_bo': _L0_xattn_in['bo'], 'L0_ffn_w_red': _L0_ffn_in['w_red'], 'L0_ffn_wg': _L0_ffn_in['wg'], 'L0_ffn_W1': _L0_ffn_in['W1'], 'L0_ffn_b1': _L0_ffn_in['b1'], 'L0_ffn_W2': _L0_ffn_in['W2'], 'L0_ffn_b2': _L0_ffn_in['b2'], 'L1_xattn_Wq': _L1_xattn_in['Wq'], 'L1_xattn_Wk': _L1_xattn_in['Wk'], 'L1_xattn_Wv': _L1_xattn_in['Wv'], 'L1_xattn_gq': _L1_xattn_in['gq'], 'L1_xattn_bq': _L1_xattn_in['bq'], 'L1_xattn_gk': _L1_xattn_in['gk'], 'L1_xattn_bk': _L1_xattn_in['bk'], 'L1_xattn_gv': _L1_xattn_in['gv'], 'L1_xattn_bv': _L1_xattn_in['bv'], 'L1_ffn_sg': _L1_ffn_in['sg'], 'L1_ffn_su': _L1_ffn_in['su'], 'L1_ffn_sd': _L1_ffn_in['sd'], 'L1_ffn_rg': _L1_ffn_in['rg'], 'L1_ffn_ru': _L1_ffn_in['ru'], 'L1_ffn_rd': _L1_ffn_in['rd'], 'L1_ffn_wr': _L1_ffn_in['wr'], 'L1_ffn_rb': _L1_ffn_in['rb']}

def reference(x, ctx_1024, mask_1x1xSxS2_ik0, mask_BxSxS2_bk0, L0_xattn_Wq, L0_xattn_bq, L0_xattn_Wk, L0_xattn_bk, L0_xattn_Wv, L0_xattn_bv, L0_xattn_Wo, L0_xattn_bo, L0_ffn_w_red, L0_ffn_wg, L0_ffn_W1, L0_ffn_b1, L0_ffn_W2, L0_ffn_b2, L1_xattn_Wq, L1_xattn_Wk, L1_xattn_Wv, L1_xattn_gq, L1_xattn_bq, L1_xattn_gk, L1_xattn_bk, L1_xattn_gv, L1_xattn_bv, L1_ffn_sg, L1_ffn_su, L1_ffn_sd, L1_ffn_rg, L1_ffn_ru, L1_ffn_rd, L1_ffn_wr, L1_ffn_rb):
    import jax
    import jax.numpy as jnp

    def _L0_xattn_ref(Q, K, V, mask, Wq, bq, Wk, bk, Wv, bv, Wo, bo):
        import jax, jax.numpy as jnp
        import numpy as np
        D_MODEL = 256
        NUM_HEADS = 16
        HEAD_DIM = D_MODEL // NUM_HEADS
        B, S = (2, 512)
        b, sq, _ = Q.shape
        sk = K.shape[1]
        q = Q @ Wq.T + bq
        k = K @ Wk.T + bk
        v = V @ Wv.T + bv
        q = q.reshape(b, sq, NUM_HEADS, HEAD_DIM).transpose(0, 2, 1, 3)
        k = k.reshape(b, sk, NUM_HEADS, HEAD_DIM).transpose(0, 2, 1, 3)
        v = v.reshape(b, sk, NUM_HEADS, HEAD_DIM).transpose(0, 2, 1, 3)
        scores = jnp.einsum('bhqd,bhkd->bhqk', q, k) / jnp.sqrt(jnp.asarray(HEAD_DIM, q.dtype))
        scores = jnp.where(mask == 0, jnp.asarray(-jnp.inf, scores.dtype), scores)
        attn = jax.nn.softmax(scores, axis=-1)
        out = jnp.einsum('bhqk,bhkd->bhqd', attn, v)
        out = out.transpose(0, 2, 1, 3).reshape(b, sq, D_MODEL)
        return out @ Wo.T + bo

    def _L0_ffn_ref(hidden_states, w_red, wg, W1, b1, W2, b2):
        import jax, jax.numpy as jnp
        import numpy as np
        B, T, E, C, H, G = (2, 512, 8, 256, 512, 16)
        b, t, c = hidden_states.shape
        x = hidden_states.reshape(-1, c)
        x_red = x @ w_red
        wg_n = wg / jnp.maximum(jnp.linalg.norm(wg, axis=1, keepdims=True), 0.0001)
        logits = x_red @ wg_n.T
        gates = jax.nn.softmax(logits, axis=1)
        scores = jnp.max(gates, axis=1)
        idx = jnp.argmax(gates, axis=1)
        h = jnp.einsum('nc,ech->neh', x, W1) + b1[None]
        h = jnp.take_along_axis(h, idx[:, None, None], axis=1)[:, 0, :]
        h = jax.nn.gelu(h, approximate=False)
        o = jnp.einsum('nh,ehc->nec', h, W2) + b2[None]
        o = jnp.take_along_axis(o, idx[:, None, None], axis=1)[:, 0, :]
        o = o * scores[:, None]
        return o.reshape(b, t, c)

    def _L1_xattn_ref(query_antecedent, key_antecedent, value_antecedent, mask, Wq, Wk, Wv, gq, bq, gk, bk, gv, bv):
        import jax, jax.numpy as jnp
        import numpy as np
        EPS = 1e-05
        NEG_BIAS = -1000000000.0
        N_HEADS = 16

        def layer_norm(x, gamma, beta):
            mu = jnp.mean(x, axis=-1, keepdims=True)
            var = jnp.mean(jnp.square(x - mu), axis=-1, keepdims=True)
            return (x - mu) * jax.lax.rsqrt(var + EPS) * gamma + beta

        def split_heads(x, n_heads):
            b, s, d = x.shape
            return x.reshape(b, s, n_heads, d // n_heads).transpose(0, 2, 1, 3)
        q = layer_norm(query_antecedent @ Wq, gq, bq)
        k = layer_norm(key_antecedent @ Wk, gk, bk)
        v = layer_norm(value_antecedent @ Wv, gv, bv)
        qh, kh, vh = (split_heads(t, N_HEADS) for t in (q, k, v))
        dk = qh.shape[-1]
        sim = jnp.einsum('bhqd,bhkd->bhqk', qh / jnp.sqrt(jnp.float32(dk)), kh)
        bias = NEG_BIAS * (~mask).astype(sim.dtype)[:, None]
        masked = sim + bias
        weights = jax.nn.softmax(masked, axis=-1)
        outh = jnp.einsum('bhqk,bhkd->bhqd', weights, vh)
        B, H, S, dh = outh.shape
        out = outh.transpose(0, 2, 1, 3).reshape(B, S, H * dh)
        return out

    def _L1_ffn_ref(x, sg, su, sd, rg, ru, rd, wr, rb):
        import jax, jax.numpy as jnp
        import numpy as np
        H, I, E_ROUTED, TOP_K = (256, 704, 7, 2)
        B, S = (4, 512)

        def _expert(h, g, u, d):
            return jnp.einsum('...i,hi->...h', jax.nn.silu(h @ g.T) * (h @ u.T), d)
        shared_out = _expert(x, sg, su, sd)
        logits = x @ wr.T + rb
        probs = jax.nn.softmax(logits, axis=-1)
        scores, idx = jax.lax.top_k(probs, TOP_K)
        scores = scores / scores.sum(axis=-1, keepdims=True)
        w = jnp.sum(scores[..., None] * jax.nn.one_hot(idx, E_ROUTED, dtype=x.dtype), axis=-2)
        out = shared_out
        for e in range(E_ROUTED):
            out = out + w[..., e:e + 1] * _expert(x, rg[e], ru[e], rd[e])
        return out
    x = x + _L0_xattn_ref(_layernorm(x, axis=-1), ctx_1024, ctx_1024, mask_1x1xSxS2_ik0, L0_xattn_Wq, L0_xattn_bq, L0_xattn_Wk, L0_xattn_bk, L0_xattn_Wv, L0_xattn_bv, L0_xattn_Wo, L0_xattn_bo)
    x = x + _L0_ffn_ref(_layernorm(x, axis=-1), L0_ffn_w_red, L0_ffn_wg, L0_ffn_W1, L0_ffn_b1, L0_ffn_W2, L0_ffn_b2)
    x = x + _L1_xattn_ref(_layernorm(x, axis=-1), ctx_1024, ctx_1024, mask_BxSxS2_bk0, L1_xattn_Wq, L1_xattn_Wk, L1_xattn_Wv, L1_xattn_gq, L1_xattn_bq, L1_xattn_gk, L1_xattn_bk, L1_xattn_gv, L1_xattn_bv)
    x = x + _L1_ffn_ref(_layernorm(x, axis=-1), L1_ffn_sg, L1_ffn_su, L1_ffn_sd, L1_ffn_rg, L1_ffn_ru, L1_ffn_rd, L1_ffn_wr, L1_ffn_rb)
    return x

_drawn_inputs = setup_inputs


def setup_inputs(seed=0):
    import zlib

    import numpy as np

    out = dict(_drawn_inputs(seed))
    spreads = {'L0_xattn_bq': (0.0, 0.8),
     'L0_xattn_bk': (0.0, 2.0),
     'L0_xattn_bv': (0.0, 0.289),
     'L0_xattn_bo': (0.0, 0.1),
     'L1_xattn_gq': (1.0, 0.2),
     'L1_xattn_bq': (0.0, 0.504),
     'L1_xattn_gk': (1.0, 0.2),
     'L1_xattn_bk': (0.0, 2.0),
     'L1_xattn_gv': (1.0, 0.2),
     'L1_xattn_bv': (0.0, 0.1),
     'L1_ffn_rb': (0.0, 0.8)}
    factors = {'L0_xattn_Wq': 8.0,
     'L0_xattn_Wk': 8.0,
     'L0_ffn_w_red': 4.377,
     'L0_ffn_wg': 4.445,
     'L0_ffn_W1': 4.387,
     'L0_ffn_b1': 8.0,
     'L0_ffn_W2': 4.249,
     'L0_ffn_b2': 8.0,
     'L1_ffn_rg': 3.326,
     'L1_ffn_ru': 3.286,
     'L1_ffn_rd': 3.285,
     'L1_ffn_wr': 4.074,
     'L1_ffn_sg': 3.188,
     'L1_ffn_su': 2.946,
     'L1_ffn_sd': 2.91}
    for name, (base, spread) in spreads.items():
        noise = np.random.default_rng([zlib.crc32(name.encode()), seed]).standard_normal(out[name].shape)
        drawn = base * np.exp(spread * noise) if base else spread * noise
        out[name] = jnp.asarray(drawn.astype(out[name].dtype))
    for name, factor in factors.items():
        out[name] = (out[name] * factor).astype(out[name].dtype)
    return out
```

```python
from contextlib import ExitStack

import concourse.bass as bass
from concourse import mybir

F32 = mybir.dt.float32
BF16 = mybir.dt.bfloat16
I32 = mybir.dt.int32
U8 = mybir.dt.uint8
ALU = mybir.AluOpType
ACT = mybir.ActivationFunctionType
AX = mybir.AxisListType.X

D = 256
H = 16
HD = 16
NB = 2
S = 512
SK = 1024
NT = NB * S // 128
VW = HD + 1
E0, F0 = 8, 512
E1, F1 = 8, 704
NJ1 = 6
EPS = 1e-5
Q_PART = (0, 0, 0, 1, 1, 2)
K_PART = (0, 1, 2, 0, 1, 0)
NSTACK = 16 * len(Q_PART)


def build(nc, A, out):
    ctx = ExitStack()
    pe, dve, act, pool, sp = nc.tensor, nc.vector, nc.scalar, nc.gpsimd, nc.sync

    def sem(name):
        return ctx.enter_context(nc.semaphore(name))

    own = {id(pe): sem("s_pe"), id(dve): sem("s_dve"), id(act): sem("s_act"), id(pool): sem("s_pool")}
    count = {}
    seen = {}

    def inc(ins, s, n=1):
        ins.then_inc(s, n)
        count[id(s)] = count.get(id(s), 0) + n
        return (s, count[id(s)])

    def wait(eng, *tokens):
        for t in tokens:
            if t is None:
                continue
            if isinstance(t, list):
                wait(eng, *t)
                continue
            s, v = t
            if seen.get((id(eng), id(s)), 0) < v:
                eng.wait_ge(s, v)
                seen[(id(eng), id(s))] = v

    def done(eng, ins):
        return inc(ins, own[id(eng)])

    def V(ins):
        return done(dve, ins)

    def C(ins):
        return done(act, ins)

    def M(ins):
        return done(pe, ins)

    def G(ins):
        return done(pool, ins)

    def sb(name, shape, dt):
        return ctx.enter_context(nc.sbuf_tensor(name, shape, dt))

    dsem = {}

    def dma(eng, name, dst, src, **kw):
        if name not in dsem:
            dsem[name] = sem("d_" + name)
        return inc(eng.dma_start(dst, src, **kw), dsem[name], 16)

    X = sb("X", [128, NT, D], F32)
    XN = sb("XN", [128, NT, D], F32)
    XT = sb("XT", [128, 2, NT * 128], F32)
    CT = sb("CT", [128, 2, NB * SK], F32)
    FE = sb("FE", [128, 2, 1024], F32)
    SP = sb("SP", [128, 3, 2, 1024], BF16)
    QS = sb("QS", [128, H, NB * S], BF16)
    KS = sb("KS", [128, H, SK], BF16)
    VV = sb("VV", [128, 8, H, VW], F32)
    MV = sb("MV", [128, 16, 2], F32)
    ST = sb("ST", [128, 16, 6], F32)
    NW = sb("NW", [128, 5, 16], F32)
    ident = sb("ident", [128, 128], F32)
    WP = sb("WP", [128, 4, 2, D], F32)
    BC = sb("BC", [128, 8, D], F32)
    bcol = sb("bcol", [128, 2, 2], F32)
    SM = sb("SM", [128, 2, SK], F32)
    MB = sb("MB", [128, SK], F32)
    MI = sb("MI", [128, SK], I32)
    MU = MI[:, 0:SK // 4].bitcast(U8)
    mx = sb("mx", [128, 2, H], F32)
    nmx = sb("nmx", [128, H], F32)
    okr = sb("okr", [128, H], F32)
    rl = sb("rl", [128, H], F32)
    ACC = sb("ACC", [128, NT, D], F32)
    HB = sb("HB", [128, 2, F1], F32)
    HT = sb("HT", [128, 2, NJ1, 128], F32)
    WU = QS[:, :, :].rearrange("p h n -> p (h n)").bitcast(F32)[:, 0:8 * F1].rearrange("p (s k n) -> p s k n", s=2, k=2)
    WD = KS[:, :, :].rearrange("p h n -> p (h n)").bitcast(F32)[:, 0:2 * NJ1 * D].rearrange("p (s k n) -> p s k n", s=2, k=NJ1)
    B1 = sb("B1", [128, 2, F0], F32)
    B2 = sb("B2", [128, 2, D], F32)
    iota_e = sb("iota_e", [128, E0], F32)
    LG = sb("LG", [128, NT, E0], F32)
    R1 = sb("R1", [128, NT, E0], F32)
    R2 = sb("R2", [128, NT, E0], F32)
    OH = sb("OH", [128, 2, NT, E0], F32)
    GW = sb("GW", [128, NT, E0], F32)
    rs = sb("rs", [128, 6, NT], F32)
    wred = sb("wred", [128, 2, 16], F32)
    wr = sb("wr", [128, 2, E1 - 1], F32)
    rbb = sb("rbb", [128, E1 - 1], F32)
    xrT = sb("xrT", [16, NB * S], F32)
    wg = sb("wg", [8, 16], F32)
    wgs = sb("wgs", [8, 8], F32)
    wgn = sb("wgn", [8, 16], F32)
    wgT = sb("wgT", [16, 8], F32)

    PS = ctx.enter_context(nc.psum_tensor("PS", [128, 8, 512], F32))
    sd_q = nc.dram_tensor("scratch_q", [3, D, 1024], BF16).ap()
    sd_k = nc.dram_tensor("scratch_k", [3, D, 1024], BF16).ap()

    PT = AT = PV_T = None
    rel = [None] * 8

    def bb(ap, n):
        return ap.unsqueeze(2).to_broadcast([ap.shape[0], ap.shape[1], n])

    t_x = dma(sp, "x", X[:, :, :], A["x"].rearrange("(t p) c -> p t c", p=128))
    t_ct = dma(act, "ct", CT[:, :, :], A["ctxT"].rearrange("(k p) n -> p k n", p=128))

    def row_bc(ap):
        return ap.rearrange("(a n) -> a n", a=1).to_broadcast([128, ap.shape[0]])

    def load_proj(l, after):
        wait(pool, after)
        t = None
        for i, n in enumerate(["WqT", "WkT", "WvT", "WoT"] if l == 0 else ["Wq", "Wk", "Wv"]):
            t = dma(pool, "wp", WP[:, i, :, :], A[f"L{l}_xattn_{n}"].rearrange("(k p) n -> p k n", p=128))
        if l == 0:
            for i, n in enumerate(["bq", "bk"]):
                t = dma(pool, "wp", bcol[:, i, :], A[f"L0_xattn_{n}"].rearrange("(k p) -> p k", p=128), allow_slow_non_contiguous=True)
            for i, n in enumerate(["bv", "bo"]):
                t = dma(pool, "wp", BC[:, i, :], row_bc(A[f"L0_xattn_{n}"]))
        else:
            for i, n in enumerate(["gq", "bq", "gk", "bk", "gv", "bv"]):
                t = dma(pool, "wp", BC[:, i, :], row_bc(A[f"L1_xattn_{n}"]))
        return t

    t_wp = load_proj(0, None)
    t_small = [
        dma(pool, "small", wred[:, :, :], A["L0_ffn_w_red"].rearrange("(k p) g -> p k g", p=128)),
        dma(pool, "small", wg[:, :], A["L0_ffn_wg"]),
        dma(pool, "small", wr[:, :, :], A["L1_ffn_wrT"].rearrange("(k p) g -> p k g", p=128), allow_slow_non_contiguous=True),
        dma(pool, "small", rbb[:, :], row_bc(A["L1_ffn_rb"])),
    ]
    t_id0 = G(pool.memset(ident[:, :], 0.0))
    wait(pool, t_id0)
    t_id = G(pool.affine_select(out=ident[:, :], in_=ident[:, :], compare_op=ALU.not_equal, fill=1.0, base=0,
                                pattern=[[-1, 128]], channel_multiplier=1))
    t_small = t_small[-1]
    t_iota = G(pool.iota(iota_e[:, :], pattern=[[1, E0]], base=0, channel_multiplier=0,
                         allow_small_or_imprecise_dtypes=True))
    t_ones = V(dve.memset(VV[:, :, :, HD:VW], 1.0))

    def rsqrt(n, t_var, var, eps):
        a, b, y, t = (NW[:, i, 0:n] for i in range(4))
        wait(dve, t_var)
        V(dve.tensor_scalar(a, var, eps, -0.5, ALU.add, ALU.mult))
        wait(dve, V(dve.tensor_scalar(b, var, eps, None, ALU.add)))
        wait(dve, V(dve.tensor_scalar(y.bitcast(I32), b.bitcast(I32), -0.5, float(0x5F3759DF), ALU.mult, ALU.add)))
        for _ in range(4):
            wait(dve, V(dve.tensor_tensor(t, y, y, ALU.mult)))
            wait(dve, V(dve.tensor_tensor(t, t, a, ALU.mult)))
            last = V(dve.scalar_tensor_tensor(y, t, 1.5, y, ALU.add, ALU.mult))
            wait(dve, last)
        return y, last

    def layernorm(srcs, dsts, t_src):
        n = len(srcs)
        wait(dve, t_src)
        for i, s in enumerate(srcs):
            t = V(dve.bn_stats(ST[:, i, :], s))
        wait(dve, t)
        for i in range(n):
            t = V(dve.bn_aggr(MV[:, i, :], ST[:, i, :]))
        y, _ = rsqrt(n, t, MV[:, 0:n, 1], EPS)
        toks = []
        for i, (s, d) in enumerate(zip(srcs, dsts)):
            toks.append(V(dve.tensor_scalar(d, s, MV[:, i, 0:1], y[:, i:i + 1], ALU.subtract, ALU.mult)))
        return toks

    state = {"alt": 0}

    def evac(dst, src, t):
        state["alt"] ^= 1
        if state["alt"]:
            wait(act, t)
            return C(act.activation(dst, src, ACT.Copy))
        wait(dve, t)
        return V(dve.tensor_copy(dst, src))

    def transpose_blocks(src_of, ntile, dstT, toks, bank0=0):
        outs = []
        for t in range(ntile):
            bk = bank0 + t % 2
            wait(pe, t_id, toks[t], rel[bk])
            for k in range(2):
                m = pe.transpose(PS[:, bk, k * 128:(k + 1) * 128], src_of(t)[:, k * 128:(k + 1) * 128], ident[:, :])
            tk = M(m)
            rel[bk] = evac(dstT[:, :, t * 128:(t + 1) * 128], PS[:, bk, 0:256].rearrange("p (k n) -> p k n", k=2), tk)
            outs.append(rel[bk])
        return outs

    def split_store(n, t_f, sd, dst, parts):
        wait(dve, t_f)
        wait(dve, state.get("sp_free"))
        f = FE[:, :, 0:n]
        t = V(dve.tensor_copy(SP[:, 0, :, 0:n], f))
        wait(dve, t)
        t = V(dve.tensor_tensor(f, f, SP[:, 0, :, 0:n], ALU.subtract))
        wait(dve, t)
        t = V(dve.tensor_copy(SP[:, 1, :, 0:n], f))
        wait(dve, t)
        t = V(dve.tensor_tensor(f, f, SP[:, 1, :, 0:n], ALU.subtract))
        wait(dve, t)
        t = V(dve.tensor_copy(SP[:, 2, :, 0:n], f))
        state["fe_free"] = t
        wait(sp, t)
        for s in range(3):
            tw = dma(sp, "split_out", sd[s].rearrange("(k p) n -> p k n", p=128)[:, :, 0:n], SP[:, s, :, 0:n])
        state["sp_free"] = tw
        wait(sp, tw)
        wait(sp, state.get("stack_free"))
        for i, s in enumerate(parts):
            td = dma(sp, "stack_in", dst[16 * i:16 * i + 16, :, 0:n],
                     sd[s].rearrange("(h d) n -> d h n", d=HD)[:, :, 0:n])
        return td

    def proj_T(i, src, n, bias, scale, t_src):
        toks = []
        for fb in range(2):
            for c in range(0, n, 512):
                bk = 2 + (fb * (n // 512) + c // 512) % 2
                wait(pe, t_wp, t_src, rel[bk])
                for k in range(2):
                    m = pe.matmul(PS[:, bk, :], WP[:, i, k, fb * 128:(fb + 1) * 128], src[:, k, c:c + 512],
                                  start=(k == 0), stop=(k == 1))
                tk = M(m)
                wait(dve, tk, state.get("fe_free"))
                rel[bk] = V(dve.tensor_scalar(FE[:, fb, c:c + 512], PS[:, bk, :], bias[:, fb:fb + 1], scale,
                                              ALU.add, ALU.mult))
                toks.append(rel[bk])
        return toks

    def proj_rows(i, src, cols, bank, t_src):
        wait(pe, t_wp, t_src, rel[bank])
        for j, c in enumerate(cols):
            for k in range(2):
                m = pe.matmul(PS[:, bank, j * 256:(j + 1) * 256], src[:, k, c:c + 128], WP[:, i, k, :],
                              start=(k == 0), stop=(k == 1))
        return M(m)

    def norm_proj(i, g, src, cols, dsts, t_src):
        toks = []
        for c in range(0, len(cols), 4):
            part = cols[c:c + 4]
            tks = [proj_rows(i, src, part[0:2], 4, t_src), proj_rows(i, src, part[2:4], 5, t_src)]
            srcs = [PS[:, 4 + j // 2, (j % 2) * 256:(j % 2 + 1) * 256] for j in range(4)]
            tn = layernorm(srcs, [XN[:, j, :] for j in range(4)], tks)
            rel[4] = rel[5] = tn[-1]
            wait(dve, tn[-1])
            for j in range(4):
                t1 = V(dve.tensor_tensor(XN[:, j, :], XN[:, j, :], BC[:, g, :], ALU.mult))
            wait(dve, t1)
            for j in range(4):
                wait(dve, state.get("nd_free"))
                toks.append(V(dve.tensor_tensor(dsts(c + j), XN[:, j, :] if i != 2 else XN[:, j, :].rearrange("p (h d) -> p h d", d=HD),
                                                BC[:, g + 1, :] if i != 2 else BC[:, g + 1, :].rearrange("p (h d) -> p h d", d=HD), ALU.add)))
        return toks

    def attention(l, t_in):
        nonlocal t_wp
        toks = layernorm([X[:, t, :] for t in range(NT)], [XN[:, t, :] for t in range(NT)], t_in)
        t_xt = transpose_blocks(lambda t: XN[:, t, :], NT, XT, toks)
        if l == 0:
            t_f = proj_T(0, XT, 1024, bcol[:, 0, :], 0.25, t_xt)
        else:
            tq = norm_proj(0, 0, XT, [128 * t for t in range(NT)], lambda j: ACC[:, j, :], t_xt)
            wait(act, state.get("fe_free"))
            wait(dve, state.get("fe_free"))
            t_f = transpose_blocks(lambda t: ACC[:, t, :], NT, FE, tq)
            wait(dve, t_f)
            t_f = V(dve.tensor_scalar(FE[:, :, :], FE[:, :, :], 0.25, None, ALU.mult))
        t_qs = split_store(1024, t_f, sd_q, QS, Q_PART)
        state["stack_free"] = None
        it = 0
        pv_last = None
        for b in range(NB):
            cols = [b * SK + 128 * k for k in range(8)]
            wait(pe, t_ct)
            if l == 0:
                t_f = proj_T(1, CT[:, :, b * SK:(b + 1) * SK], SK, bcol[:, 1, :], 1.0, t_ct)
            else:
                tq = norm_proj(1, 2, CT, cols, lambda j: ACC[:, j, :], t_ct)
                wait(act, state.get("fe_free"))
                wait(dve, state.get("fe_free"))
                t_f = transpose_blocks(lambda t: ACC[:, t, :], NT, FE, tq)
            t_ks = split_store(SK, t_f, sd_k, KS, K_PART)
            if l == 0:
                for c in range(0, 8, 2):
                    tk = proj_rows(2, CT, cols[c:c + 2], 4 + c // 2 % 2, t_ct)
                    wait(dve, tk, t_ones, pv_last)
                    for j in range(2):
                        t_v = V(dve.tensor_tensor(VV[:, c + j, :, 0:HD],
                                                  PS[:, 4 + c // 2 % 2, j * 256:(j + 1) * 256].rearrange("p (h d) -> p h d", d=HD),
                                                  BC[:, 0, :].rearrange("p (h d) -> p h d", d=HD), ALU.add))
                    rel[4 + c // 2 % 2] = t_v
            else:
                state["nd_free"] = pv_last
                t_v = norm_proj(2, 4, CT, cols, lambda j: VV[:, j, :, 0:HD], t_ct)[-1]
                state["nd_free"] = None
            for qb in range(4):
                t = b * 4 + qb
                if l == 0:
                    wait(sp, state.get("mi_free"))
                    t_m = dma(sp, "mask", MI[:, :], A["mask0"][qb * 128:(qb + 1) * 128, :])
                    msrc, mval = MI[:, :], -3.0e38
                else:
                    wait(sp, state.get("mi_free"))
                    t_m = dma(sp, "mask", MU, A["mask1"][b, qb * 128:(qb + 1) * 128, :])
                    msrc, mval = MU, -1.0e9
                wait(dve, t_m, state.get("mb_free"))
                t_mb = V(dve.tensor_scalar(MB[:, :], msrc, 0.0, mval, ALU.is_equal, ALU.mult))
                state["mi_free"] = t_mb
                t_exp = [None, None]
                prev = None

                def finish(h, p, t_e):
                    wait(pe, t_e, t_v)
                    for half in range(2):
                        bk = 4 + half
                        wait(pe, rel[bk])
                        for j in range(4):
                            kb = half * 4 + j
                            m = pe.transpose(PS[:, bk, j * 128:(j + 1) * 128], SM[:, p, kb * 128:(kb + 1) * 128], ident[:, :])
                        tk = M(m)
                        wait(act, state.get("pt_free"))
                        wait(dve, state.get("pt_free"))
                        rel[bk] = evac(HTv[:, half * 512:(half + 1) * 512], PS[:, bk, :], tk)
                    wait(pe, rel[4], rel[5], rel[6] if h == 0 else None)
                    for kb in range(8):
                        m = pe.matmul(PS[:, 6, h * VW:(h + 1) * VW], HTv[:, kb * 128:(kb + 1) * 128],
                                      VV[:, kb, h, :], start=(kb == 0), stop=(kb == 7))
                    state["pt_free"] = M(m)
                    return state["pt_free"]

                HTv = HT[:, :, :, :].rearrange("p a j n -> p (a j n)")
                for h in range(H):
                    p = h % 2
                    for half in range(2):
                        bk = 2 * p + half
                        wait(pe, t_qs, t_ks, rel[bk])
                        m = pe.matmul(PS[:, bk, :], QS[0:NSTACK, h, t * 128:(t + 1) * 128],
                                      KS[0:NSTACK, h, half * 512:(half + 1) * 512], start=True, stop=True)
                    tk = M(m)
                    wait(dve, tk, t_mb, state.get(("sm", p)))
                    wait(dve, state.get("mx_free"))
                    t_s = V(dve.tensor_tensor_reduce(out=SM[:, p, :], in0=PS[:, 2 * p:2 * p + 2, :].rearrange("p a n -> p (a n)"),
                                                     in1=MB[:, :], scale=1.0, scalar=-3.4e38, op0=ALU.add, op1=ALU.max,
                                                     accum_out=mx[:, 0, h:h + 1]))
                    rel[2 * p] = rel[2 * p + 1] = t_s
                    state["mb_free"] = t_s
                    wait(dve, t_s)
                    t_n = V(dve.tensor_scalar(nmx[:, h:h + 1], mx[:, 0, h:h + 1], -1.0, None, ALU.mult))
                    wait(act, t_s, t_n)
                    t_e = C(act.activation(SM[:, p, :], SM[:, p, :], ACT.Exp, bias=nmx[:, h:h + 1]))
                    if prev is not None:
                        state[("sm", 1 - p)] = finish(h - 1, 1 - p, prev)
                    prev = t_e
                state[("sm", 1)] = finish(H - 1, 1, prev)
                pv_last = state[("sm", 1)]
                state["mx_free"] = t_e
                wait(dve, pv_last)
                o = PS[:, 6, 0:H * VW].rearrange("p (h v) -> p h v", v=VW)
                if l == 0:
                    V(dve.tensor_scalar(okr[:, :], mx[:, 0, :], -1.0e38, None, ALU.is_gt))
                    wait(dve, V(dve.tensor_copy(rl[:, :], o[:, :, HD])))
                    wait(dve, V(dve.tensor_tensor(rl[:, :], rl[:, :], okr[:, :], ALU.mult)))
                else:
                    wait(dve, V(dve.tensor_copy(rl[:, :], o[:, :, HD])))
                wait(dve, V(dve.reciprocal(rl[:, :], rl[:, :])))
                t_o = V(dve.tensor_tensor(ACC[:, t, :].rearrange("p (h d) -> p h d", d=HD), o[:, :, 0:HD],
                                          bb(rl[:, :], HD), ALU.mult))
                rel[6] = t_o
                if l == 1:
                    wait(dve, t_o)
                    t_out = V(dve.tensor_tensor(X[:, t, :], X[:, t, :], ACC[:, t, :], ALU.add))
            state["stack_free"] = pv_last
        if l == 0:
            t_ot = transpose_blocks(lambda t: ACC[:, t, :], NT, XT, [t_o] * NT)
            for t in range(NT):
                tk = proj_rows(3, XT, [t * 128], 4 + t % 2, t_ot)
                wait(dve, tk)
                t1 = V(dve.tensor_tensor(ACC[:, t, :], PS[:, 4 + t % 2, 0:256], BC[:, 1, :], ALU.add))
                rel[4 + t % 2] = t1
                wait(dve, t1)
                t_out = V(dve.tensor_tensor(X[:, t, :], X[:, t, :], ACC[:, t, :], ALU.add))
        state["stack_free"] = None
        t_wp_free = [t_out, pv_last]
        if l == 0:
            t_wp = load_proj(1, t_wp_free)
        return [t_out, pv_last]

    def first_max(P, n, oh, mrow, idx, t_p):
        wait(dve, t_p)
        wait(dve, V(dve.tensor_reduce(mrow, P, AX, ALU.max)))
        r2 = R2[:, :, 0:n]
        wait(dve, V(dve.tensor_tensor(r2, P, bb(mrow, n), ALU.not_equal)))
        io = iota_e[:, 0:n].unsqueeze(1).to_broadcast([128, NT, n])
        wait(dve, t_iota)
        wait(dve, V(dve.scalar_tensor_tensor(r2, r2, 100.0, io, ALU.mult, ALU.add)))
        wait(dve, V(dve.tensor_reduce(idx, r2, AX, ALU.min)))
        t = V(dve.tensor_tensor(oh, r2, bb(idx, n), ALU.is_equal))
        wait(dve, t)
        return t

    def softmax_rows(n, t_l):
        lg, p = LG[:, :, 0:n], R1[:, :, 0:n]
        wait(dve, t_l)
        wait(dve, V(dve.tensor_reduce(rs[:, 0, :], lg, AX, ALU.max)))
        t = V(dve.tensor_tensor(lg, lg, bb(rs[:, 0, :], n), ALU.subtract))
        wait(act, t)
        wait(dve, C(act.activation(p, lg, ACT.Exp)))
        wait(dve, V(dve.tensor_reduce(rs[:, 1, :], p, AX, ALU.add)))
        wait(dve, V(dve.reciprocal(rs[:, 2, :], rs[:, 1, :])))
        wait(dve, V(dve.tensor_tensor(p, p, bb(rs[:, 2, :], n), ALU.mult)))
        return p

    def gates0(t_xt):
        wait(dve, t_small)
        wait(dve, V(dve.tensor_tensor(wgn[:, :], wg[:, :], wg[:, :], ALU.mult)))
        wait(dve, V(dve.tensor_reduce(wgs[:, 0:1], wgn[:, :], AX, ALU.add)))
        wait(dve, V(dve.tensor_scalar(wgs[:, 1:2], wgs[:, 0:1], 1e-8, None, ALU.max)))
        wait(dve, V(dve.tensor_scalar(wgs[:, 2:3].bitcast(I32), wgs[:, 1:2].bitcast(I32), -0.5, float(0x5F3759DF), ALU.mult, ALU.add)))
        for _ in range(4):
            wait(dve, V(dve.tensor_tensor(wgs[:, 3:4], wgs[:, 2:3], wgs[:, 2:3], ALU.mult)))
            wait(dve, V(dve.tensor_tensor(wgs[:, 3:4], wgs[:, 3:4], wgs[:, 1:2], ALU.mult)))
            wait(dve, V(dve.tensor_scalar(wgs[:, 3:4], wgs[:, 3:4], -0.5, 1.5, ALU.mult, ALU.add)))
            wait(dve, V(dve.tensor_tensor(wgs[:, 2:3], wgs[:, 2:3], wgs[:, 3:4], ALU.mult)))
        t = V(dve.tensor_scalar(wgn[:, :], wg[:, :], wgs[:, 2:3], None, ALU.mult))
        wait(pe, t, t_id, rel[0])
        tk = M(pe.transpose(PS[0:16, 0, 0:8], wgn[:, :], ident[0:8, 0:8]))
        wait(dve, tk)
        rel[0] = V(dve.tensor_copy(wgT[:, :], PS[0:16, 0, 0:8]))
        for c in range(2):
            wait(pe, t_xt, rel[1], t_small)
            for k in range(2):
                m = pe.matmul(PS[0:16, 1, :], wred[:, k, :], XT[:, k, c * 512:(c + 1) * 512], start=(k == 0), stop=(k == 1))
            wait(dve, M(m))
            rel[1] = V(dve.tensor_copy(xrT[:, c * 512:(c + 1) * 512], PS[0:16, 1, :]))
        wait(pe, rel[0], rel[1])
        for t in range(NT):
            m = pe.matmul(PS[:, 0, t * 8:(t + 1) * 8], xrT[:, t * 128:(t + 1) * 128], wgT[:, :], start=True, stop=True)
        wait(dve, M(m))
        rel[0] = V(dve.tensor_copy(LG[:, :, :], PS[:, 0, 0:64].rearrange("p (t e) -> p t e", e=8)))
        p = softmax_rows(E0, rel[0])
        first_max(p, E0, OH[:, 0, :, :], rs[:, 3, :], rs[:, 4, :], None)
        return V(dve.tensor_tensor(GW[:, :, :], OH[:, 0, :, :], bb(rs[:, 3, :], E0), ALU.mult))

    def gates1(t_xt):
        n = E1 - 1
        wait(pe, t_xt, rel[0], t_small)
        for t in range(NT):
            for k in range(2):
                m = pe.matmul(PS[:, 0, t * 8:t * 8 + n], XT[:, k, t * 128:(t + 1) * 128], wr[:, k, :],
                              start=(k == 0), stop=(k == 1))
        wait(dve, M(m), t_small)
        rel[0] = V(dve.tensor_tensor(LG[:, :, 0:n], PS[:, 0, 0:64].rearrange("p (t e) -> p t e", e=8)[:, :, 0:n],
                                     rbb[:, :].unsqueeze(1).to_broadcast([128, NT, n]), ALU.add))
        p = softmax_rows(n, rel[0])
        o1, o2 = OH[:, 0, :, 0:n], OH[:, 1, :, 0:n]
        first_max(p, n, o1, rs[:, 3, :], rs[:, 5, :], None)
        p2 = LG[:, :, 0:n]
        wait(dve, V(dve.scalar_tensor_tensor(p2, o1, -4.0, p, ALU.mult, ALU.add)))
        first_max(p2, n, o2, rs[:, 4, :], rs[:, 5, :], None)
        wait(dve, V(dve.tensor_tensor(rs[:, 0, :], rs[:, 3, :], rs[:, 4, :], ALU.add)))
        wait(dve, V(dve.reciprocal(rs[:, 0, :], rs[:, 0, :])))
        wait(dve, V(dve.tensor_tensor(o1, o1, o2, ALU.add)))
        wait(dve, V(dve.tensor_tensor(p, p, bb(rs[:, 0, :], n), ALU.mult)))
        return V(dve.tensor_tensor(GW[:, :, 1:E1], p, o1, ALU.mult))

    def ffn(l, t_in):
        nh = F0 if l == 0 else F1
        nj = nh // 128 + (nh % 128 > 0)
        ne = 8
        t_w = {}
        up_done, down_done = {}, {}

        def load(e):
            s = e % 2
            wait(sp, up_done.get(e - 2), down_done.get(e - 2), t_in if e < 2 else None)
            if l == 0:
                dma(sp, f"w{s}", WU[:, s, :, 0:F0], A["L0_ffn_W1"][e].rearrange("(k p) n -> p k n", p=128))
                dma(sp, f"w{s}", WD[:, s, 0:nj, :], A["L0_ffn_W2"][e].rearrange("(k p) n -> p k n", p=128))
                dma(sp, f"w{s}", B1[:, s, :], row_bc(A["L0_ffn_b1"][e]))
                t_w[e] = dma(sp, f"w{s}", B2[:, s, :], row_bc(A["L0_ffn_b2"][e]))
            else:
                g, u, d = ((A["sgT"], A["suT"], A["sdT"]) if e == 0 else
                           (A["rgT"][e - 1], A["ruT"][e - 1], A["rdT"][e - 1]))
                dma(sp, f"w{s}", WU[:, s, :, 0:F1], g.rearrange("(k p) n -> p k n", p=128))
                dma(sp, f"w{s}", WU[:, s, :, F1:2 * F1], u.rearrange("(k p) n -> p k n", p=128))
                dma(sp, f"w{s}", WD[:, s, 0:5, :], d[0:640, :].rearrange("(k p) n -> p k n", p=128))
                t_w[e] = dma(sp, f"w{s}", WD[0:64, s, 5, :], d[640:704, :])

        load(0)
        toks = layernorm([X[:, t, :] for t in range(NT)], [XN[:, t, :] for t in range(NT)], t_in)
        t_xt = transpose_blocks(lambda t: XN[:, t, :], NT, XT, toks)
        t_g = gates0(t_xt) if l == 0 else gates1(t_xt)
        items = [(e, t) for e in range(ne) for t in range(NT)]
        ht_free = [None, None]
        hb_free = [None, None]
        t_acc = [None]

        def up0(i, e, t):
            s, bk, p = e % 2, i % 2, i % 2
            wait(pe, t_xt, t_w[e], rel[bk])
            for k in range(2):
                m = pe.matmul(PS[:, bk, :], XT[:, k, t * 128:(t + 1) * 128], WU[:, s, k, 0:F0], start=(k == 0), stop=(k == 1))
            tk = M(m)
            wait(dve, tk, hb_free[p], t_w[e])
            t1 = V(dve.tensor_tensor(HB[:, p, 0:F0], PS[:, bk, :], B1[:, s, :], ALU.add))
            rel[bk] = t1
            wait(act, t1)
            return tk, C(act.activation(HB[:, p, 0:F0], HB[:, p, 0:F0], ACT.Gelu))

        def up1(i, e, t, which):
            s, p = e % 2, i % 2
            b0 = 2 * which
            wait(pe, t_xt, t_w[e], rel[b0], rel[b0 + 1])
            for half in range(2):
                for k in range(2):
                    m = pe.matmul(PS[:, b0 + half, 0:352], XT[:, k, t * 128:(t + 1) * 128],
                                  WU[:, s, k, which * F1 + half * 352:which * F1 + (half + 1) * 352],
                                  start=(k == 0), stop=(k == 1))
            tk = M(m)
            hb = HB[:, p, :].rearrange("p (a n) -> p a n", a=2)
            if which == 0:
                wait(act, tk, hb_free[p])
                tc = C(act.activation(hb, PS[:, 0:2, 0:352], ACT.Silu))
                rel[0] = rel[1] = tc
                return tk, tc
            wait(dve, tk, state["silu"])
            tc = V(dve.tensor_tensor(hb, hb, PS[:, 2:4, 0:352], ALU.mult))
            rel[2] = rel[3] = tc
            return tk, tc

        def turn(i, t_h):
            p = i % 2
            rows = [min(128, nh - 128 * j) for j in range(nj)]
            wait(pe, t_h, rel[4], rel[5])
            for j in range(nj):
                m = pe.transpose(PS[0:rows[j], 4 + j // 4, (j % 4) * 128:(j % 4 + 1) * 128],
                                 HB[:, p, j * 128:j * 128 + rows[j]], ident[:, :])
            tk = M(m)
            hb_free[p] = tk
            wait(act, tk, ht_free[p])
            ta = C(act.activation(HT[:, p, 0:4, :].rearrange("p j n -> p (j n)"), PS[:, 4, :], ACT.Copy))
            rel[4] = ta
            if nj > 4:
                wait(dve, tk, ht_free[p])
                tb = V(dve.tensor_copy(HT[:, p, 4, :], PS[:, 5, 0:128]))
                tb = V(dve.tensor_copy(HT[0:64, p, 5, :], PS[0:64, 5, 128:256]))
                rel[5] = tb
                return [ta, tb]
            return [ta]

        def down(i, e, t, t_h):
            s, p = e % 2, i % 2
            bk = 6 + i % 2
            wait(pe, t_h, rel[bk], t_w[e])
            for j in range(nj):
                r = min(128, nh - 128 * j)
                m = pe.matmul(PS[:, bk, 0:D], HT[0:r, p, j, :], WD[0:r, s, j, :], start=(j == 0), stop=(j == nj - 1))
            tk = M(m)
            ht_free[p] = tk
            wait(dve, tk, t_g)
            if l == 0:
                t1 = V(dve.tensor_tensor(ACC[:, t, :], PS[:, bk, 0:D], B2[:, s, :], ALU.add))
                rel[bk] = t1
                wait(dve, t1)
                t_acc[0] = V(dve.scalar_tensor_tensor(X[:, t, :], ACC[:, t, :], GW[:, t, e:e + 1], X[:, t, :], ALU.mult, ALU.add))
                return [tk, t_acc[0]]
            if e == 0:
                t_acc[0] = V(dve.tensor_tensor(X[:, t, :], PS[:, bk, 0:D], X[:, t, :], ALU.add))
            else:
                t_acc[0] = V(dve.scalar_tensor_tensor(X[:, t, :], PS[:, bk, 0:D], GW[:, t, e:e + 1], X[:, t, :], ALU.mult, ALU.add))
            rel[bk] = t_acc[0]
            return [tk, t_acc[0]]

        wait(dve, toks[-1])
        prev = None
        for i, (e, t) in enumerate(items):
            if t == 1 and e + 1 < ne:
                load(e + 1)
            if l == 0:
                tk, th = up0(i, e, t)
                if prev:
                    tt = turn(i - 1, prev[2])
            else:
                tk, tsil = up1(i, e, t, 0)
                state["silu"] = tsil
                if prev:
                    tt = turn(i - 1, prev[2])
                tk, th = up1(i, e, t, 1)
            up_done[e] = tk
            if prev:
                down_done[prev[0]] = down(i - 1, prev[0], prev[1], tt)
            prev = (e, t, th)
        tt = turn(i, prev[2])
        down(i, prev[0], prev[1], tt)
        return [t_acc[0], ht_free[0], ht_free[1]]

    t = attention(0, t_x)
    t = ffn(0, t)
    t = attention(1, t)
    t = ffn(1, t)
    wait(sp, t)
    t = dma(sp, "out", out.rearrange("(t p) c -> p t c", p=128), X[:, :, :])
    wait(sp, t)
    ctx.close()


def laid_out(i, np):
    c = np.ascontiguousarray
    a = {
        "x": c(i["x"]).reshape(NB * S, D),
        "ctxT": c(i["ctx_1024"].transpose(2, 0, 1)).reshape(D, NB * SK),
        "mask0": c(i["mask_1x1xSxS2_ik0"]).reshape(S, SK),
        "mask1": c(i["mask_BxSxS2_bk0"]),
    }
    for n in ("Wq", "Wk", "Wv", "Wo"):
        a[f"L0_xattn_{n}T"] = c(i[f"L0_xattn_{n}"].T)
    for n in ("L0_xattn_bq", "L0_xattn_bk", "L0_xattn_bv", "L0_xattn_bo", "L0_ffn_w_red", "L0_ffn_wg", "L0_ffn_W1",
              "L0_ffn_b1", "L0_ffn_W2", "L0_ffn_b2", "L1_xattn_Wq", "L1_xattn_Wk", "L1_xattn_Wv", "L1_xattn_gq",
              "L1_xattn_bq", "L1_xattn_gk", "L1_xattn_bk", "L1_xattn_gv", "L1_xattn_bv", "L1_ffn_rb"):
        a[n] = c(i[n])
    a["L1_ffn_wrT"] = c(i["L1_ffn_wr"].T)
    for n in ("sg", "su", "sd"):
        a[n + "T"] = c(i["L1_ffn_" + n].T)
    for n in ("rg", "ru", "rd"):
        a[n + "T"] = c(i["L1_ffn_" + n].transpose(0, 2, 1))
    return a


def kernel(**inputs):
    import numpy as np
    import concourse.bacc as bacc
    from concourse.bass_utils import run_bass_kernel_spmd

    nc = bacc.Bacc("TRN2", target_bir_lowering=False, num_devices=1)
    arrays = laid_out({k: np.asarray(v) for k, v in inputs.items()}, np)
    aps = {n: nc.dram_tensor("in_" + n, v.shape, mybir.dt.from_np(v.dtype), kind="ExternalInput").ap()
           for n, v in arrays.items()}
    out = nc.dram_tensor("out", [NB * S, D], F32, kind="ExternalOutput").ap()
    build(nc, aps, out)
    r = run_bass_kernel_spmd(nc, [{"in_" + n: v for n, v in arrays.items()}], core_ids=[0])
    return r.results[0]["out"].reshape(NB, S, D)
```

```python
from contextlib import ExitStack

import concourse.bass as bass
from concourse import mybir

F32 = mybir.dt.float32
BF16 = mybir.dt.bfloat16
I32 = mybir.dt.int32
U32 = mybir.dt.uint32
U8 = mybir.dt.uint8
ALU = mybir.AluOpType
ACT = mybir.ActivationFunctionType
AX = mybir.AxisListType.X

D = 256
H = 16
HD = 16
NB = 2
S = 512
SK = 1024
FK = 256
NT = NB * S // 128
VW = HD + 1
VT = H * VW + 16
E0, F0 = 8, 512
E1, F1 = 7, 704
NJ0, NJ1 = 4, 6
TILES0 = 15
TILES1 = 22
EPS = 1e-5
BIG = -3.0e38
SLOT = 2 * 2 * F1 + NJ1 * D
EXP0 = 2 * F0 + NJ0 * D
Q_PART = (0, 0, 0, 1, 1, 2)
K_PART = (0, 1, 2, 0, 1, 0)
NS = 16 * len(Q_PART)
MAGIC = float(0x5F3759DF)


def build(nc, A, out):
    ctx = ExitStack()
    pe, dve, act, pool, sp = nc.tensor, nc.vector, nc.scalar, nc.gpsimd, nc.sync
    engines = (pe, dve, act, pool, sp)

    def sem(name):
        return ctx.enter_context(nc.semaphore(name))

    def sb(name, shape, dt):
        return ctx.enter_context(nc.sbuf_tensor(name, shape, dt))

    state = {"queue": {id(e): [] for e in engines}, "branch": ""}
    segments = []
    count, seen, own = {}, {}, {}

    def put(eng, fn, *a, **k):
        item = [fn, a, k, []]
        state["queue"][id(eng)].append(item)
        return item

    def inc(item, s, n=1):
        item[3].append((s, n))
        count[id(s)] = count.get(id(s), 0) + n
        return (s, count[id(s)])

    def wait(eng, *tokens):
        for t in tokens:
            if isinstance(t, list):
                wait(eng, *t)
            elif t is not None and seen.get((id(eng), id(t[0])), 0) < t[1]:
                put(eng, eng.wait_ge, t[0], t[1])
                seen[(id(eng), id(t[0]))] = t[1]

    def own_sem(eng, name):
        key = (id(eng), state["branch"])
        if key not in own:
            own[key] = sem(f"s_{name}{state['branch']}")
        return own[key]

    def V(fn, *a, **k):
        return inc(put(dve, fn, *a, **k), own_sem(dve, "dve"))

    def C(fn, *a, **k):
        return inc(put(act, fn, *a, **k), own_sem(act, "act"))

    def M(fn, *a, **k):
        return inc(put(pe, fn, *a, **k), own_sem(pe, "pe"))

    def G(fn, *a, **k):
        return inc(put(pool, fn, *a, **k), own_sem(pool, "pool"))

    def VC(fn, *a, **k):
        t = V(fn, *a, **k)
        wait(dve, t)
        return t

    def seen_dve():
        s = own_sem(dve, "dve")
        return (s, count[id(s)])

    dsem = {}

    def dma(eng, name, dst, src, **kw):
        name = name + state["branch"]
        if name not in dsem:
            dsem[name] = sem("d_" + name)
        return inc(put(eng, eng.dma_start, dst, src, **kw), dsem[name], 16)

    def wdma(name, dst, src):
        if name not in dsem:
            dsem[name] = sem("d_" + name)
        return inc(put(sp, sp.dma_start, dst, src), dsem[name], 16)

    def issue(items):
        for fn, a, k, incs in items:
            ins = fn(*a, **k)
            for s, n in incs:
                ins.then_inc(s, n)

    def branch(flag, t_flag, fast, general):
        for e in engines:
            wait(e, t_flag)
        segments.append((state["queue"], None, None))
        before, known, rel0 = dict(count), dict(seen), list(rel)
        ways, after = [], []
        for name, body in (("_f", fast), ("_g", general)):
            state["queue"] = {id(e): [] for e in engines}
            state["branch"] = name
            count.clear()
            count.update(before)
            count.update({k: v for k, v in private.items()})
            seen.clear()
            seen.update(known)
            rel[:] = rel0
            wait(dve, body())
            t_join = inc(put(dve, dve.memset, junk[:, :], 0.0), s_join)
            ways.append(state["queue"])
            shared = {k: v for k, v in count.items() if k not in branch_sems()}
            private.update({k: v for k, v in count.items() if k in branch_sems()})
            after.append(shared)
            state["branch"] = ""
        assert after[0] == after[1], "the ways leave different counts"
        count.update(private)
        seen.clear()
        seen.update(known)
        rel[:] = [t_join] * 8
        segments.append((flag, ways[0], ways[1]))
        state["queue"] = {id(e): [] for e in engines}
        return t_join

    private = {}

    def branch_sems():
        return {id(s) for k, s in own.items() if k[1]} | {id(s) for k, s in dsem.items() if k.endswith(("_f", "_g"))}

    s_join = sem("s_join")

    X = sb("X", [128, NT, D], F32)
    XT = sb("XT", [128, 2, NT * 128], F32)
    CT = sb("CT", [128, 2 * SK], F32)
    CTf = CT[:, 0:1024].rearrange("p (k n) -> p k n", k=2)
    CTg = CT[:, :].rearrange("p (k n) -> p k n", k=2)
    OHE = CT[:, 1024:2048].bitcast(BF16)[:, 0:TILES0 * 128].rearrange("p (t n) -> p t n", n=128)
    PTg = CT[:, 0:1024]
    WP = sb("WP", [128, 4, 2, D], F32)
    BC = sb("BC", [128, 2, D], F32)
    col = sb("col", [128, 4, 2], F32)
    VR = sb("VR", [128, 8 * VT], F32)
    VV = VR[:, :].rearrange("p (t v) -> p t v", v=VT)
    HB = VR[:, 0:2 * F1].rearrange("p (a n) -> p a n", a=2)
    XL = VR[:, 2 * F1:2 * F1 + 2 * D].rearrange("p (a n) -> p a n", a=2)
    YO = VR[:, 2 * F1 + 2 * D:2 * F1 + 2 * D + D]
    PR = sb("PR", [128, 4096], F32)
    XN = PR[:, 0:2048].rearrange("p (t c) -> p t c", c=D)
    NR = PR[:, 2048:4096].rearrange("p (t c) -> p t c", c=D)
    HT = PR[:, 2048:2048 + 2 * NJ1 * 128].rearrange("p (a j n) -> p a j n", a=2, n=128)
    XS = PR[:, 3584:4096].rearrange("p (a k n) -> p a k n", a=2, k=2)
    SMg = PR[:, 0:2048].rearrange("p (a n) -> p a n", a=2)
    MBg = PR[:, 2048:3072]
    MIg = PR[:, 3072:4096].bitcast(I32)
    MUg = PR[:, 3072:3328].bitcast(U8)
    W = sb("W", [128, 8 * SLOT], F32)
    a0 = 4 * SLOT
    QS = W[:, a0:a0 + 8192].bitcast(BF16).rearrange("p (h n) -> p h n", h=H)
    KS = W[:, a0 + 8192:a0 + 12288].bitcast(BF16).rearrange("p (h n) -> p h n", h=H)
    QSg = W[:, a0:a0 + 4096].bitcast(BF16).rearrange("p (h n) -> p h n", h=H)
    KSg = W[:, a0 + 4096:a0 + 12288].bitcast(BF16).rearrange("p (h n) -> p h n", h=H)
    FE = W[:, a0 + 12288:a0 + 14336].rearrange("p (i k n) -> p i k n", i=2, k=2)
    SP = W[:, a0 + 14336:a0 + 17408].bitcast(BF16).rearrange("p (i s k n) -> p i s k n", i=2, s=3, k=2)
    OB = FE[:, :, :, :].rearrange("p i k n -> p i (k n)").rearrange("p i (q c) -> p i q c", c=D)
    PX = [PR[:, 1024 * i:1024 * (i + 1)] for i in range(4)] + \
         [W[:, a0 + 14336 + 1024 * i:a0 + 14336 + 1024 * (i + 1)] for i in range(2)]
    OS = W[:, a0 + 16384:a0 + 17408].rearrange("p (i n) -> p i n", i=2)
    xrT = W[0:16, a0 + 12288:a0 + 13312]
    m0i = PR[:, :].bitcast(I32).rearrange("p (q n) -> p q n", q=4)
    m1i = XT[:, :, :].rearrange("p k n -> p (k n)").bitcast(U8).rearrange("p (q n) -> p q n", q=8)
    mu = W[:, a0:a0 + 6144].bitcast(BF16).rearrange("p (q n) -> p q n", q=12)
    mc = W[:, a0 + 6144:a0 + 9216].rearrange("p (q n) -> p q n", q=3)
    mt = W[:, a0 + 9216:a0 + 12288].rearrange("p (q n) -> p q n", q=3)
    bsf = W[0:8, a0 + 12288:a0 + 12288 + 768]
    bsp = W[0:8, a0 + 14336:a0 + 14336 + 1152].bitcast(BF16).rearrange("p (s n) -> p s n", s=3)

    ident = sb("ident", [128, 128], F32)
    identb = sb("identb", [128, 128], BF16)
    upper = sb("upper", [128, 128], BF16)
    onesb = sb("onesb", [128, 128], BF16)
    BS = sb("BS", [24, 768], BF16)
    maskrow = W[0:1, a0 + 15616:a0 + 16128].bitcast(BF16).rearrange("p (l n) -> p l n", l=2)
    flags = sb("flags", [128, 2], I32)
    fsum = sb("fsum", [128, 8], F32)
    junk = sb("junk", [128, 1], F32)
    MV = sb("MV", [128, 16, 2], F32)
    ST = sb("ST", [128, 16, 6], F32)
    NW = sb("NW", [128, 5, 16], F32)
    mx = sb("mx", [128, 2, 4, H], F32)
    msb = sb("msb", [128, 2, 4, 3, H], BF16)
    MT = sb("MT", [48, 2, 512], BF16)
    rlf = sb("rlf", [128, 4, 4], F32)
    nmx = sb("nmx", [128, H], F32)
    okr = sb("okr", [128, H], F32)
    rl = sb("rl", [128, H], F32)
    iota_e = sb("iota_e", [128, 8], F32)
    iota_j = sb("iota_j", [128, 8], F32)
    iota_t = sb("iota_t", [128, TILES1], F32)
    rowe = sb("rowe", [24, 1], F32)
    LG = sb("LG", [128, NT, 8], F32)
    R1 = sb("R1", [128, NT, 8], F32)
    R2 = sb("R2", [128, NT, 8], F32)
    OH = sb("OH", [128, 3, NT, 8], F32)
    OHb = sb("OHb", [128, NT, 8], BF16)
    RK = sb("RK", [128, NT, 8], F32)
    CN = sb("CN", [128, NT, 8], F32)
    ne = sb("ne", [128, 4, 8], F32)
    nt8 = sb("nt8", [128, 8, 8], F32)
    te = sb("te", [128, TILES1, 8], F32)
    tef = sb("tef", [128, TILES1], F32)
    tei = sb("tei", [128, TILES1], I32)
    posf = sb("posf", [128, 2, NT], F32)
    posi = sb("posi", [128, 2, NT], I32)
    gw = sb("gw", [128, 2, NT], F32)
    rs = sb("rs", [128, 6, NT], F32)
    wred = sb("wred", [128, 2, 16], F32)
    wr = sb("wr", [128, 2, E1], F32)
    rbb = sb("rbb", [128, E1], F32)
    wg = sb("wg", [8, 16], F32)
    wgs = sb("wgs", [8, 8], F32)
    wgn = sb("wgn", [8, 16], F32)
    wgT = sb("wgT", [16, 8], F32)

    PS = ctx.enter_context(nc.psum_tensor("PS", [128, 8, 512], F32))
    sd = nc.dram_tensor("scratch_split", [2, 3, D, 512], BF16).ap()
    md = nc.dram_tensor("scratch_max", [2, 3, H, 512], BF16).ap()
    mr = nc.dram_tensor("scratch_mask", [2, NB * FK], BF16).ap()
    bd = nc.dram_tensor("scratch_bias", [3, 8, 768], BF16).ap()
    xs = nc.dram_tensor("scratch_x", [TILES1 * 128, D], F32).ap()
    ys = nc.dram_tensor("scratch_y", [TILES1 * 128, D], F32).ap()

    rel = [None] * 8

    def bb(ap, n):
        return ap.unsqueeze(len(ap.shape)).to_broadcast(list(ap.shape) + [n])

    def row_bc(ap):
        return ap.rearrange("(a n) -> a n", a=1).to_broadcast([128, ap.shape[0]])

    ev = [0]

    def evac(dst, src, t):
        ev[0] ^= 1
        if ev[0]:
            wait(act, t)
            return C(act.activation, dst, src, ACT.Copy)
        wait(dve, t)
        return V(dve.tensor_copy, dst, src)

    t_m0 = dma(sp, "m0", m0i, A["mask0"].rearrange("(q p) n -> p q n", p=128))
    t_m1 = dma(sp, "m1", m1i, A["mask1"].rearrange("b (q p) n -> p (b q) n", p=128))
    t_x = dma(sp, "x", X[:, :, :], A["x"].rearrange("(t p) c -> p t c", p=128))
    ctx_v = A["ctxT"].rearrange("(k p) (b n) -> p k b n", p=128, b=NB)
    t_ct = None
    for b in range(NB):
        t_ct = dma(act, "ct", CTf[:, :, b * FK:(b + 1) * FK], ctx_v[:, :, b, SK - FK:SK])

    def load_proj(l, after):
        wait(sp, after)
        for i, n in enumerate(["WkT", "WvT", "WqT", "WoT"] if l == 0 else ["Wk", "Wv", "Wq"]):
            t = dma(sp, "wp", WP[:, i, :, :], A[f"L{l}_xattn_{n}"].rearrange("(k p) n -> p k n", p=128))
        for i, n in enumerate(["bk", "bq"] if l == 0 else ["gk", "bk", "gq", "bq"]):
            t = dma(sp, "wp", col[:, i, :], A[f"L{l}_xattn_{n}"].rearrange("(k p) -> p k", p=128),
                    allow_slow_non_contiguous=True)
        for i, n in enumerate(["bv", "bo"] if l == 0 else ["gv", "bv"]):
            t = dma(sp, "wp", BC[:, i, :], row_bc(A[f"L{l}_xattn_{n}"]))
        return t

    t_wp = load_proj(0, None)
    dma(act, "small", wred[:, :, :], A["L0_ffn_w_red"].rearrange("(k p) g -> p k g", p=128))
    dma(act, "small", wg[:, :], A["L0_ffn_wg"])
    dma(act, "small", wr[:, :, :], A["L1_ffn_wrT"].rearrange("(k p) g -> p k g", p=128), allow_slow_non_contiguous=True)
    dma(act, "small", rbb[:, :], row_bc(A["L1_ffn_rb"]))
    dma(act, "small", bsf[:, 0:F0], A["L0_ffn_b1"])
    t_small = dma(act, "small", bsf[:, F0:F0 + D], A["L0_ffn_b2"])

    t = G(pool.memset, ident[:, :], 0.0)
    G(pool.memset, onesb[:, :], 1.0)
    t1 = G(pool.memset, upper[:, :], 1.0)
    wait(pool, t1)
    t_id = G(pool.affine_select, out=ident[:, :], in_=ident[:, :], compare_op=ALU.not_equal, fill=1.0, base=0,
             pattern=[[-1, 128]], channel_multiplier=1)
    t_up = G(pool.affine_select, out=upper[:, :], in_=upper[:, :], compare_op=ALU.is_gt, fill=0.0, base=0,
             pattern=[[1, 128]], channel_multiplier=-1)
    G(pool.iota, iota_e[:, :], pattern=[[1, 8]], base=0, channel_multiplier=0, allow_small_or_imprecise_dtypes=True)
    G(pool.iota, iota_j[:, :], pattern=[[128, 8]], base=0, channel_multiplier=0, allow_small_or_imprecise_dtypes=True)
    G(pool.iota, iota_t[:, :], pattern=[[1, TILES1]], base=0, channel_multiplier=0, allow_small_or_imprecise_dtypes=True)
    t_iota = G(pool.iota, rowe[:, :], pattern=[[0, 1]], base=0, channel_multiplier=1, allow_small_or_imprecise_dtypes=True)
    wait(dve, t_id, t_iota)
    V(dve.tensor_copy, identb[:, :], ident[:, :])
    for _ in range(2):
        t = VC(dve.tensor_scalar, junk[0:24, :], rowe[:, :], 8.0, -8.0, ALU.is_ge, ALU.mult)
        t_rowe = VC(dve.tensor_tensor, rowe[:, :], rowe[:, :], junk[0:24, :], ALU.add)

    wait(pool, t_m1)
    t_mu1 = G(pool.tensor_scalar, mu[:, 4:12, :], m1i, 0.0, None, ALU.is_gt)
    wait(dve, t_m0)
    t_mu0 = V(dve.tensor_scalar, mu[:, 0:4, :], m0i, 0.0, None, ALU.not_equal)

    def key_counts(which, t_mu):
        wait(pe, t_mu, t_iota, rel[6], rel[7])
        for half in range(2):
            for q in range(4):
                m = put(pe, pe.matmul, PS[:, 6 + half, :], onesb[:, :], mu[:, which * 4 + q, half * 512:(half + 1) * 512],
                        start=(q == 0), stop=(q == 3))
        tk = inc(m, own_sem(pe, "pe"))
        wait(dve, tk)
        c = mc[:, which, :]
        t = V(dve.tensor_copy, c, PS[:, 6:8, :].rearrange("p a n -> p (a n)"))
        rel[6] = rel[7] = t
        wait(dve, t)
        VC(dve.tensor_scalar, mt[:, which, :], c, -1.0, 512.0, ALU.mult, ALU.add)
        VC(dve.tensor_tensor, mt[:, which, FK * 3:SK], mt[:, which, FK * 3:SK], c[:, FK * 3:SK], ALU.mult)
        VC(dve.tensor_copy, mt[:, which, 0:FK * 3], c[:, 0:FK * 3])
        VC(dve.tensor_reduce, fsum[:, 4 + which:5 + which], c[:, FK * 3:SK], AX, ALU.add)
        return VC(dve.tensor_reduce, fsum[:, which:which + 1], mt[:, which, :], AX, ALU.add)

    def flag_of(l, whiches):
        fl = junk[:, 0:1]
        first = True
        for w in whiches:
            VC(dve.tensor_scalar, fsum[:, w:w + 1], fsum[:, w:w + 1], 0.0, None, ALU.is_equal)
            VC(dve.tensor_scalar, fsum[:, 4 + w:5 + w], fsum[:, 4 + w:5 + w], 0.0, None, ALU.is_gt)
            VC(dve.tensor_tensor, fsum[:, w:w + 1], fsum[:, w:w + 1], fsum[:, 4 + w:5 + w], ALU.mult)
            if first:
                VC(dve.tensor_copy, fl, fsum[:, w:w + 1])
            else:
                VC(dve.tensor_tensor, fl, fl, fsum[:, w:w + 1], ALU.mult)
            first = False
        t = VC(dve.tensor_copy, flags[:, l:l + 1], fl)
        for b in range(NB):
            w = whiches[b % len(whiches)]
            t = V(dve.tensor_scalar, maskrow[0:1, l, b * FK:(b + 1) * FK], mc[0:1, w, 3 * FK:SK], 0.0, -1.0e30,
                  ALU.is_equal, ALU.mult)
        wait(sp, t)
        return t, dma(sp, "mrow", mr[l:l + 1, :], maskrow[0:1, l, :])

    key_counts(0, t_mu0)
    t_flag0, t_mr0 = flag_of(0, [0])

    wait(dve, t_small)
    VC(dve.tensor_copy, bsp[:, 0, :], bsf)
    VC(dve.tensor_tensor, bsf, bsf, bsp[:, 0, :], ALU.subtract)
    VC(dve.tensor_copy, bsp[:, 1, :], bsf)
    VC(dve.tensor_tensor, bsf, bsf, bsp[:, 1, :], ALU.subtract)
    t = VC(dve.tensor_copy, bsp[:, 2, :], bsf)
    wait(sp, t)
    t = dma(sp, "bd", bd.rearrange("s e n -> e s n"), bsp)
    wait(sp, t)
    t_bs = dma(sp, "bs", BS[:, :], bd.rearrange("s e n -> (s e) n"))

    key_counts(1, t_mu1)
    key_counts(2, t_mu1)
    t_flag1, t_mr1 = flag_of(1, [1, 2])
    t_setup = [t_flag1, t_mr0, t_mr1, t_bs, t_mu1]

    wait(pool, t_mu1)
    t_z = G(pool.memset, XT[:, 0, :], 0.0)
    wait(sp, t_z)
    t_xz = dma(sp, "xz", xs.rearrange("(a p r) c -> p a (r c)", p=128, r=2),
               XT[:, 0:1, 0:512].to_broadcast([128, TILES1 // 2, 512]))

    def rsqrt(n, var, eps):
        a, b, y, t = (NW[:, i, 0:n] for i in range(4))
        V(dve.tensor_scalar, a, var, eps, -0.5, ALU.add, ALU.mult)
        VC(dve.tensor_scalar, b, var, eps, None, ALU.add)
        VC(dve.tensor_scalar, y.bitcast(I32), b.bitcast(I32), -0.5, MAGIC, ALU.mult, ALU.add)
        for _ in range(4):
            VC(dve.tensor_tensor, t, y, y, ALU.mult)
            VC(dve.tensor_tensor, t, t, a, ALU.mult)
            VC(dve.scalar_tensor_tensor, y, t, 1.5, y, ALU.add, ALU.mult)
        return y

    nw_free = [None]

    def stats(srcs, t_src):
        n = len(srcs)
        wait(dve, nw_free[0])
        for s, t in zip(srcs, t_src):
            wait(dve, t)
            t = V(dve.bn_stats, ST[:, srcs.index(s), :], s)
        wait(dve, t)
        for i in range(n):
            t = V(dve.bn_aggr, MV[:, i, :], ST[:, i, :])
        wait(dve, t)
        y = rsqrt(n, MV[:, 0:n, 1], EPS)
        t = VC(dve.scalar_tensor_tensor, NW[:, 4, 0:n], MV[:, 0:n, 0], -1.0, y, ALU.mult, ALU.mult)
        return y, NW[:, 4, 0:n], t

    def normalise(srcs, dsts, t_src, t_dst=None):
        y, nb, t = stats(srcs, t_src)
        toks = []
        wait(act, t, t_dst)
        wait(dve, t_dst)
        for i, (s, d) in enumerate(zip(srcs, dsts)):
            if i // 2 % 2:
                toks.append(C(act.activation, d, s, ACT.Identity, bias=nb[:, i:i + 1], scale=y[:, i:i + 1]))
            else:
                toks.append(V(dve.tensor_scalar, d, s, MV[:, i, 0:1], y[:, i:i + 1], ALU.subtract, ALU.mult))
        nw_free[0] = toks[-2:]
        return toks

    def turn4(srcs, toks, banks, finish):
        for t in range(4):
            wait(pe, toks[t])
        wait(pe, t_id)
        outs = []
        for k in range(2):
            wait(pe, rel[banks[k]])
            for t in range(4):
                m = put(pe, pe.transpose, PS[:, banks[k], t * 128:(t + 1) * 128], srcs[t][:, k * 128:(k + 1) * 128],
                        ident[:, :])
            rel[banks[k]] = finish(k, banks[k], inc(m, own_sem(pe, "pe")))
            outs.append(rel[banks[k]])
        return outs

    def ln_turned(t_in):
        xt = []
        toks = normalise([X[:, t, :] for t in range(NT)], [XN[:, t, :] for t in range(NT)], t_in)
        for g in range(2):
            xt.append(turn4([XN[:, 4 * g + j, :] for j in range(4)], toks[4 * g:4 * g + 4], (6, 7),
                            lambda k, bk, tk: evac(XT[:, k, g * 512:(g + 1) * 512], PS[:, bk, :], tk)))
        return toks, xt

    st = {}

    def split_chunk(t_f, dst, parts, t_dst):
        i = st["chunk"] % 2
        st["chunk"] += 1
        f = FE[:, i, :, :]
        p = [SP[:, i, s, :, :] for s in range(3)]
        wait(act, t_f, st["sp_free"][i])
        t = C(act.activation, p[0], f, ACT.Copy)
        wait(dve, t, t_f)
        t = V(dve.tensor_tensor, f, f, p[0], ALU.subtract)
        wait(act, t)
        t = C(act.activation, p[1], f, ACT.Copy)
        wait(dve, t)
        t = VC(dve.tensor_tensor, f, f, p[1], ALU.subtract)
        t2 = V(dve.tensor_copy, p[2], f)
        st["fe_free"][i] = t2
        wait(sp, t2)
        for s in range(3):
            tw = dma(sp, f"so{i}", sd[i, s].rearrange("(k p) n -> p k n", p=128), p[s])
        st["sp_free"][i] = tw
        wait(sp, tw, t_dst)
        for r, s in enumerate(parts):
            td = dma(sp, f"si{i}", dst[16 * r:16 * r + 16], sd[i, s].rearrange("(h d) n -> d h n", d=HD))
        return td

    def project_turned(wi, ci, scale, src, t_src):
        i = st["chunk"] % 2
        toks = []
        for fb in range(2):
            bk = fb
            wait(pe, t_wp, t_src, rel[bk])
            for k in range(2):
                m = put(pe, pe.matmul, PS[:, bk, :], WP[:, wi, k, fb * 128:(fb + 1) * 128], src[:, k, :],
                        start=(k == 0), stop=(k == 1))
            tk = inc(m, own_sem(pe, "pe"))
            wait(dve, tk, st["fe_free"][i], t_wp)
            rel[bk] = V(dve.tensor_scalar, FE[:, i, fb, :], PS[:, bk, :], col[:, ci, fb:fb + 1], scale, ALU.add, ALU.mult)
            toks.append(rel[bk])
        return toks

    def rows_of(wi, src, cols, banks, t_src):
        toks = []
        for j, c in enumerate(cols):
            bk = banks[j // 2]
            if j % 2 == 0:
                wait(pe, t_wp, t_src, rel[bk])
            for k in range(2):
                m = put(pe, pe.matmul, PS[:, bk, (j % 2) * 256:(j % 2 + 1) * 256], src[:, k, c:c + 128], WP[:, wi, k, :],
                        start=(k == 0), stop=(k == 1))
            tk = inc(m, own_sem(pe, "pe"))
            toks.append(tk)
        return toks, [PS[:, banks[j // 2], (j % 2) * 256:(j % 2 + 1) * 256] for j in range(len(cols))]

    def project_normed(wi, gi, scale, src, cols, t_src, nr, t_nr, banks=(2, 3)):
        i = st["chunk"] % 2
        tks, ps = rows_of(wi, src, cols, banks, t_src)
        for b_ in banks:
            wait(dve, tks[-1])
        nrs = [NR[:, nr + j, :] for j in range(4)]
        toks = normalise(ps, nrs, [tks[1], tks[1], tks[3], tks[3]], t_nr)
        for j, b_ in enumerate(banks):
            rel[b_] = [toks[2 * j], toks[2 * j + 1]]

        def finish(k, bk, tk):
            wait(dve, tk, st["fe_free"][i])
            t = VC(dve.tensor_scalar, FE[:, i, k, :], PS[:, bk, :], col[:, gi, k:k + 1], col[:, gi + 1, k:k + 1],
                   ALU.mult, ALU.add)
            if scale != 1.0:
                t = V(dve.tensor_scalar, FE[:, i, k, :], FE[:, i, k, :], scale, None, ALU.mult)
            return t

        return turn4(nrs, toks, (0, 1), finish)

    def values(l, src, cols, v0, t_src, t_free, banks, nr=0, t_nr=None):
        toks = []
        wait(dve, t_free)
        t = VC(dve.memset, VR[:, v0 * VT:(v0 + len(cols)) * VT], 1.0)
        for c in range(0, len(cols), 4):
            tks, ps = rows_of(1, src, cols[c:c + 4], banks, t_src)
            dst = [VV[:, v0 + c + j, 0:H * VW].rearrange("p (h v) -> p h v", v=VW)[:, :, 0:HD] for j in range(4)]
            bc = [BC[:, i, :].rearrange("p (h d) -> p h d", d=HD) for i in range(2)]
            if l == 0:
                for j in range(4):
                    wait(dve, tks[j // 2 * 2 + 1], t_wp)
                    tv = V(dve.tensor_tensor, dst[j], ps[j].rearrange("p (h d) -> p h d", d=HD), bc[0], ALU.add)
                    toks.append(tv)
                    rel[banks[j // 2]] = tv
            else:
                nrs = [NR[:, nr + j, :] for j in range(4)]
                tn = normalise(ps, nrs, [tks[1], tks[1], tks[3], tks[3]], t_nr)
                for j, b_ in enumerate(banks):
                    rel[b_] = [tn[2 * j], tn[2 * j + 1]]
                wait(pool, t, t_wp)
                for j in range(4):
                    wait(pool, tn[j])
                    tg = G(pool.tensor_tensor, nrs[j], nrs[j], BC[:, 0, :], ALU.mult)
                    wait(pool, tg)
                    tv = G(pool.tensor_tensor, dst[j], nrs[j].rearrange("p (h d) -> p h d", d=HD), bc[1], ALU.add)
                    toks.append(tv)
                t_nr = tv
        return toks

    def start_attention():
        st.clear()
        st.update(chunk=0, fe_free=[None, None], sp_free=[None, None])
        nw_free[0] = None

    def attention_fast(l, t_in, prefetch):
        def body():
            start_attention()
            wait(pool, t_in)
            wait(act, t_in)
            t_k1 = G(pool.memset, KS[96:100, :, :], 1.0)
            t_q1 = G(pool.memset, QS[96:97, :, :], 1.0)
            wait(sp, t_k1, t_q1)
            t_kb = dma(sp, "kb", KS[96:97, :, :], mr[l:l + 1, :].unsqueeze(1).to_broadcast([1, H, NB * FK]))
            kcols = [128 * j for j in range(4)]
            if l == 0:
                toks, xt = ln_turned([t_in] * NT)
                t_f = project_turned(0, 0, 1.0, CTf, t_ct)
                t_ks = split_chunk(t_f, KS[:, :, :], K_PART, None)
                t_f = project_turned(2, 1, 0.25, XT[:, :, 0:512], xt[0])
                t_q0 = split_chunk(t_f, QS[:, :, 0:512], Q_PART, None)
                t_f = project_turned(2, 1, 0.25, XT[:, :, 512:1024], xt[1])
                t_q2 = split_chunk(t_f, QS[:, :, 512:1024], Q_PART, None)
                t_v = values(0, CTf, kcols, 0, t_ct, t_in, (2, 3))
            else:
                wait(dve, t_in)
                t_f = project_normed(0, 0, 1.0, CTf, kcols, t_ct, 0, None)
                t_ks = split_chunk(t_f, KS[:, :, :], K_PART, None)
                toks, xt = ln_turned([t_in] * NT)
                t_f = project_normed(2, 2, 0.25, XT, [128 * j for j in range(4)], xt[0], 4, None, (4, 5))
                t_q0 = split_chunk(t_f, QS[:, :, 0:512], Q_PART, None)
                t_f = project_normed(2, 2, 0.25, XT, [512 + 128 * j for j in range(4)], xt[1], 0, None)
                t_q2 = split_chunk(t_f, QS[:, :, 512:1024], Q_PART, None)
                t_v = values(1, CTf, kcols, 0, t_ct, t_in, (4, 5), 4)
            t_q = [t_q0, t_q2]
            prefetch(0)
            pair = [0]

            def next_pair():
                p = pair[0] % 3
                pair[0] += 1
                return 2 * p

            def score_max(b, u):
                qb, hg = u // 4, u % 4
                b0 = next_pair()
                wait(pe, t_q[b], t_ks, t_kb, rel[b0], rel[b0 + 1])
                for j in range(4):
                    h = 4 * hg + j
                    m = put(pe, pe.matmul, PS[:, b0 + j // 2, (j % 2) * FK:(j % 2 + 1) * FK],
                            QS[0:NS + 1, h, (4 * b + qb) * 128:(4 * b + qb + 1) * 128],
                            KS[0:NS + 1, h, b * FK:(b + 1) * FK], start=True, stop=True)
                wait(dve, inc(m, own_sem(pe, "pe")))
                t = V(dve.tensor_reduce, mx[:, b, qb, 4 * hg:4 * hg + 4],
                      PS[:, b0:b0 + 2, :].rearrange("p a (j n) -> p (a j) n", n=FK), AX, ALU.max)
                rel[b0] = rel[b0 + 1] = t
                return t

            def max_rows(b):
                m_ = mx[:, b, :, :]
                wait(dve, seen_dve())
                VC(dve.tensor_scalar, m_, m_, -1.0, None, ALU.mult)
                for s in range(3):
                    VC(dve.tensor_copy, msb[:, b, :, s, :], m_)
                    if s < 2:
                        t = VC(dve.tensor_tensor, m_, m_, msb[:, b, :, s, :], ALU.subtract)
                wait(pe, seen_dve(), rel[7], t_idb)
                pb = PS[0:48, 7, 0:256].bitcast(BF16)
                for qb in range(4):
                    m = put(pe, pe.transpose, pb[:, qb * 128:(qb + 1) * 128],
                            msb[:, b, qb, :, :].rearrange("p s h -> p (s h)"), identb[:, :])
                wait(dve, inc(m, own_sem(pe, "pe")))
                t = V(dve.tensor_copy, MT[:, b, :], pb)
                rel[7] = t
                wait(sp, t)
                t = dma(sp, f"mo{b}", md[b].rearrange("s h n -> (s h) n"), MT[:, b, :])
                wait(sp, t, t_q[b])
                return dma(sp, f"mi{b}", QS[97:100, :, b * 512:(b + 1) * 512], md[b])

            px_free = [t_v + t_q] * 6
            px_tok = [None] * 6
            n_exp = [0]

            def weights_of(b, h, t_m):
                b0 = next_pair()
                wait(pe, t_m, t_ks, t_kb, rel[b0], rel[b0 + 1])
                for kb in range(2):
                    m = put(pe, pe.matmul, PS[:, b0 + kb, :],
                            KS[0:NS + 4, h, b * FK + kb * 128:b * FK + (kb + 1) * 128],
                            QS[0:NS + 4, h, b * 512:(b + 1) * 512], start=True, stop=True)
                slot = n_exp[0] % 6
                n_exp[0] += 1
                wait(act, inc(m, own_sem(pe, "pe")), px_free[slot])
                t = C(act.activation, PX[slot], PS[:, b0:b0 + 2, :].rearrange("p a n -> p (a n)"), ACT.Exp)
                rel[b0] = rel[b0 + 1] = t
                px_tok[slot] = t
                return slot

            def combine(b, g, slots):
                wait(pe, t_v[-1], t_v[-2], rel[6])
                for kb in range(2):
                    for j in range(4):
                        h = 4 * g + j
                        wait(pe, px_tok[slots[j]])
                        m = put(pe, pe.matmul, PS[32 * j:32 * j + 32, 6, :],
                                VV[:, 2 * b + kb, h * VW:h * VW + 32],
                                PX[slots[j]][:, kb * 512:(kb + 1) * 512], start=(kb == 0), stop=(kb == 1),
                                skip_group_check=True)
                tk = inc(m, own_sem(pe, "pe"))
                for s in slots:
                    px_free[s] = tk
                i = g % 2
                wait(dve, tk, st.get(("os", i)), t_q[1])
                t = V(dve.tensor_copy, OS[:, i, :], PS[:, 6, :])
                rel[6] = t
                wait(pe, t, rel[7])
                for qb in range(4):
                    m = put(pe, pe.transpose, PS[:, 7, qb * 128:(qb + 1) * 128], OS[:, i, qb * 128:(qb + 1) * 128],
                            ident[:, :])
                tk = inc(m, own_sem(pe, "pe"))
                st[("os", i)] = tk
                wait(dve, tk)
                o = PS[:, 7, :].rearrange("p (q j v) -> p q j v", q=4, v=32)
                VC(dve.reciprocal, rlf[:, :, :], o[:, :, :, HD])
                dst = OB[:, b, :, 64 * g:64 * (g + 1)].rearrange("p q (j d) -> p q j d", d=HD)
                for qb in range(4):
                    t = V(dve.tensor_tensor, dst[:, qb], o[:, qb, :, 0:HD], bb(rlf[:, qb, :], HD), ALU.mult)
                rel[7] = t
                return t

            fin = []

            def close(b, t_o):
                if l == 1:
                    wait(pool, t_o)
                    for qb in range(4):
                        fin.append(G(pool.tensor_tensor, X[:, 4 * b + qb, :], X[:, 4 * b + qb, :], OB[:, b, qb, :], ALU.add))
                    return
                xo = turn4([OB[:, b, j, :] for j in range(4)], [t_o] * 4, (6, 7),
                           lambda k, bk, tk: evac(XT[:, k, b * 512:(b + 1) * 512], PS[:, bk, :], tk))
                tks, ps = rows_of(3, XT, [b * 512 + 128 * j for j in range(4)], (6, 7), xo)
                for j in range(4):
                    x = X[:, 4 * b + j, :]
                    wait(dve, tks[j // 2 * 2 + 1])
                    t = V(dve.tensor_tensor, x, x, ps[j], ALU.add)
                    rel[6 + j // 2] = t
                    wait(pool, t)
                    fin.append(G(pool.tensor_tensor, x, x, BC[:, 1, :], ALU.add))

            for u in range(16):
                score_max(0, u)
            t_mi0 = max_rows(0)
            prefetch(1)
            slots = []
            for u in range(16):
                score_max(1, u)
                if u >= 4:
                    slots.append(weights_of(0, u - 4, t_mi0))
                    if len(slots) == 4:
                        t_o = combine(0, (u - 4) // 4, slots)
                        slots = []
            t_mi1 = max_rows(1)
            prefetch(2)
            for h in range(12, 16):
                slots.append(weights_of(0, h, t_mi0))
            t_o = combine(0, 3, slots)
            slots = []
            for h in range(H):
                slots.append(weights_of(1, h, t_mi1))
                if h == 1:
                    close(0, t_o)
                if len(slots) == 4:
                    t_o = combine(1, h // 4, slots)
                    slots = []
            close(1, t_o)
            return fin + [t_o, t_xz, px_free[0], px_free[1]]

        return body

    def attention_general(l, t_in, prefetch):
        def body():
            start_attention()
            for e in (pool, act, dve, sp, pe):
                wait(e, t_in)
            toks, xt = ln_turned([t_in] * NT)
            t_prev = xt[0] + xt[1]
            t_last = None
            fin = []
            for b in range(NB):
                wait(sp, t_prev)
                t_c = dma(sp, "ctg", CTg, ctx_v[:, :, b, :])
                t_ks = []
                for c in range(2):
                    src = CTg[:, :, c * 512:(c + 1) * 512]
                    if l == 0:
                        t_f = project_turned(0, 0, 1.0, src, t_c)
                    else:
                        t_f = project_normed(0, 0, 1.0, CTg, [512 * c + 128 * j for j in range(4)], t_c, 0, t_prev)
                    t_ks.append(split_chunk(t_f, KSg[:, :, c * 512:(c + 1) * 512], K_PART, t_prev))
                if l == 0:
                    t_f = project_turned(2, 1, 0.25, XT[:, :, b * 512:(b + 1) * 512], t_prev)
                else:
                    t_f = project_normed(2, 2, 0.25, XT, [512 * b + 128 * j for j in range(4)], t_prev, 0, None)
                t_q = split_chunk(t_f, QSg[:, :, :], Q_PART, t_prev)
                t_v = values(l, CTg, [128 * j for j in range(8)], 0, t_c, t_prev, (2, 3), 0, t_prev)
                t_prep = [t_q] + t_ks + t_v
                for e in (sp, dve, pe, act):
                    wait(e, t_prep)
                t_pt = None
                t_mb = t_sm = None
                sm_free = [None, None]
                for qb in range(4):
                    wait(sp, t_mb)
                    if l == 0:
                        t_m = dma(sp, "mask", MIg, A["mask0"][qb * 128:(qb + 1) * 128, :])
                        src, val = MIg, BIG
                    else:
                        t_m = dma(sp, "mask", MUg, A["mask1"][b, qb * 128:(qb + 1) * 128, :])
                        src, val = MUg, -1.0e9
                    wait(dve, t_m)
                    t_mb = VC(dve.tensor_scalar, MBg, src, 0.0, val, ALU.is_equal, ALU.mult)
                    for h in range(H):
                        p = h % 2
                        wait(pe, rel[2 * p], rel[2 * p + 1])
                        for half in range(2):
                            m = put(pe, pe.matmul, PS[:, 2 * p + half, :], QSg[0:NS, h, qb * 128:(qb + 1) * 128],
                                    KSg[0:NS, h, half * 512:(half + 1) * 512], start=True, stop=True)
                        wait(dve, inc(m, own_sem(pe, "pe")), sm_free[p])
                        t_s = VC(dve.tensor_tensor_reduce, out=SMg[:, p, :],
                                 in0=PS[:, 2 * p:2 * p + 2, :].rearrange("p a n -> p (a n)"), in1=MBg, scale=1.0,
                                 scalar=-3.4e38, op0=ALU.add, op1=ALU.max, accum_out=rl[:, h:h + 1])
                        rel[2 * p] = rel[2 * p + 1] = t_s
                        t_n = V(dve.tensor_scalar, nmx[:, h:h + 1], rl[:, h:h + 1], -1.0, None, ALU.mult)
                        wait(act, t_n)
                        t_e = C(act.activation, SMg[:, p, :], SMg[:, p, :], ACT.Exp, bias=nmx[:, h:h + 1])
                        wait(pe, t_e)
                        for half in range(2):
                            bk = 4 + half
                            wait(pe, rel[bk])
                            for j in range(4):
                                kb = half * 4 + j
                                m = put(pe, pe.transpose, PS[:, bk, j * 128:(j + 1) * 128],
                                        SMg[:, p, kb * 128:(kb + 1) * 128], ident[:, :])
                            tk = inc(m, own_sem(pe, "pe"))
                            wait(act, t_pt)
                            wait(dve, t_pt)
                            rel[bk] = evac(PTg[:, half * 512:(half + 1) * 512], PS[:, bk, :], tk)
                        sm_free[p] = tk
                        wait(pe, rel[4], rel[5], rel[6] if h == 0 else None)
                        for kb in range(8):
                            m = put(pe, pe.matmul, PS[:, 6, h * VW:(h + 1) * VW], PTg[:, kb * 128:(kb + 1) * 128],
                                    VV[:, kb, h * VW:(h + 1) * VW], start=(kb == 0), stop=(kb == 7))
                        t_pt = inc(m, own_sem(pe, "pe"))
                    wait(dve, t_pt)
                    o = PS[:, 6, 0:H * VW].rearrange("p (h v) -> p h v", v=VW)
                    if l == 0:
                        VC(dve.tensor_scalar, okr[:, :], rl[:, :], -1.0e38, None, ALU.is_gt)
                    VC(dve.tensor_copy, rl[:, :], o[:, :, HD])
                    if l == 0:
                        VC(dve.tensor_tensor, rl[:, :], rl[:, :], okr[:, :], ALU.mult)
                    VC(dve.reciprocal, rl[:, :], rl[:, :])
                    ob = OB[:, b, qb, :]
                    wait(dve, t_prep)
                    t_o = V(dve.tensor_tensor, ob.rearrange("p (h d) -> p h d", d=HD), o[:, :, 0:HD], bb(rl[:, :], HD), ALU.mult)
                    rel[6] = t_o
                    x = X[:, 4 * b + qb, :]
                    wait(dve, t_o)
                    if l == 1:
                        t_last = VC(dve.tensor_tensor, x, x, ob, ALU.add)
                    else:
                        c0 = (4 * b + qb) * 128
                        wait(pe, t_o, rel[7])
                        for k in range(2):
                            m = put(pe, pe.transpose, PS[:, 7, k * 128:(k + 1) * 128], ob[:, k * 128:(k + 1) * 128], ident[:, :])
                        wait(dve, inc(m, own_sem(pe, "pe")))
                        t = VC(dve.tensor_copy, XT[:, :, c0:c0 + 128], PS[:, 7, 0:256].rearrange("p (k n) -> p k n", k=2))
                        wait(pe, t)
                        for k in range(2):
                            m = put(pe, pe.matmul, PS[:, 7, 256:512], XT[:, k, c0:c0 + 128], WP[:, 3, k, :],
                                    start=(k == 0), stop=(k == 1))
                        wait(dve, inc(m, own_sem(pe, "pe")))
                        rel[7] = VC(dve.tensor_tensor, x, x, PS[:, 7, 256:512], ALU.add)
                        t_last = VC(dve.tensor_tensor, x, x, BC[:, 1, :], ALU.add)
                t_prev = [t_last, t_pt, t_e]
                fin += t_prev
            wait(sp, t_prev)
            for b in range(NB):
                t_c = dma(sp, "ctb", CTf[:, :, b * FK:(b + 1) * FK], ctx_v[:, :, b, SK - FK:SK])
            for i in range(3):
                prefetch(i)
            return fin + [t_c, t_xz]

        return body

    def first_max(P, n, oh, mrow, idx):
        VC(dve.tensor_reduce, mrow, P, AX, ALU.max)
        r2 = R2[:, :, 0:n]
        VC(dve.tensor_tensor, r2, P, bb(mrow, n), ALU.not_equal)
        VC(dve.scalar_tensor_tensor, r2, r2, 100.0, iota_e[:, 0:n].unsqueeze(1).to_broadcast([128, NT, n]), ALU.mult, ALU.add)
        VC(dve.tensor_reduce, idx, r2, AX, ALU.min)
        VC(dve.tensor_tensor, oh, r2, bb(idx, n), ALU.is_equal)

    def softmax_rows(n):
        lg, p = LG[:, :, 0:n], R1[:, :, 0:n]
        VC(dve.tensor_reduce, rs[:, 0, :], lg, AX, ALU.max)
        wait(act, VC(dve.tensor_tensor, lg, lg, bb(rs[:, 0, :], n), ALU.subtract))
        wait(dve, C(act.activation, p, lg, ACT.Exp))
        VC(dve.tensor_reduce, rs[:, 1, :], p, AX, ALU.add)
        VC(dve.reciprocal, rs[:, 2, :], rs[:, 1, :])
        VC(dve.tensor_tensor, p, p, bb(rs[:, 2, :], n), ALU.mult)
        return p

    def expert_directions():
        wait(dve, t_small)
        VC(dve.tensor_tensor, wgn[:, :], wg[:, :], wg[:, :], ALU.mult)
        VC(dve.tensor_reduce, wgs[:, 0:1], wgn[:, :], AX, ALU.add)
        VC(dve.tensor_scalar, wgs[:, 1:2], wgs[:, 0:1], 1e-8, None, ALU.max)
        VC(dve.tensor_scalar, wgs[:, 2:3].bitcast(I32), wgs[:, 1:2].bitcast(I32), -0.5, MAGIC, ALU.mult, ALU.add)
        for _ in range(4):
            VC(dve.tensor_tensor, wgs[:, 3:4], wgs[:, 2:3], wgs[:, 2:3], ALU.mult)
            VC(dve.tensor_tensor, wgs[:, 3:4], wgs[:, 3:4], wgs[:, 1:2], ALU.mult)
            VC(dve.tensor_scalar, wgs[:, 3:4], wgs[:, 3:4], -0.5, 1.5, ALU.mult, ALU.add)
            VC(dve.tensor_tensor, wgs[:, 2:3], wgs[:, 2:3], wgs[:, 3:4], ALU.mult)
        t = VC(dve.tensor_scalar, wgn[:, :], wg[:, :], wgs[:, 2:3], None, ALU.mult)
        wait(pe, t, t_id, rel[6])
        tk = M(pe.transpose, PS[0:16, 6, 0:8], wgn[:, :], ident[0:8, 0:8])
        wait(dve, tk)
        rel[6] = VC(dve.tensor_copy, wgT[:, :], PS[0:16, 6, 0:8])
        return rel[6]

    def logits0(xt):
        for c in range(2):
            wait(pe, xt[c], rel[c])
            for k in range(2):
                m = put(pe, pe.matmul, PS[0:16, c, :], wred[:, k, :], XT[:, k, c * 512:(c + 1) * 512], start=(k == 0), stop=(k == 1))
            rel[c] = evac(xrT[:, c * 512:(c + 1) * 512], PS[0:16, c, :], inc(m, own_sem(pe, "pe")))
        wait(pe, t_wgT, rel[2])
        for t in range(NT):
            wait(pe, rel[t // 4])
            m = put(pe, pe.matmul, PS[:, 2, t * 8:(t + 1) * 8], xrT[:, t * 128:(t + 1) * 128], wgT[:, :], start=True, stop=True)
        wait(dve, inc(m, own_sem(pe, "pe")))
        rel[2] = VC(dve.tensor_copy, LG[:, :, :], PS[:, 2, 0:64].rearrange("p (t e) -> p t e", e=8))

    def logits1(xt):
        wait(pe, rel[6])
        for t in range(NT):
            wait(pe, xt[t // 4])
            for k in range(2):
                m = put(pe, pe.matmul, PS[:, 6, t * 8:t * 8 + E1], XT[:, k, t * 128:(t + 1) * 128], wr[:, k, :],
                        start=(k == 0), stop=(k == 1))
        wait(dve, inc(m, own_sem(pe, "pe")))
        rel[6] = VC(dve.tensor_tensor, LG[:, :, 0:E1], PS[:, 6, 0:64].rearrange("p (t e) -> p t e", e=8)[:, :, 0:E1],
                    rbb[:, :].unsqueeze(1).to_broadcast([128, NT, E1]), ALU.add)

    def routes(n, choices, oh_all, ntile):
        VC(dve.tensor_copy, OHb[:, :, 0:n], oh_all)
        ob = OHb[:, :, 0:n]
        wait(pe, seen_dve(), t_up, rel[6], rel[7])
        put(pe, pe.matmul, PS[:, 7, 0:NT * n], upper[:, :], ob, start=True, stop=True)
        tk = M(pe.matmul, PS[:, 6, 0:NT * n], onesb[:, :], ob, start=True, stop=True)
        wait(dve, tk)
        rk, cn = RK[:, :, 0:n], CN[:, :, 0:n]
        V(dve.tensor_copy, rk, PS[:, 7, 0:NT * n].rearrange("p (t e) -> p t e", e=n))
        rel[6] = rel[7] = VC(dve.tensor_copy, cn, PS[:, 6, 0:NT * n].rearrange("p (t e) -> p t e", e=n))
        tot, tl, base = ne[:, 0, 0:n], ne[:, 1, 0:n], ne[:, 2, 0:n]
        VC(dve.tensor_reduce, tot, cn.rearrange("p t e -> p e t"), AX, ALU.add)
        c8 = nt8[:, 0:n, 0:7]
        VC(dve.tensor_tensor, c8, bb(tot, 7), iota_j[:, 1:8].unsqueeze(1).to_broadcast([128, n, 7]), ALU.is_gt)
        VC(dve.tensor_reduce, tl, c8, AX, ALU.add)
        VC(dve.memset, ne[:, 3, :], 1.0)
        VC(dve.tensor_tensor, tl, tl, ne[:, 3, 0:n], ALU.add)
        VC(dve.tensor_tensor_scan, ne[:, 3, 0:n], ne[:, 3, 0:n], tl, 0.0, ALU.mult, ALU.add)
        VC(dve.tensor_tensor, base, ne[:, 3, 0:n], tl, ALU.subtract)
        t3 = te[:, 0:ntile, 0:n]
        VC(dve.tensor_tensor, t3, bb(iota_t[:, 0:ntile], n), base.unsqueeze(1).to_broadcast([128, ntile, n]), ALU.is_ge)
        VC(dve.tensor_reduce, tef[:, 0:ntile], t3, AX, ALU.add)
        VC(dve.tensor_scalar, tef[:, 0:ntile], tef[:, 0:ntile], -1.0, None, ALU.add)
        t_te = VC(dve.tensor_copy, tei[:, 0:ntile], tef[:, 0:ntile])
        VC(dve.tensor_scalar, base, base, 128.0, None, ALU.mult)
        for t in range(NT):
            VC(dve.tensor_tensor, rk[:, t, :], rk[:, t, :], base, ALU.add)
            if t < NT - 1:
                VC(dve.tensor_tensor, base, base, cn[:, t, :], ALU.add)
        for c, oh in enumerate(choices):
            VC(dve.tensor_tensor, R2[:, :, 0:n], rk, oh, ALU.mult)
            VC(dve.tensor_reduce, posf[:, c, :], R2[:, :, 0:n], AX, ALU.add)
            t_p = VC(dve.tensor_copy, posi[:, c, :], posf[:, c, :])
        return t_te, t_p

    def scatter(nc_, toks, t_p, t_free):
        wait(pool, t_p, t_free, t_xz)
        for t in toks:
            wait(pool, t)
        for c in range(nc_):
            for t in range(NT):
                off = bass.IndirectOffsetOnAxis(ap=posi[:, c, t:t + 1].bitcast(U32), axis=0)
                tk = inc(put(pool, pool.indirect_dma_start, xs, off, XN[:, t, :], None), s_scatter, 16)
        return tk

    def gather(c, t, dst, t_w, ntile):
        wait(pool, t_w)
        off = bass.IndirectOffsetOnAxis(ap=posi[:, c, t:t + 1].bitcast(U32), axis=0)
        key = f"gt{c}{t}"
        if key not in dsem:
            dsem[key] = sem(key)
        return inc(put(pool, pool.indirect_dma_start, dst, None, ys[0:ntile * 128, :], off), dsem[key], 16)

    s_scatter = sem("s_scatter")

    def load_x(i, t_in):
        p = i % 2
        wait(sp, t_in, fl["xl"][p])
        t = dma(sp, f"xl{p}", XL[:, p, :], xs[i * 128:(i + 1) * 128, :])
        return t

    fl = {}

    def turn_x(i, t_l):
        p = i % 2
        wait(pe, t_l, rel[7])
        for k in range(2):
            m = put(pe, pe.transpose, PS[:, 7, k * 128:(k + 1) * 128], XL[:, p, k * 128:(k + 1) * 128], ident[:, :])
        tk = inc(m, own_sem(pe, "pe"))
        fl["xl"][p] = tk
        wait(dve, tk, fl["xs"][p])
        t = V(dve.tensor_copy, XS[:, p, :, :], PS[:, 7, 0:256].rearrange("p (k n) -> p k n", k=2))
        rel[7] = t
        return t

    def expert(i, hold, n):
        hold["v"] = pe.value_load(tei[0:1, i:i + 1], min_val=0, max_val=n - 1)

    def turn_h(i, nj, nh, t_h):
        p = i % 2
        rows = [min(128, nh - 128 * j) for j in range(nj)]
        wait(pe, t_h, rel[4], rel[5] if nj > 4 else None)
        for j in range(nj):
            m = put(pe, pe.transpose, PS[0:rows[j], 4 + j // 4, (j % 4) * 128:(j % 4 + 1) * 128],
                    HB[:, p, j * 128:j * 128 + rows[j]], ident[:, :])
            if j == 3:
                tk4 = inc(m, own_sem(pe, "pe"))
        tk = tk4 if nj == 4 else inc(m, own_sem(pe, "pe"))
        fl["hb"][p] = tk
        if nj == 4:
            wait(dve, tk4, fl["ht"][p])
            rel[4] = V(dve.tensor_copy, HT[:, p, 0:4, :].rearrange("p j n -> p (j n)"), PS[:, 4, :])
            return [rel[4]]
        wait(act, tk4, fl["ht"][p])
        rel[4] = C(act.activation, HT[:, p, 0:4, :].rearrange("p j n -> p (j n)"), PS[:, 4, :], ACT.Copy)
        wait(dve, tk, fl["ht"][p])
        V(dve.tensor_copy, HT[:, p, 4, :], PS[:, 5, 0:128])
        rel[5] = V(dve.tensor_copy, HT[0:64, p, 5, :], PS[0:64, 5, 128:256])
        return [rel[4], rel[5]]

    def down(i, nj, nh, hold, base, stride, t_h, bias):
        p = i % 2
        wait(pe, t_h, rel[6])
        for j in range(nj):
            r = min(128, nh - 128 * j)
            o = base + j * D
            m = put(pe, lambda r=r, o=o, j=j, p=p: pe.matmul(
                PS[:, 6, 0:D], HT[0:r, p, j, :], W[0:r, bass.ds(hold["v"] * stride + o, D)],
                start=(j == 0), stop=(j == nj - 1 and not bias)))
        if bias:
            m = put(pe, pe.matmul, PS[:, 6, 0:D], OHE[0:24, i, :], BS[:, F0:F0 + D], start=False, stop=True)
        tk = inc(m, own_sem(pe, "pe"))
        fl["ht"][p] = tk
        return tk

    def store_y(i, tk):
        wait(act, tk, fl["yo"][0])
        t = C(act.activation, YO, PS[:, 6, 0:D], ACT.Copy)
        rel[6] = t
        wait(sp, t)
        fl["yo"][0] = dma(sp, "yo", ys[i * 128:(i + 1) * 128, :], YO)
        return fl["yo"][0]

    def up0(i, hold, t_x_, t_w):
        p, bk = i % 2, i % 2
        wait(pe, t_x_, t_w, t_bs, rel[bk])
        put(pe, pe.matmul, PS[:, bk, :], OHE[0:24, i, :], BS[:, 0:F0], start=True, stop=False)
        for k in range(2):
            m = put(pe, lambda k=k, p=p, bk=bk: pe.matmul(
                PS[:, bk, :], XS[:, p, k, :], W[:, bass.ds(hold["v"] * EXP0 + k * F0, F0)], start=False, stop=(k == 1)))
        tk = inc(m, own_sem(pe, "pe"))
        fl["xs"][p] = tk
        wait(act, tk, fl["hb"][p])
        t = C(act.activation, HB[:, p, 0:F0], PS[:, bk, :], ACT.Gelu)
        rel[bk] = t
        return t

    def up1(i, which, hold, lhs, t_x_, t_w):
        p, b0 = i % 2, 2 * which
        wait(pe, t_x_, t_w, rel[b0], rel[b0 + 1])
        for half in range(2):
            for k in range(2):
                o = k * 2 * F1 + which * F1 + half * 352
                m = put(pe, lambda k=k, half=half, o=o: pe.matmul(
                    PS[:, b0 + half, 0:352], lhs[k], W[:, bass.ds(hold["v"] * SLOT + o, 352)],
                    start=(k == 0), stop=(k == 1)))
        tk = inc(m, own_sem(pe, "pe"))
        hb = HB[:, p, :].rearrange("p (a n) -> p a n", a=2)
        if which == 0:
            wait(act, tk, fl["hb"][p])
            t = C(act.activation, hb, PS[:, 0:2, 0:352], ACT.Silu)
            fl["silu"] = t
        else:
            fl["xs"][p] = tk
            wait(dve, tk, fl["silu"])
            t = V(dve.tensor_tensor, hb, hb, PS[:, 2:4, 0:352], ALU.mult)
        rel[b0] = rel[b0 + 1] = t
        return t

    def clear_flags():
        nw_free[0] = None
        fl.clear()
        fl.update(xl=[None] * 2, xs=[None] * 2, hb=[None] * 2, ht=[None] * 2, yo=[None], silu=None)

    def load0(e, after):
        wait(sp, after)
        o = e * EXP0
        wdma(f"wa{e}", W[:, o:o + 2 * F0].rearrange("p (k n) -> p k n", k=2), A["L0_ffn_W1"][e].rearrange("(k p) n -> p k n", p=128))
        return wdma(f"wa{e}", W[:, o + 2 * F0:o + EXP0].rearrange("p (k n) -> p k n", n=D),
                    A["L0_ffn_W2"][e].rearrange("(k p) n -> p k n", p=128))

    def load1(e, after):
        wait(sp, after)
        g, u, d = (A["sgT"], A["suT"], A["sdT"]) if e == 0 else (A["rgT"][e - 1], A["ruT"][e - 1], A["rdT"][e - 1])
        o = e * SLOT
        up = W[:, o:o + 4 * F1].rearrange("p (k w n) -> p k w n", k=2, w=2)
        dn = W[:, o + 4 * F1:o + SLOT].rearrange("p (k n) -> p k n", n=D)
        wdma(f"wb{e}", up[:, :, 0, :], g.rearrange("(k p) n -> p k n", p=128))
        wdma(f"wb{e}", up[:, :, 1, :], u.rearrange("(k p) n -> p k n", p=128))
        wdma(f"wb{e}", dn[:, 0:5, :], d[0:640, :].rearrange("(k p) n -> p k n", p=128))
        return wdma(f"wb{e}", dn[0:64, 5, :], d[640:704, :])

    t_w0, t_w1 = {}, {}

    def prefetch0(i):
        for e in ((0, 1, 2), (3, 4, 5), (6, 7))[i]:
            t_w0[e] = load0(e, None)

    def prefetch1(i):
        for e in ((0,), (1, 2), (3,))[i]:
            t_w1[e] = load1(e, t_ffn0)

    def ffn0(t_in):
        clear_flags()
        for e in (sp, act, pool, dve, pe):
            wait(e, t_in)
        toks, xt = ln_turned([t_in] * NT)
        logits0(xt)
        p = softmax_rows(E0)
        oh = OH[:, 0, :, :]
        first_max(p, E0, oh, gw[:, 0, :], rs[:, 4, :])
        t_te, t_p = routes(E0, [oh], oh, TILES0)
        t_s = scatter(1, toks, t_p, None)
        V(dve.tensor_tensor, OHE[0:24], bb(tef[0:24, 0:TILES0], 128),
          rowe[:, :].unsqueeze(1).to_broadcast([24, TILES0, 128]), ALU.is_equal)
        t_oh = seen_dve()
        wait(pe, t_oh, t_te)
        hold = [{} for _ in range(TILES0)]
        t_x_ = {}
        t_l = {0: load_x(0, t_s), 1: load_x(1, t_s)}
        t_x_[0] = turn_x(0, t_l[0])
        prev = None
        tws = [t_w0[e] for e in range(8)]
        for i in range(TILES0):
            put(pe, lambda i=i: expert(i, hold[i], E0))
            th = up0(i, hold[i], t_x_[i], tws if i == 0 else None)
            if i + 1 < TILES0:
                t_x_[i + 1] = turn_x(i + 1, t_l[i + 1])
            if i + 2 < TILES0:
                t_l[i + 2] = load_x(i + 2, t_s)
            if prev is not None:
                tk = down(i - 1, NJ0, F0, hold[i - 1], 2 * F0, EXP0, turn_h(i - 1, NJ0, F0, prev), True)
                store_y(i - 1, tk)
            prev = th
        i = TILES0 - 1
        tk = down(i, NJ0, F0, hold[i], 2 * F0, EXP0, turn_h(i, NJ0, F0, prev), True)
        t_y = store_y(i, tk)
        fin = []
        for t in range(NT):
            tg = gather(0, t, XN[:, t, :], t_y, TILES0)
            wait(dve, tg)
            fin.append(V(dve.scalar_tensor_tensor, X[:, t, :], XN[:, t, :], gw[:, 0, t:t + 1], X[:, t, :], ALU.mult, ALU.add))
        return fin[-1]

    def ffn1(t_in):
        clear_flags()
        for e in (sp, act, pool, dve, pe):
            wait(e, t_in)
        for e in range(4, 8):
            t_w1[e] = load1(e, t_in)
        toks, xt = ln_turned([t_in] * NT)
        logits1(xt)
        p = softmax_rows(E1)
        o1, o2, oa = (OH[:, i, :, 0:E1] for i in range(3))
        g1, g2 = gw[:, 0, :], gw[:, 1, :]
        first_max(p, E1, o1, g1, rs[:, 5, :])
        VC(dve.scalar_tensor_tensor, LG[:, :, 0:E1], o1, -4.0, p, ALU.mult, ALU.add)
        first_max(LG[:, :, 0:E1], E1, o2, g2, rs[:, 5, :])
        VC(dve.tensor_tensor, rs[:, 0, :], g1, g2, ALU.add)
        VC(dve.reciprocal, rs[:, 0, :], rs[:, 0, :])
        VC(dve.tensor_tensor, g1, g1, rs[:, 0, :], ALU.mult)
        VC(dve.tensor_tensor, g2, g2, rs[:, 0, :], ALU.mult)
        VC(dve.tensor_tensor, oa, o1, o2, ALU.add)
        t_te, t_p = routes(E1, [o1, o2], oa, TILES1)
        t_s = scatter(2, toks, t_p, None)
        wait(pe, t_te)
        n = NT + TILES1
        hold = [{} for _ in range(n)]
        t_l, t_x_ = {}, {}
        prev = None
        t_y = None

        def lhs(i):
            if i < NT:
                return [XT[:, k, i * 128:(i + 1) * 128] for k in range(2)]
            return [XS[:, i % 2, k, :] for k in range(2)]

        def finish(i, th):
            tk = down(i, NJ1, F1, hold[i], 4 * F1, SLOT, th, False)
            if i < NT:
                wait(dve, tk)
                rel[6] = V(dve.tensor_tensor, X[:, i, :], X[:, i, :], PS[:, 6, 0:D], ALU.add)
                return None
            return store_y(i - NT, tk)

        def pull(i):
            if NT <= i < n:
                j = i - NT
                wait(sp, t_s, fl["xl"][i % 2])
                t_l[i] = dma(sp, f"xl{i % 2}", XL[:, i % 2, :], xs[j * 128:(j + 1) * 128, :])

        for i in range(n):
            if i < NT:
                hold[i]["v"] = 0
                t_x_[i] = xt[i // 4]
                tw = t_w1[0]
            else:
                tw = [t_w1[e] for e in range(1, min(7, i - NT + 1) + 1)]
                put(pe, lambda i=i: expert1(i - NT, hold[i]))
            up1(i, 0, hold[i], lhs(i), t_x_[i], tw)
            pull(i + 2)
            if prev is not None:
                th = turn_h(i - 1, NJ1, F1, prev)
            if NT <= i + 1 < n:
                t_x_[i + 1] = turn_x(i + 1, t_l[i + 1])
            new = up1(i, 1, hold[i], lhs(i), None, None)
            if prev is not None:
                t_y = finish(i - 1, th) or t_y
            prev = new
        t_y = finish(n - 1, turn_h(n - 1, NJ1, F1, prev))
        fin = []
        o_v = out.rearrange("(t p) c -> p t c", p=128)
        Y2 = XT[:, :, :].rearrange("p k n -> p (k n)").rearrange("p (t c) -> p t c", c=D)
        for t in range(NT):
            ta = gather(0, t, XN[:, t, :], t_y, TILES1)
            tb = gather(1, t, Y2[:, t, :], t_y, TILES1)
            wait(dve, ta)
            VC(dve.scalar_tensor_tensor, X[:, t, :], XN[:, t, :], gw[:, 0, t:t + 1], X[:, t, :], ALU.mult, ALU.add)
            wait(dve, tb)
            tf = V(dve.scalar_tensor_tensor, X[:, t, :], Y2[:, t, :], gw[:, 1, t:t + 1], X[:, t, :], ALU.mult, ALU.add)
            wait(act, tf)
            fin.append(dma(act, "out", o_v[:, t, :], X[:, t, :]))
        return fin[-1]

    def expert1(i, hold):
        hold["v"] = pe.value_load(tei[0:1, i:i + 1], min_val=0, max_val=E1 - 1) + 1

    wait(dve, t_id)
    t_idb = V(dve.tensor_copy, junk[:, :], ident[:, 0:1])
    t_wgT = expert_directions()
    t_in0 = [t_x, t_wgT, t_idb] + t_setup + [t_xz]
    t = branch(flags[0:1, 0:1], t_in0, attention_fast(0, t_in0, prefetch0), attention_general(0, t_in0, prefetch0))
    t_wp = load_proj(1, t)
    t_ffn0 = ffn0(t)
    t_in1 = [t_ffn0, t_wp]
    t = branch(flags[0:1, 1:2], t_in1, attention_fast(1, t_in1, prefetch1), attention_general(1, t_in1, prefetch1))
    t = ffn1(t)
    wait(sp, t)
    segments.append((state["queue"], None, None))

    for a, b, c in segments:
        if b is None:
            for e in engines:
                issue(a[id(e)])
        else:
            for e in engines:
                v = e.value_load(a, min_val=0, max_val=1)
                with e.If(v == 1):
                    issue(b[id(e)])
                with e.Else():
                    issue(c[id(e)])
    ctx.close()
def laid_out(i, np):
    c = np.ascontiguousarray
    a = {
        "x": c(i["x"]).reshape(NB * S, D),
        "ctxT": c(i["ctx_1024"].transpose(2, 0, 1)).reshape(D, NB * SK),
        "mask0": c(i["mask_1x1xSxS2_ik0"]).reshape(S, SK),
        "mask1": c(i["mask_BxSxS2_bk0"]),
    }
    for n in ("Wq", "Wk", "Wv", "Wo"):
        a[f"L0_xattn_{n}T"] = c(i[f"L0_xattn_{n}"].T)
    for n in ("L0_xattn_bq", "L0_xattn_bk", "L0_xattn_bv", "L0_xattn_bo", "L0_ffn_w_red", "L0_ffn_wg", "L0_ffn_W1",
              "L0_ffn_b1", "L0_ffn_W2", "L0_ffn_b2", "L1_xattn_Wq", "L1_xattn_Wk", "L1_xattn_Wv", "L1_xattn_gq",
              "L1_xattn_bq", "L1_xattn_gk", "L1_xattn_bk", "L1_xattn_gv", "L1_xattn_bv", "L1_ffn_rb"):
        a[n] = c(i[n])
    a["L1_ffn_wrT"] = c(i["L1_ffn_wr"].T)
    for n in ("sg", "su", "sd"):
        a[n + "T"] = c(i["L1_ffn_" + n].T)
    for n in ("rg", "ru", "rd"):
        a[n + "T"] = c(i["L1_ffn_" + n].transpose(0, 2, 1))
    return a


def kernel(**inputs):
    import numpy as np
    import concourse.bacc as bacc
    from concourse.bass_utils import run_bass_kernel_spmd

    nc = bacc.Bacc("TRN2", target_bir_lowering=False, num_devices=1)
    arrays = laid_out({k: np.asarray(v) for k, v in inputs.items()}, np)
    aps = {n: nc.dram_tensor("in_" + n, v.shape, mybir.dt.from_np(v.dtype), kind="ExternalInput").ap()
           for n, v in arrays.items()}
    out = nc.dram_tensor("out", [NB * S, D], F32, kind="ExternalOutput").ap()
    build(nc, aps, out)
    r = run_bass_kernel_spmd(nc, [{"in_" + n: v for n, v in arrays.items()}], core_ids=[0])
    return r.results[0]["out"].reshape(NB, S, D)
```

```python
from contextlib import ExitStack

import concourse.bass as bass
from concourse import mybir

F32 = mybir.dt.float32
BF16 = mybir.dt.bfloat16
I32 = mybir.dt.int32
U32 = mybir.dt.uint32
U8 = mybir.dt.uint8
ALU = mybir.AluOpType
ACT = mybir.ActivationFunctionType
AX = mybir.AxisListType.X

D = 256
H = 16
HD = 16
NB = 2
S = 512
SK = 1024
FK = 256
NT = NB * S // 128
VW = HD + 1
VT = H * VW + 16
E0, F0 = 8, 512
E1, F1 = 7, 704
NJ0, NJ1 = 4, 6
TILES0 = 15
TILES1 = 22
COUNTS0 = (12, 13, TILES0)
COUNTS1 = (19, 20, TILES1)
EPS = 1e-5
BIG = -3.0e38
SLOT = 2 * 2 * F1 + NJ1 * D
EXP0 = 2 * F0 + NJ0 * D
Q_PART = (0, 0, 0, 1, 1, 2)
K_PART = (0, 1, 2, 0, 1, 0)
NS = 16 * len(Q_PART)
MAGIC = float(0x5F3759DF)


def build(nc, A, out):
    ctx = ExitStack()
    pe, dve, act, pool, sp = nc.tensor, nc.vector, nc.scalar, nc.gpsimd, nc.sync
    engines = (pe, dve, act, pool, sp)

    def sem(name):
        return ctx.enter_context(nc.semaphore(name))

    def sb(name, shape, dt):
        return ctx.enter_context(nc.sbuf_tensor(name, shape, dt))

    state = {"queue": {id(e): [] for e in engines}, "branch": ""}
    segments = []
    rel, ev, nw_free = [None] * 8, [0], [None]
    count, seen, own = {}, {}, {}

    def put(eng, fn, *a, **k):
        item = [fn, a, k, []]
        state["queue"][id(eng)].append(item)
        return item

    def inc(item, s, n=1):
        item[3].append((s, n))
        count[id(s)] = count.get(id(s), 0) + n
        return (s, count[id(s)])

    def wait(eng, *tokens):
        for t in tokens:
            if isinstance(t, list):
                wait(eng, *t)
            elif t is not None and seen.get((id(eng), id(t[0])), 0) < t[1]:
                put(eng, eng.wait_ge, t[0], t[1])
                seen[(id(eng), id(t[0]))] = t[1]

    def own_sem(eng, name):
        key = (id(eng), state["branch"])
        if key not in own:
            own[key] = sem(f"s_{name}{state['branch']}")
        return own[key]

    def V(fn, *a, **k):
        return inc(put(dve, fn, *a, **k), own_sem(dve, "dve"))

    def C(fn, *a, **k):
        return inc(put(act, fn, *a, **k), own_sem(act, "act"))

    def M(fn, *a, **k):
        return inc(put(pe, fn, *a, **k), own_sem(pe, "pe"))

    def G(fn, *a, **k):
        return inc(put(pool, fn, *a, **k), own_sem(pool, "pool"))

    def VC(fn, *a, **k):
        t = V(fn, *a, **k)
        wait(dve, t)
        return t

    def seen_dve():
        s = own_sem(dve, "dve")
        return (s, count[id(s)])

    dsem = {}

    def dma(eng, name, dst, src, **kw):
        name = name + state["branch"]
        if name not in dsem:
            dsem[name] = sem("d_" + name)
        return inc(put(eng, eng.dma_start, dst, src, **kw), dsem[name], 16)

    def wdma(name, dst, src):
        if name not in dsem:
            dsem[name] = sem("d_" + name)
        return inc(put(sp, sp.dma_start, dst, src), dsem[name], 16)

    def issue(items):
        for fn, a, k, incs in items:
            ins = fn(*a, **k)
            for s, n in incs:
                ins.then_inc(s, n)

    def branch(flag, t_flag, ways):
        for e in engines:
            wait(e, t_flag)
        segments.append((state["queue"], None))
        before, known, rel0, alt = dict(count), dict(seen), list(rel), ev[0]
        state["branch"] = f"_{len(segments)}"
        made, after = [], []
        for value, body in ways:
            state["queue"] = {id(e): [] for e in engines}
            count.clear()
            count.update(before)
            seen.clear()
            seen.update(known)
            rel[:] = rel0
            ev[0] = alt
            nw_free[0] = None
            wait(dve, body())
            t_join = inc(put(dve, dve.memset, junk[:, :], 0.0), s_join)
            made.append((value, state["queue"]))
            inside = {id(x) for k, x in own.items() if k[1] == state["branch"]}
            inside |= {id(x) for k, x in dsem.items() if k.endswith(state["branch"])}
            after.append({k: v for k, v in count.items() if k not in inside})
        assert all(a == after[0] for a in after), "the ways leave different counts"
        count.clear()
        count.update(after[0])
        seen.clear()
        seen.update(known)
        rel[:] = [t_join] * 8
        nw_free[0] = None
        state["branch"] = ""
        segments.append((flag, made))
        state["queue"] = {id(e): [] for e in engines}
        return t_join

    s_join = sem("s_join")

    X = sb("X", [128, NT, D], F32)
    XT = sb("XT", [128, 2, NT * 128], F32)
    CT = sb("CT", [128, 2 * SK], F32)
    CTf = CT[:, 0:1024].rearrange("p (k n) -> p k n", k=2)
    CTg = CT[:, :].rearrange("p (k n) -> p k n", k=2)
    OHE = CT[:, 1024:2048].bitcast(BF16)[:, 0:TILES0 * 128].rearrange("p (t n) -> p t n", n=128)
    PTg = CT[:, 0:1024]
    WP = sb("WP", [128, 4, 2, D], F32)
    BC = sb("BC", [128, 2, D], F32)
    col = sb("col", [128, 4, 2], F32)
    VR = sb("VR", [128, 8 * VT], F32)
    VV = VR[:, :].rearrange("p (t v) -> p t v", v=VT)
    HB = VR[:, 0:2 * F1].rearrange("p (a n) -> p a n", a=2)
    XL = VR[:, 2 * F1:2 * F1 + 2 * D].rearrange("p (a n) -> p a n", a=2)
    YO = VR[:, 2 * F1 + 2 * D:2 * F1 + 2 * D + D]
    PR = sb("PR", [128, 4096], F32)
    XN = PR[:, 0:2048].rearrange("p (t c) -> p t c", c=D)
    NR = PR[:, 2048:4096].rearrange("p (t c) -> p t c", c=D)
    HT = PR[:, 2048:2048 + 2 * NJ1 * 128].rearrange("p (a j n) -> p a j n", a=2, n=128)
    XS = PR[:, 3584:4096].rearrange("p (a k n) -> p a k n", a=2, k=2)
    SMg = PR[:, 0:2048].rearrange("p (a n) -> p a n", a=2)
    MBg = PR[:, 2048:3072]
    MIg = PR[:, 3072:4096].bitcast(I32)
    MUg = PR[:, 3072:3328].bitcast(U8)
    W = sb("W", [128, 8 * SLOT], F32)
    a0 = 4 * SLOT
    QS = W[:, a0:a0 + 8192].bitcast(BF16).rearrange("p (h n) -> p h n", h=H)
    KS = W[:, a0 + 8192:a0 + 12288].bitcast(BF16).rearrange("p (h n) -> p h n", h=H)
    QSg = W[:, a0:a0 + 4096].bitcast(BF16).rearrange("p (h n) -> p h n", h=H)
    KSg = W[:, a0 + 4096:a0 + 12288].bitcast(BF16).rearrange("p (h n) -> p h n", h=H)
    FE = W[:, a0 + 12288:a0 + 14336].rearrange("p (i k n) -> p i k n", i=2, k=2)
    SP = W[:, a0 + 14336:a0 + 17408].bitcast(BF16).rearrange("p (i s k n) -> p i s k n", i=2, s=3, k=2)
    OB = FE[:, :, :, :].rearrange("p i k n -> p i (k n)").rearrange("p i (q c) -> p i q c", c=D)
    PX = [PR[:, 1024 * i:1024 * (i + 1)] for i in range(4)] + \
         [W[:, a0 + 14336 + 1024 * i:a0 + 14336 + 1024 * (i + 1)] for i in range(2)]
    OS = W[:, a0 + 16384:a0 + 17408].rearrange("p (i n) -> p i n", i=2)
    m0i = W[:, 0:4096].bitcast(I32).rearrange("p (q n) -> p q n", q=4)
    mu0 = W[:, 4096:6144].bitcast(BF16).rearrange("p (q n) -> p q n", q=4)
    mu1 = W[:, a0:a0 + 4096].bitcast(BF16).rearrange("p (q n) -> p q n", q=8)
    m1i = W[:, a0 + 4096:a0 + 6144].bitcast(U8).rearrange("p (q n) -> p q n", q=8)
    xrT = W[0:16, a0:a0 + 1024]
    mc, mt, maskrow = [], [], []
    for o in (6144, a0 + 6144):
        mc.append(W[:, o:o + 512].rearrange("p (q n) -> p q n", q=2))
        mt.append(W[:, o + 512:o + 768])
        maskrow.append(W[0:1, o + 768:o + 1024].bitcast(BF16))
    NK = W[:, a0 + 16384:a0 + 17408].rearrange("p (t c) -> p t c", c=D)
    bsf = PR[0:8, 2048:2816]
    bsp = PR[0:8, 2816:3968].bitcast(BF16).rearrange("p (s n) -> p s n", s=3)

    ident = sb("ident", [128, 128], F32)
    identb = sb("identb", [128, 128], BF16)
    upper = sb("upper", [128, 128], BF16)
    onesb = sb("onesb", [128, 128], BF16)
    BS = sb("BS", [24, 768], BF16)
    flags = sb("flags", [128, 2], I32)
    fsum = sb("fsum", [128, 8], F32)
    junk = sb("junk", [128, 1], F32)
    zero = sb("zero", [128, 256], F32)
    MV = sb("MV", [128, 16, 2], F32)
    ST = sb("ST", [128, 16, 6], F32)
    NW = sb("NW", [128, 5, 16], F32)
    mx = sb("mx", [128, 2, 4, H], F32)
    msb = sb("msb", [128, 2, 4, 3, H], BF16)
    MT = sb("MT", [48, 2, 512], BF16)
    rlf = sb("rlf", [128, 4, 4], F32)
    nmx = sb("nmx", [128, H], F32)
    okr = sb("okr", [128, H], F32)
    rl = sb("rl", [128, H], F32)
    iota_e = sb("iota_e", [128, 8], F32)
    iota_j = sb("iota_j", [128, 8], F32)
    iota_t = sb("iota_t", [128, TILES1], F32)
    rowe = sb("rowe", [24, 1], F32)
    LG = sb("LG", [128, NT, 8], F32)
    R1 = sb("R1", [128, NT, 8], F32)
    R2 = sb("R2", [128, NT, 8], F32)
    OH = sb("OH", [128, 3, NT, 8], F32)
    OHb = sb("OHb", [128, NT, 8], BF16)
    RK = sb("RK", [128, 8, NT], F32)
    CN = sb("CN", [128, 2, 8, NT], F32)
    later = sb("later", [128, 8, NT], F32)
    one8 = sb("one8", [128, 8], F32)
    ne = sb("ne", [128, 4, 8], F32)
    nt8 = sb("nt8", [128, 8, 8], F32)
    te = CT[:, 1024:1024 + TILES1 * 8].rearrange("p (t e) -> p t e", e=8)
    tef = sb("tef", [128, TILES1], F32)
    tei = sb("tei", [128, TILES1 + 1], I32)
    posf = sb("posf", [128, 2, NT], F32)
    posi = sb("posi", [128, 2, NT], I32)
    gw = sb("gw", [128, 2, NT], F32)
    rs = sb("rs", [128, 6, NT], F32)
    wred = sb("wred", [128, 2, 16], F32)
    wr = sb("wr", [128, 2, E1], F32)
    rbb = sb("rbb", [128, E1], F32)
    wg = sb("wg", [8, 16], F32)
    wgs = sb("wgs", [8, 8], F32)
    wgn = sb("wgn", [8, 16], F32)
    wgT = sb("wgT", [16, 8], F32)

    PS = ctx.enter_context(nc.psum_tensor("PS", [128, 8, 512], F32))
    sd = nc.dram_tensor("scratch_split", [2, 3, D, 512], BF16).ap()
    md = nc.dram_tensor("scratch_max", [2, 3, H, 512], BF16).ap()
    mr = nc.dram_tensor("scratch_mask", [2, NB * FK], BF16).ap()
    bd = nc.dram_tensor("scratch_bias", [3, 8, 768], BF16).ap()
    xs = nc.dram_tensor("scratch_x", [TILES1 * 128, D], F32).ap()
    ys = nc.dram_tensor("scratch_y", [TILES1 * 128, D], F32).ap()

    def bb(ap, n):
        return ap.unsqueeze(len(ap.shape)).to_broadcast(list(ap.shape) + [n])

    def row_bc(ap):
        return ap.rearrange("(a n) -> a n", a=1).to_broadcast([128, ap.shape[0]])

    def evac(dst, src, t):
        ev[0] ^= 1
        if ev[0]:
            wait(act, t)
            return C(act.activation, dst, src, ACT.Copy)
        wait(dve, t)
        return V(dve.tensor_copy, dst, src)

    x_v = A["x"].rearrange("(t p) c -> p t c", p=128)
    ctx_v = A["ctxT"].rearrange("(k p) (b n) -> p k b n", p=128, b=NB)
    dma(act, "small", wg[:, :], A["L0_ffn_wg"])
    dma(act, "small", bsf[:, 0:F0], A["L0_ffn_b1"])
    t_small = dma(act, "small", bsf[:, F0:F0 + D], A["L0_ffn_b2"])
    t_x = []
    for b in range(NB):
        t_ct = dma(act, "ct", CTf[:, :, b * FK:(b + 1) * FK], ctx_v[:, :, b, SK - FK:SK])
    for b in range(NB):
        t_x.append(dma(act, f"x{b}", X[:, 4 * b:4 * b + 4, :], x_v[:, 4 * b:4 * b + 4, :]))
    dma(act, "small2", wred[:, :, :], A["L0_ffn_w_red"].rearrange("(k p) g -> p k g", p=128))
    dma(act, "small2", wr[:, :, :], A["L1_ffn_wrT"].rearrange("(k p) g -> p k g", p=128), allow_slow_non_contiguous=True)
    t_small2 = dma(act, "small2", rbb[:, :], row_bc(A["L1_ffn_rb"]))

    def load_proj(l, after):
        wait(sp, after)
        for i, n in enumerate(["bk", "bq"] if l == 0 else ["gk", "bk", "gq", "bq"]):
            t_c = dma(sp, "wpc", col[:, i, :], A[f"L{l}_xattn_{n}"].rearrange("(k p) -> p k", p=128),
                      allow_slow_non_contiguous=True)
        toks = [None] * 4
        for i, n in ((0, "Wk"), (2, "Wq"), (1, "Wv"), (3, "Wo"))[0:4 - l]:
            toks[i] = dma(sp, f"wp{i}", WP[:, i, :, :],
                          A[f"L{l}_xattn_{n}" + "T" * (1 - l)].rearrange("(k p) n -> p k n", p=128))
        for i, n in enumerate(["bv", "bo"] if l == 0 else ["gv", "bv"]):
            t_b = dma(sp, "wpb", BC[:, i, :], row_bc(A[f"L{l}_xattn_{n}"]))
        return toks + [t_c, t_b]

    def ones_rows(after):
        wait(sp, after)
        one = A["ones"].bitcast(BF16)
        dma(sp, "ones", QS[96:97, :, :], one.rearrange("a (h n) -> a h n", h=H))
        return dma(sp, "ones", KS[97:100, :, :],
                   one[:, 0:H * NB * FK].rearrange("a (h n) -> a h n", h=H).to_broadcast([3, H, NB * FK]))

    t_wp = load_proj(0, None)
    t_m0 = dma(sp, "m0", m0i, A["mask0"].rearrange("(q p) n -> p q n", p=128))
    t_one0 = ones_rows(None)

    t = G(pool.memset, ident[:, :], 0.0)
    G(pool.memset, onesb[:, :], 1.0)
    t_zero = G(pool.memset, zero[:, :], 0.0)
    t1 = G(pool.memset, upper[:, :], 1.0)
    wait(pool, t1)
    t = G(pool.iota, later[:, :, :], pattern=[[0, 8], [1, NT]], base=0, channel_multiplier=0, allow_small_or_imprecise_dtypes=True)
    wait(pool, t)
    G(pool.tensor_scalar, later[:, :, :], later[:, :, :], 0.0, None, ALU.is_gt)
    G(pool.memset, one8[:, :], 1.0)
    t_id = G(pool.affine_select, out=ident[:, :], in_=ident[:, :], compare_op=ALU.not_equal, fill=1.0, base=0,
             pattern=[[-1, 128]], channel_multiplier=1)
    t_up = G(pool.affine_select, out=upper[:, :], in_=upper[:, :], compare_op=ALU.is_gt, fill=0.0, base=0,
             pattern=[[1, 128]], channel_multiplier=-1)
    G(pool.iota, iota_e[:, :], pattern=[[1, 8]], base=0, channel_multiplier=0, allow_small_or_imprecise_dtypes=True)
    G(pool.iota, iota_j[:, :], pattern=[[128, 8]], base=0, channel_multiplier=0, allow_small_or_imprecise_dtypes=True)
    G(pool.iota, iota_t[:, :], pattern=[[1, TILES1]], base=0, channel_multiplier=0, allow_small_or_imprecise_dtypes=True)
    t_iota = G(pool.iota, rowe[:, :], pattern=[[0, 1]], base=0, channel_multiplier=1, allow_small_or_imprecise_dtypes=True)
    wait(dve, t_id, t_iota)
    V(dve.tensor_copy, identb[:, :], ident[:, :])
    for _ in range(2):
        t = VC(dve.tensor_scalar, junk[0:24, :], rowe[:, :], 8.0, -8.0, ALU.is_ge, ALU.mult)
        t_rowe = VC(dve.tensor_tensor, rowe[:, :], rowe[:, :], junk[0:24, :], ALU.add)

    def key_counts(l, b, mu, t_mu, bk=6):
        wait(pe, t_mu, t_iota, rel[bk], rel[bk + 1])
        for half in range(2):
            for q in range(4):
                m = put(pe, pe.matmul, PS[:, bk + half, :], onesb[:, :], mu[:, b * 4 + q, half * 512:(half + 1) * 512],
                        start=(q == 0), stop=(q == 3))
        wait(dve, inc(m, own_sem(pe, "pe")))
        c, u = mc[l][:, b, :], mt[l]
        flat = PS[:, bk:bk + 2, :].rearrange("p a n -> p (a n)")
        V(dve.tensor_reduce, fsum[:, b:b + 1], flat[:, 0:3 * FK], AX, ALU.add)
        rel[bk] = rel[bk + 1] = t = V(dve.tensor_copy, c, flat[:, 3 * FK:SK])
        wait(dve, t)
        V(dve.tensor_scalar, u, c, -1.0, 512.0, ALU.mult, ALU.add)
        VC(dve.tensor_reduce, fsum[:, 4 + b:5 + b], c, AX, ALU.add)
        VC(dve.tensor_tensor, u, u, c, ALU.mult)
        VC(dve.tensor_reduce, fsum[:, 2:3], u, AX, ALU.add)
        VC(dve.tensor_tensor, fsum[:, b:b + 1], fsum[:, b:b + 1], fsum[:, 2:3], ALU.add)

    def mask_row(l, nb, eng):
        for b in range(NB):
            t = V(dve.tensor_scalar, maskrow[l][:, b * FK:(b + 1) * FK], mc[l][0:1, b % nb, :], 0.0, -1.0e30,
                  ALU.is_equal, ALU.mult)
        wait(eng, t)
        t = dma(eng, f"mrow{l}", mr[l:l + 1, :], maskrow[l])
        wait(eng, t)
        return dma(eng, f"kb{l}", KS[96:97, :, :], mr[l:l + 1, :].unsqueeze(1).to_broadcast([1, H, NB * FK]))

    def flag_of(l, nb):
        for w in range(nb):
            VC(dve.tensor_scalar, fsum[:, w:w + 1], fsum[:, w:w + 1], 0.0, None, ALU.is_equal)
            VC(dve.tensor_scalar, fsum[:, 4 + w:5 + w], fsum[:, 4 + w:5 + w], 0.0, None, ALU.is_gt)
            VC(dve.tensor_tensor, fsum[:, w:w + 1], fsum[:, w:w + 1], fsum[:, 4 + w:5 + w], ALU.mult)
            if w:
                VC(dve.tensor_tensor, fsum[:, w:w + 1], fsum[:, w:w + 1], fsum[:, 0:1], ALU.mult)
        return VC(dve.tensor_copy, flags[:, l:l + 1], fsum[:, nb - 1:nb])

    wait(dve, t_small)
    VC(dve.tensor_copy, bsp[:, 0, :], bsf)
    VC(dve.tensor_tensor, bsf, bsf, bsp[:, 0, :], ALU.subtract)
    VC(dve.tensor_copy, bsp[:, 1, :], bsf)
    VC(dve.tensor_tensor, bsf, bsf, bsp[:, 1, :], ALU.subtract)
    t = VC(dve.tensor_copy, bsp[:, 2, :], bsf)
    wait(pool, t)
    t = dma(pool, "bd", bd.rearrange("s e n -> e s n"), bsp)
    wait(pool, t)
    t_bs = dma(pool, "bs", BS[:, :], bd.rearrange("s e n -> (s e) n"))

    def rsqrt(n, var, eps):
        a, b, y, t = (NW[:, i, 0:n] for i in range(4))
        V(dve.tensor_scalar, a, var, eps, -0.5, ALU.add, ALU.mult)
        VC(dve.tensor_scalar, b, var, eps, None, ALU.add)
        VC(dve.tensor_scalar, y.bitcast(I32), b.bitcast(I32), -0.5, MAGIC, ALU.mult, ALU.add)
        for _ in range(3):
            VC(dve.tensor_tensor, t, y, y, ALU.mult)
            VC(dve.tensor_tensor, t, t, a, ALU.mult)
            VC(dve.scalar_tensor_tensor, y, t, 1.5, y, ALU.add, ALU.mult)
        return y

    def stats(srcs, t_src):
        n = len(srcs)
        wait(dve, nw_free[0])
        for s, t in zip(srcs, t_src):
            wait(dve, t)
            t = V(dve.bn_stats, ST[:, srcs.index(s), :], s)
        wait(dve, t)
        for i in range(n):
            t = V(dve.bn_aggr, MV[:, i, :], ST[:, i, :])
        wait(dve, t)
        y = rsqrt(n, MV[:, 0:n, 1], EPS)
        t = VC(dve.scalar_tensor_tensor, NW[:, 4, 0:n], MV[:, 0:n, 0], -1.0, y, ALU.mult, ALU.mult)
        return y, NW[:, 4, 0:n], t

    def normalise(srcs, dsts, t_src, t_dst=None, alone=False):
        y, nb, t = stats(srcs, t_src)
        toks = []
        if not alone:
            wait(act, t, t_dst)
        wait(dve, t_dst)
        for i, (s, d) in enumerate(zip(srcs, dsts)):
            if i // 2 % 2 and not alone:
                toks.append(C(act.activation, d, s, ACT.Identity, bias=nb[:, i:i + 1], scale=y[:, i:i + 1]))
            else:
                toks.append(V(dve.tensor_scalar, d, s, MV[:, i, 0:1], y[:, i:i + 1], ALU.subtract, ALU.mult))
        nw_free[0] = toks[-2:]
        return toks

    def turn4(srcs, toks, banks, finish):
        for t in range(4):
            wait(pe, toks[t])
        wait(pe, t_id)
        outs = []
        for k in range(2):
            wait(pe, rel[banks[k]])
            for t in range(4):
                m = put(pe, pe.transpose, PS[:, banks[k], t * 128:(t + 1) * 128], srcs[t][:, k * 128:(k + 1) * 128],
                        ident[:, :])
            rel[banks[k]] = finish(k, banks[k], inc(m, own_sem(pe, "pe")))
            outs.append(rel[banks[k]])
        return outs

    def ln_turned(t_in):
        toks = normalise([X[:, t, :] for t in range(NT)], [XN[:, t, :] for t in range(NT)], t_in)
        return toks, [turn4([XN[:, 4 * g + j, :] for j in range(4)], toks[4 * g:4 * g + 4], (6, 7),
                            lambda k, bk, tk: evac(XT[:, k, g * 512:(g + 1) * 512], PS[:, bk, :], tk))
                      for g in range(2)]

    st = {}

    def split_chunk(t_f, dst, parts, t_dst, eng=sp):
        i = st["chunk"] % 2
        q = "" if eng is sp else "p"
        st["chunk"] += 1
        f = FE[:, i, :, :]
        p = [SP[:, i, s, :, :] for s in range(3)]
        wait(act, t_f, st["sp_free"][i])
        t = C(act.activation, p[0], f, ACT.Copy)
        wait(dve, t, t_f)
        t = V(dve.tensor_tensor, f, f, p[0], ALU.subtract)
        wait(act, t)
        t = C(act.activation, p[1], f, ACT.Copy)
        wait(dve, t)
        t = VC(dve.tensor_tensor, f, f, p[1], ALU.subtract)
        t2 = V(dve.tensor_copy, p[2], f)
        st["fe_free"][i] = t2
        wait(eng, t2)
        for s in range(3):
            tw = dma(eng, f"so{i}{q}", sd[i, s].rearrange("(k p) n -> p k n", p=128), p[s])
        st["sp_free"][i] = tw
        wait(eng, tw, t_dst)
        for r, s in enumerate(parts):
            td = dma(eng, f"si{i}{q}", dst[16 * r:16 * r + 16], sd[i, s].rearrange("(h d) n -> d h n", d=HD))
        return td

    def project_turned(wi, ci, scale, src, t_src):
        i = st["chunk"] % 2
        toks = []
        for fb in range(2):
            bk = fb
            wait(pe, t_wp[wi], t_src, rel[bk])
            for k in range(2):
                m = put(pe, pe.matmul, PS[:, bk, :], WP[:, wi, k, fb * 128:(fb + 1) * 128], src[:, k, :],
                        start=(k == 0), stop=(k == 1))
            tk = inc(m, own_sem(pe, "pe"))
            wait(dve, tk, st["fe_free"][i], t_wp[4])
            rel[bk] = V(dve.tensor_scalar, FE[:, i, fb, :], PS[:, bk, :], col[:, ci, fb:fb + 1], scale, ALU.add, ALU.mult)
            toks.append(rel[bk])
        return toks

    def rows_of(wi, src, cols, banks, t_src):
        toks = []
        for j, c in enumerate(cols):
            bk = banks[j // 2]
            if j % 2 == 0:
                wait(pe, t_wp[wi], t_src, rel[bk])
            for k in range(2):
                m = put(pe, pe.matmul, PS[:, bk, (j % 2) * 256:(j % 2 + 1) * 256], src[:, k, c:c + 128], WP[:, wi, k, :],
                        start=(k == 0), stop=(k == 1))
            tk = inc(m, own_sem(pe, "pe"))
            toks.append(tk)
        return toks, [PS[:, banks[j // 2], (j % 2) * 256:(j % 2 + 1) * 256] for j in range(len(cols))]

    def project_normed(wi, gi, scale, src, cols, t_src, nr, t_nr, banks=(2, 3), NR=NR):
        i = st["chunk"] % 2
        tks, ps = rows_of(wi, src, cols, banks, t_src)
        for b_ in banks:
            wait(dve, tks[-1])
        nrs = [NR[:, nr + j, :] for j in range(4)]
        toks = normalise(ps, nrs, [tks[1], tks[1], tks[3], tks[3]], t_nr)
        for j, b_ in enumerate(banks):
            rel[b_] = [toks[2 * j], toks[2 * j + 1]]

        def finish(k, bk, tk):
            wait(dve, tk, st["fe_free"][i], t_wp[4])
            t = VC(dve.tensor_scalar, FE[:, i, k, :], PS[:, bk, :], col[:, gi, k:k + 1], col[:, gi + 1, k:k + 1],
                   ALU.mult, ALU.add)
            if scale != 1.0:
                t = V(dve.tensor_scalar, FE[:, i, k, :], FE[:, i, k, :], scale, None, ALU.mult)
            return t

        return turn4(nrs, toks, (0, 1), finish)

    def values(l, src, cols, v0, t_src, t_free, banks, nr=0, t_nr=None):
        toks = []
        wait(dve, t_free)
        t = VC(dve.memset, VR[:, v0 * VT:(v0 + len(cols)) * VT], 1.0)
        for c in range(0, len(cols), 4):
            tks, ps = rows_of(1, src, cols[c:c + 4], banks, t_src)
            dst = [VV[:, v0 + c + j, 0:H * VW].rearrange("p (h v) -> p h v", v=VW)[:, :, 0:HD] for j in range(4)]
            bc = [BC[:, i, :].rearrange("p (h d) -> p h d", d=HD) for i in range(2)]
            if l == 0:
                for j in range(4):
                    wait(dve, tks[j // 2 * 2 + 1], t_wp[5])
                    tv = V(dve.tensor_tensor, dst[j], ps[j].rearrange("p (h d) -> p h d", d=HD), bc[0], ALU.add)
                    toks.append(tv)
                    rel[banks[j // 2]] = tv
            else:
                nrs = [NR[:, nr + j, :] for j in range(4)]
                tn = normalise(ps, nrs, [tks[1], tks[1], tks[3], tks[3]], t_nr)
                for j, b_ in enumerate(banks):
                    rel[b_] = [tn[2 * j], tn[2 * j + 1]]
                wait(pool, t, t_wp[5])
                for j in range(4):
                    wait(pool, tn[j])
                    tg = G(pool.tensor_tensor, nrs[j], nrs[j], BC[:, 0, :], ALU.mult)
                    wait(pool, tg)
                    tv = G(pool.tensor_tensor, dst[j], nrs[j].rearrange("p (h d) -> p h d", d=HD), bc[1], ALU.add)
                    toks.append(tv)
                t_nr = tv
        return toks

    def start_attention():
        st.clear()
        st.update(chunk=0, fe_free=[None, None], sp_free=[None, None])
        nw_free[0] = None

    KCOLS = [128 * j for j in range(4)]

    def keys0():
        start_attention()
        t_f = project_turned(0, 0, 1.0, CTf, t_ct)
        return split_chunk(t_f, KS[:, :, :], K_PART, None)

    def queries(l, b, t_src, nr, banks):
        if l == 0:
            t_f = project_turned(2, 1, 0.25, XT[:, :, 512 * b:512 * b + 512], t_src)
        else:
            t_f = project_normed(2, 2, 0.25, XT, [512 * b + c for c in KCOLS], t_src, nr, None, banks)
        return split_chunk(t_f, QS[:, :, 512 * b:512 * b + 512], Q_PART, None)

    def normed_keys1():
        start_attention()
        tks, ps = rows_of(0, CTf, KCOLS, (2, 3), t_ct)
        toks = normalise(ps, [NK[:, j, :] for j in range(4)], [tks[1], tks[1], tks[3], tks[3]])
        rel[2], rel[3] = toks[0:2], toks[2:4]
        return toks

    def masks_keys1(toks, t_s, t_mu, made):
        start_attention()
        nrs = [NK[:, j, :] for j in range(4)]

        def finish(k, bk, tk):
            wait(dve, tk, t_s, t_wp[4])
            return V(dve.tensor_scalar, FE[:, 0, k, :], PS[:, bk, :], col[:, 0, k:k + 1], col[:, 1, k:k + 1], ALU.mult, ALU.add)

        t_f = turn4(nrs, toks, (2, 3), finish)
        yield
        made["ks"] = split_chunk(t_f, KS[:, :, :], K_PART, None, eng=pool)
        yield
        for b in range(NB):
            key_counts(1, b, mu1, t_mu, 2)
            yield
        made["kb"] = mask_row(1, 2, pool)
        made["flag"] = flag_of(1, 2)


    def front(l, t_src):
        rows = [OB[:, t // 4, t % 4, :] for t in range(NT)]
        toks = normalise([X[:, t, :] for t in range(NT)], rows, [t_src] * NT, t_src)
        xt = [turn4(rows[4 * b:4 * b + 4], toks[4 * b:4 * b + 4], (6, 7),
                    lambda k, bk, tk: evac(XT[:, k, b * 512:(b + 1) * 512], PS[:, bk, :], tk)) for b in range(NB)]
        n = (E0, E1)[l]
        wait(pe, t_small2, t_wgT, rel[5])
        for b in range(NB if l == 0 else 0):
            wait(pe, xt[b], rel[b])
            for k in range(2):
                m = put(pe, pe.matmul, PS[0:16, b, :], wred[:, k, :], XT[:, k, b * 512:(b + 1) * 512], start=(k == 0), stop=(k == 1))
            rel[b] = evac(xrT[:, b * 512:(b + 1) * 512], PS[0:16, b, :], inc(m, own_sem(pe, "pe")))
        for t in range(NT):
            if l == 0:
                wait(pe, rel[t // 4])
                m = put(pe, pe.matmul, PS[:, 5, t * 8:(t + 1) * 8], xrT[:, t * 128:(t + 1) * 128], wgT[:, :], start=True, stop=True)
            else:
                wait(pe, xt[t // 4])
                for k in range(2):
                    m = put(pe, pe.matmul, PS[:, 5, t * 8:t * 8 + E1], XT[:, k, t * 128:(t + 1) * 128], wr[:, k, :],
                            start=(k == 0), stop=(k == 1))
        wait(dve, inc(m, own_sem(pe, "pe")), t_small2)
        ps, lg = PS[:, 5, 0:64].rearrange("p (t e) -> p t e", e=8)[:, :, 0:n], LG[:, :, 0:n]
        if l == 0:
            rel[5] = V(dve.tensor_copy, lg, ps)
        else:
            rel[5] = V(dve.tensor_tensor, lg, ps, rbb[:, :].unsqueeze(1).to_broadcast([128, NT, E1]), ALU.add)
        return toks + xt + [rel[5]]

    def attention_fast(l, t_in, t_ks, t_q0, prefetch):
        def body():
            keys, first = [t_ks], t_q0
            if l == 1:
                start_attention()
                for e in (pool, act, dve, sp, pe):
                    wait(e, t_in)
                keys.append(ones_rows(None))
                toks, xt = ln_turned([t_in] * NT)
                first = [queries(1, 0, xt[0], 4, (4, 5)), queries(1, 1, xt[1], 0, (2, 3))]
            return attend(l, t_in, keys, first, prefetch)

        return body

    def attend(l, t_in, t_ks, t_q, prefetch):
        prefetch(0)
        pair = [0]

        def next_pair():
            p = pair[0] % 3
            pair[0] += 1
            return 2 * p

        def score_max(b, u):
            qb, hg = u // 4, u % 4
            b0 = next_pair()
            wait(pe, t_q[b], t_ks, rel[b0], rel[b0 + 1])
            for j in range(4):
                h = 4 * hg + j
                m = put(pe, pe.matmul, PS[:, b0 + j // 2, (j % 2) * FK:(j % 2 + 1) * FK],
                        QS[0:NS + 1, h, (4 * b + qb) * 128:(4 * b + qb + 1) * 128],
                        KS[0:NS + 1, h, b * FK:(b + 1) * FK], start=True, stop=True)
            wait(dve, inc(m, own_sem(pe, "pe")))
            t = V(dve.tensor_reduce, mx[:, b, qb, 4 * hg:4 * hg + 4],
                  PS[:, b0:b0 + 2, :].rearrange("p a (j n) -> p (a j) n", n=FK), AX, ALU.max)
            rel[b0] = rel[b0 + 1] = t
            return t

        def max_rows(b):
            m_ = mx[:, b, :, :]
            wait(dve, seen_dve())
            VC(dve.tensor_scalar, m_, m_, -1.0, None, ALU.mult)
            for s in range(3):
                VC(dve.tensor_copy, msb[:, b, :, s, :], m_)
                if s < 2:
                    t = VC(dve.tensor_tensor, m_, m_, msb[:, b, :, s, :], ALU.subtract)
            wait(pe, seen_dve(), rel[7], t_idb)
            pb = PS[0:48, 7, 0:256].bitcast(BF16)
            for qb in range(4):
                m = put(pe, pe.transpose, pb[:, qb * 128:(qb + 1) * 128],
                        msb[:, b, qb, :, :].rearrange("p s h -> p (s h)"), identb[:, :])
            wait(dve, inc(m, own_sem(pe, "pe")))
            t = V(dve.tensor_copy, MT[:, b, :], pb)
            rel[7] = t
            wait(sp, t)
            t = dma(sp, f"mo{b}", md[b].rearrange("s h n -> (s h) n"), MT[:, b, :])
            wait(sp, t, t_q[b])
            return dma(sp, f"mi{b}", QS[97:100, :, b * 512:(b + 1) * 512], md[b])

        px_free = []
        px_tok = [None] * 6
        n_exp = [0]

        def weights_of(b, h, t_m):
            b0 = next_pair()
            wait(pe, t_m, rel[b0], rel[b0 + 1])
            for kb in range(2):
                m = put(pe, pe.matmul, PS[:, b0 + kb, :],
                        KS[0:NS + 4, h, b * FK + kb * 128:b * FK + (kb + 1) * 128],
                        QS[0:NS + 4, h, b * 512:(b + 1) * 512], start=True, stop=True)
            slot = n_exp[0] % 6
            n_exp[0] += 1
            wait(act, inc(m, own_sem(pe, "pe")), px_free[slot])
            t = C(act.activation, PX[slot], PS[:, b0:b0 + 2, :].rearrange("p a n -> p (a n)"), ACT.Exp)
            rel[b0] = rel[b0 + 1] = t
            px_tok[slot] = t
            return slot

        def combine(b, g, slots):
            wait(pe, t_v[-1], t_v[-2], rel[6])
            for kb in range(2):
                for j in range(4):
                    h = 4 * g + j
                    wait(pe, px_tok[slots[j]])
                    m = put(pe, pe.matmul, PS[32 * j:32 * j + 32, 6, :],
                            VV[:, 2 * b + kb, h * VW:h * VW + 32],
                            PX[slots[j]][:, kb * 512:(kb + 1) * 512], start=(kb == 0), stop=(kb == 1),
                            skip_group_check=True)
            tk = inc(m, own_sem(pe, "pe"))
            for s in slots:
                px_free[s] = tk
            i = g % 2
            wait(act, tk, st.get(("os", i)), t_q[1])
            t = C(act.activation, OS[:, i, :], PS[:, 6, :], ACT.Copy)
            rel[6] = t
            return t

        def divide(b, g, t_os):
            i = g % 2
            wait(pe, t_os, rel[7])
            for qb in range(4):
                m = put(pe, pe.transpose, PS[:, 7, qb * 128:(qb + 1) * 128], OS[:, i, qb * 128:(qb + 1) * 128],
                        ident[:, :])
            tk = inc(m, own_sem(pe, "pe"))
            st[("os", i)] = tk
            wait(dve, tk)
            o = PS[:, 7, :].rearrange("p (q j v) -> p q j v", q=4, v=32)
            VC(dve.reciprocal, rlf[:, :, :], o[:, :, :, HD])
            dst = OB[:, b, :, 64 * g:64 * (g + 1)].rearrange("p q (j d) -> p q j d", d=HD)
            t = V(dve.tensor_tensor, dst, o[:, :, :, 0:HD], bb(rlf[:, :, :], HD), ALU.mult)
            rel[7] = t
            return t

        fin = []

        def close(b, t_o):
            x = X[:, 4 * b:4 * b + 4, :]
            if l == 1:
                wait(dve, t_o)
                return V(dve.tensor_tensor, x, x, OB[:, b, :, :], ALU.add)
            xo = turn4([OB[:, b, j, :] for j in range(4)], [t_o] * 4, (6, 7),
                       lambda k, bk, tk: evac(XT[:, k, b * 512:(b + 1) * 512], PS[:, bk, :], tk))
            tks, ps = rows_of(3, XT, [b * 512 + 128 * j for j in range(4)], (6, 7), xo)
            wait(dve, t_xb)
            for j in range(2):
                wait(dve, tks[2 * j + 1])
                xj = X[:, 4 * b + 2 * j:4 * b + 2 * j + 2, :]
                rel[6 + j] = V(dve.tensor_tensor, xj, xj, PS[:, 6 + j, :].rearrange("p (t c) -> p t c", c=D), ALU.add)
            return rel[7]

        t_xb = None
        if l == 0:
            wait(pool, t_q, t_x, t_wp[5])
            t_xb = G(pool.tensor_tensor, X[:, :, :], X[:, :, :], BC[:, 1, :].unsqueeze(1).to_broadcast([128, NT, D]), ALU.add)
        for u in range(16):
            score_max(0, u)
            if u == 7:
                t_v = values(l, CTf, KCOLS, 0, t_ct, None if l == 0 else t_in, (2, 3), 4)
        px_free += [t_v + t_q + [t_bs]] * 6
        t_mi0 = max_rows(0)
        prefetch(1)
        t_mi1 = None
        slots, t_os, t_o = [], {}, {}
        u = 0
        for n in range(2 * H):
            b, h = n // H, n % H
            for _ in range(3 if n == 0 else 1):
                if u < 16:
                    score_max(1, u)
                    u += 1
            if u == 16 and t_mi1 is None:
                t_mi1 = max_rows(1)
                prefetch(2)
            slots.append(weights_of(b, h, t_mi1 if b else t_mi0))
            g = n // 4 - 1
            if n % 4 == 1 and g >= 0:
                t_os[g] = combine(g // 4, g % 4, slots[4 * g:4 * g + 4])
            if n % 4 == 2 and g >= 0:
                t_o[g] = divide(g // 4, g % 4, t_os[g])
            if n == 19:
                t_c0 = close(0, t_o[3])
        t_os[7] = combine(1, 3, slots[28:32])
        t_o[7] = divide(1, 3, t_os[7])
        fin += front(l, [t_c0, close(1, t_o[7])])
        return fin + [t_o[7], px_free[0], px_free[1]]

    def attention_general(l, t_in, prefetch):
        def body():
            start_attention()
            for e in (pool, act, dve, sp, pe):
                wait(e, t_in)
            toks, xt = ln_turned([t_in] * NT)
            t_prev = xt[0] + xt[1]
            t_last = None
            fin = []
            for b in range(NB):
                wait(sp, t_prev)
                t_c = dma(sp, "ctg", CTg, ctx_v[:, :, b, :])
                t_ks = []
                for c in range(2):
                    src = CTg[:, :, c * 512:(c + 1) * 512]
                    if l == 0:
                        t_f = project_turned(0, 0, 1.0, src, t_c)
                    else:
                        t_f = project_normed(0, 0, 1.0, CTg, [512 * c + 128 * j for j in range(4)], t_c, 0, t_prev)
                    t_ks.append(split_chunk(t_f, KSg[:, :, c * 512:(c + 1) * 512], K_PART, t_prev))
                if l == 0:
                    t_f = project_turned(2, 1, 0.25, XT[:, :, b * 512:(b + 1) * 512], t_prev)
                else:
                    t_f = project_normed(2, 2, 0.25, XT, [512 * b + 128 * j for j in range(4)], t_prev, 0, None)
                t_q = split_chunk(t_f, QSg[:, :, :], Q_PART, t_prev)
                t_v = values(l, CTg, [128 * j for j in range(8)], 0, t_c, t_prev, (2, 3), 0, t_prev)
                t_prep = [t_q] + t_ks + t_v
                for e in (sp, dve, pe, act):
                    wait(e, t_prep)
                t_pt = None
                t_mb = t_sm = None
                sm_free = [None, None]
                for qb in range(4):
                    wait(sp, t_mb)
                    if l == 0:
                        t_m = dma(sp, "mask", MIg, A["mask0"][qb * 128:(qb + 1) * 128, :])
                        src, val = MIg, BIG
                    else:
                        t_m = dma(sp, "mask", MUg, A["mask1"][b, qb * 128:(qb + 1) * 128, :])
                        src, val = MUg, -1.0e9
                    wait(dve, t_m)
                    t_mb = VC(dve.tensor_scalar, MBg, src, 0.0, val, ALU.is_equal, ALU.mult)
                    for h in range(H):
                        p = h % 2
                        wait(pe, rel[2 * p], rel[2 * p + 1])
                        for half in range(2):
                            m = put(pe, pe.matmul, PS[:, 2 * p + half, :], QSg[0:NS, h, qb * 128:(qb + 1) * 128],
                                    KSg[0:NS, h, half * 512:(half + 1) * 512], start=True, stop=True)
                        wait(dve, inc(m, own_sem(pe, "pe")), sm_free[p])
                        t_s = VC(dve.tensor_tensor_reduce, out=SMg[:, p, :],
                                 in0=PS[:, 2 * p:2 * p + 2, :].rearrange("p a n -> p (a n)"), in1=MBg, scale=1.0,
                                 scalar=-3.4e38, op0=ALU.add, op1=ALU.max, accum_out=rl[:, h:h + 1])
                        rel[2 * p] = rel[2 * p + 1] = t_s
                        t_n = V(dve.tensor_scalar, nmx[:, h:h + 1], rl[:, h:h + 1], -1.0, None, ALU.mult)
                        wait(act, t_n)
                        t_e = C(act.activation, SMg[:, p, :], SMg[:, p, :], ACT.Exp, bias=nmx[:, h:h + 1])
                        wait(pe, t_e)
                        for half in range(2):
                            bk = 4 + half
                            wait(pe, rel[bk])
                            for j in range(4):
                                kb = half * 4 + j
                                m = put(pe, pe.transpose, PS[:, bk, j * 128:(j + 1) * 128],
                                        SMg[:, p, kb * 128:(kb + 1) * 128], ident[:, :])
                            tk = inc(m, own_sem(pe, "pe"))
                            wait(act, t_pt)
                            wait(dve, t_pt)
                            rel[bk] = evac(PTg[:, half * 512:(half + 1) * 512], PS[:, bk, :], tk)
                        sm_free[p] = tk
                        wait(pe, rel[4], rel[5], rel[6] if h == 0 else None)
                        for kb in range(8):
                            m = put(pe, pe.matmul, PS[:, 6, h * VW:(h + 1) * VW], PTg[:, kb * 128:(kb + 1) * 128],
                                    VV[:, kb, h * VW:(h + 1) * VW], start=(kb == 0), stop=(kb == 7))
                        t_pt = inc(m, own_sem(pe, "pe"))
                    wait(dve, t_pt)
                    o = PS[:, 6, 0:H * VW].rearrange("p (h v) -> p h v", v=VW)
                    if l == 0:
                        VC(dve.tensor_scalar, okr[:, :], rl[:, :], -1.0e38, None, ALU.is_gt)
                    VC(dve.tensor_copy, rl[:, :], o[:, :, HD])
                    if l == 0:
                        VC(dve.tensor_tensor, rl[:, :], rl[:, :], okr[:, :], ALU.mult)
                    VC(dve.reciprocal, rl[:, :], rl[:, :])
                    ob = OB[:, b, qb, :]
                    wait(dve, t_prep)
                    t_o = V(dve.tensor_tensor, ob.rearrange("p (h d) -> p h d", d=HD), o[:, :, 0:HD], bb(rl[:, :], HD), ALU.mult)
                    rel[6] = t_o
                    x = X[:, 4 * b + qb, :]
                    wait(dve, t_o)
                    if l == 1:
                        t_last = VC(dve.tensor_tensor, x, x, ob, ALU.add)
                    else:
                        c0 = (4 * b + qb) * 128
                        wait(pe, t_o, rel[7])
                        for k in range(2):
                            m = put(pe, pe.transpose, PS[:, 7, k * 128:(k + 1) * 128], ob[:, k * 128:(k + 1) * 128], ident[:, :])
                        wait(dve, inc(m, own_sem(pe, "pe")))
                        t = VC(dve.tensor_copy, XT[:, :, c0:c0 + 128], PS[:, 7, 0:256].rearrange("p (k n) -> p k n", k=2))
                        wait(pe, t)
                        for k in range(2):
                            m = put(pe, pe.matmul, PS[:, 7, 256:512], XT[:, k, c0:c0 + 128], WP[:, 3, k, :],
                                    start=(k == 0), stop=(k == 1))
                        wait(dve, inc(m, own_sem(pe, "pe")))
                        rel[7] = VC(dve.tensor_tensor, x, x, PS[:, 7, 256:512], ALU.add)
                        t_last = VC(dve.tensor_tensor, x, x, BC[:, 1, :], ALU.add)
                t_prev = [t_last, t_pt, t_e]
                fin += t_prev
            wait(sp, t_prev)
            for b in range(NB):
                t_c = dma(sp, "ctb", CTf[:, :, b * FK:(b + 1) * FK], ctx_v[:, :, b, SK - FK:SK])
            for i in range(3):
                prefetch(i)
            fin += front(l, t_prev)
            return fin + [t_c]

        return body

    def first_max(P, n, oh, mrow, idx):
        VC(dve.tensor_reduce, mrow, P, AX, ALU.max)
        r2 = R2[:, :, 0:n]
        VC(dve.tensor_tensor, r2, P, bb(mrow, n), ALU.not_equal)
        VC(dve.scalar_tensor_tensor, r2, r2, 100.0, iota_e[:, 0:n].unsqueeze(1).to_broadcast([128, NT, n]), ALU.mult, ALU.add)
        yield
        VC(dve.tensor_reduce, idx, r2, AX, ALU.min)
        VC(dve.tensor_tensor, oh, r2, bb(idx, n), ALU.is_equal)
        yield

    def softmax_rows(n):
        lg, p = LG[:, :, 0:n], R1[:, :, 0:n]
        VC(dve.tensor_reduce, rs[:, 0, :], lg, AX, ALU.max)
        wait(act, VC(dve.tensor_tensor, lg, lg, bb(rs[:, 0, :], n), ALU.subtract))
        t = C(act.activation, p, lg, ACT.Exp)
        yield
        wait(dve, t)
        VC(dve.tensor_reduce, rs[:, 1, :], p, AX, ALU.add)
        VC(dve.reciprocal, rs[:, 2, :], rs[:, 1, :])
        VC(dve.tensor_tensor, p, p, bb(rs[:, 2, :], n), ALU.mult)
        yield

    def expert_directions():
        wait(dve, t_small)
        VC(dve.tensor_tensor, wgn[:, :], wg[:, :], wg[:, :], ALU.mult)
        VC(dve.tensor_reduce, wgs[:, 0:1], wgn[:, :], AX, ALU.add)
        VC(dve.tensor_scalar, wgs[:, 1:2], wgs[:, 0:1], 1e-8, None, ALU.max)
        VC(dve.tensor_scalar, wgs[:, 2:3].bitcast(I32), wgs[:, 1:2].bitcast(I32), -0.5, MAGIC, ALU.mult, ALU.add)
        for _ in range(4):
            VC(dve.tensor_tensor, wgs[:, 3:4], wgs[:, 2:3], wgs[:, 2:3], ALU.mult)
            VC(dve.tensor_tensor, wgs[:, 3:4], wgs[:, 3:4], wgs[:, 1:2], ALU.mult)
            VC(dve.tensor_scalar, wgs[:, 3:4], wgs[:, 3:4], -0.5, 1.5, ALU.mult, ALU.add)
            VC(dve.tensor_tensor, wgs[:, 2:3], wgs[:, 2:3], wgs[:, 3:4], ALU.mult)
        t = VC(dve.tensor_scalar, wgn[:, :], wg[:, :], wgs[:, 2:3], None, ALU.mult)
        wait(pe, t, t_id, rel[6])
        tk = M(pe.transpose, PS[0:16, 6, 0:8], wgn[:, :], ident[0:8, 0:8])
        wait(dve, tk)
        rel[6] = VC(dve.tensor_copy, wgT[:, :], PS[0:16, 6, 0:8])
        return rel[6]

    def routes(n, choices, oh_all, counts, made):
        ntile = counts[2]
        VC(dve.tensor_copy, OHb[:, :, 0:n], oh_all)
        ob = OHb[:, :, 0:n]
        wait(pe, seen_dve(), t_up, rel[7])
        put(pe, pe.matmul, PS[:, 7, 0:NT * n], upper[:, :], ob, start=True, stop=True)
        tk = M(pe.matmul, PS[:, 7, 64:64 + NT * n], onesb[:, :], ob, start=True, stop=True)
        yield
        wait(dve, tk)
        rk = RK[:, 0:n, :]
        cn, run = (CN[:, i, 0:n, :] for i in range(2))
        V(dve.tensor_copy, rk, PS[:, 7, 0:NT * n].rearrange("p (t e) -> p e t", e=n))
        rel[7] = VC(dve.tensor_copy, cn, PS[:, 7, 64:64 + NT * n].rearrange("p (t e) -> p e t", e=n))
        flat = [a.rearrange("p e t -> p (e t)") for a in (run, later[:, 0:n, :], cn)]
        VC(dve.tensor_tensor_scan, flat[0], flat[1], flat[2], 0.0, ALU.mult, ALU.add)
        tot, tl, base, ends = run[:, :, NT - 1], ne[:, 1, 0:n], ne[:, 2, 0:n], ne[:, 3, 0:n]
        V(dve.memset, ends, 1.0)
        c8 = nt8[:, 0:n, 0:7]
        VC(dve.tensor_tensor, c8, bb(tot, 7), iota_j[:, 1:8].unsqueeze(1).to_broadcast([128, n, 7]), ALU.is_gt)
        yield
        VC(dve.tensor_reduce, tl, c8, AX, ALU.add)
        V(dve.tensor_tensor, run, run, cn, ALU.subtract)
        VC(dve.tensor_tensor, tl, tl, ends, ALU.add)
        VC(dve.tensor_tensor_scan, ends, one8[:, 0:n], tl, 0.0, ALU.mult, ALU.add)
        VC(dve.tensor_tensor, base, ends, tl, ALU.subtract)
        yield
        V(dve.tensor_tensor, rk, rk, run, ALU.add)
        VC(dve.tensor_scalar, ne[:, 0, 0:n], base, 128.0, None, ALU.mult)
        VC(dve.tensor_tensor, rk, rk, bb(ne[:, 0, 0:n], NT), ALU.add)
        yield
        for c, oh in enumerate(choices):
            VC(dve.tensor_tensor, R2[:, :, 0:n], rk.rearrange("p e t -> p t e"), oh, ALU.mult)
            VC(dve.tensor_reduce, posf[:, c, :], R2[:, :, 0:n], AX, ALU.add)
            made["p"] = V(dve.tensor_copy, posi[:, c, :], posf[:, c, :])
            yield
        t3 = te[:, 0:ntile, 0:n]
        total, way, more = ends[:, n - 1:n], ne[:, 1, 0:1], ne[:, 1, 1:2]
        V(dve.tensor_scalar, way, total, counts[0] + 0.5, None, ALU.is_gt)
        V(dve.tensor_scalar, more, total, counts[1] + 0.5, None, ALU.is_gt)
        VC(dve.tensor_tensor, t3, bb(iota_t[:, 0:ntile], n), base.unsqueeze(1).to_broadcast([128, ntile, n]), ALU.is_ge)
        V(dve.tensor_tensor, tei[:, TILES1:TILES1 + 1], way, more, ALU.add)
        VC(dve.tensor_reduce, tef[:, 0:ntile], t3, AX, ALU.add)
        VC(dve.tensor_scalar, tef[:, 0:ntile], tef[:, 0:ntile], -1.0, None, ALU.add)
        made["te"] = made["way"] = VC(dve.tensor_copy, tei[:, 0:ntile], tef[:, 0:ntile])

    def scatter(nc_, toks, t_p, t_free):
        wait(pool, t_p, t_free, t_w0["xz"])
        for t in toks:
            wait(pool, t)
        for c in range(nc_):
            for t in range(NT):
                off = bass.IndirectOffsetOnAxis(ap=posi[:, c, t:t + 1].bitcast(U32), axis=0)
                tk = inc(put(pool, pool.indirect_dma_start, xs, off, OB[:, t // 4, t % 4, :], None), s_scatter, 16)
        return tk

    def gather(c, t, dst, t_w, ntile):
        wait(pool, t_w)
        off = bass.IndirectOffsetOnAxis(ap=posi[:, c, t:t + 1].bitcast(U32), axis=0)
        key = f"gt{c}{t}"
        if key not in dsem:
            dsem[key] = sem(key)
        return inc(put(pool, pool.indirect_dma_start, dst, None, ys[0:ntile * 128, :], off), dsem[key], 16)

    s_scatter = sem("s_scatter")

    def load_x(i, t_in):
        p = i % 2
        wait(sp, t_in, fl["xl"][p])
        t = dma(sp, f"xl{p}", XL[:, p, :], xs[i * 128:(i + 1) * 128, :])
        return t

    fl = {}

    def turn_x(i, t_l):
        p = i % 2
        wait(pe, t_l, rel[7])
        for k in range(2):
            m = put(pe, pe.transpose, PS[:, 7, k * 128:(k + 1) * 128], XL[:, p, k * 128:(k + 1) * 128], ident[:, :])
        tk = inc(m, own_sem(pe, "pe"))
        fl["xl"][p] = tk
        wait(dve, tk, fl["xs"][p])
        t = V(dve.tensor_copy, XS[:, p, :, :], PS[:, 7, 0:256].rearrange("p (k n) -> p k n", k=2))
        rel[7] = t
        return t

    def expert(i, hold, n):
        hold["v"] = pe.value_load(tei[0:1, i:i + 1], min_val=0, max_val=n - 1)

    def turn_h(i, nj, nh, t_h):
        p = i % 2
        rows = [min(128, nh - 128 * j) for j in range(nj)]
        wait(pe, t_h, rel[4], rel[5] if nj > 4 else None)
        for j in range(nj):
            m = put(pe, pe.transpose, PS[0:rows[j], 4 + j // 4, (j % 4) * 128:(j % 4 + 1) * 128],
                    HB[:, p, j * 128:j * 128 + rows[j]], ident[:, :])
            if j == 3:
                tk4 = inc(m, own_sem(pe, "pe"))
        tk = tk4 if nj == 4 else inc(m, own_sem(pe, "pe"))
        fl["hb"][p] = tk
        if nj == 4:
            wait(dve, tk4, fl["ht"][p])
            rel[4] = V(dve.tensor_copy, HT[:, p, 0:4, :].rearrange("p j n -> p (j n)"), PS[:, 4, :])
            return [rel[4]]
        wait(act, tk4, fl["ht"][p])
        rel[4] = C(act.activation, HT[:, p, 0:4, :].rearrange("p j n -> p (j n)"), PS[:, 4, :], ACT.Copy)
        wait(dve, tk, fl["ht"][p])
        V(dve.tensor_copy, HT[:, p, 4, :], PS[:, 5, 0:128])
        rel[5] = V(dve.tensor_copy, HT[0:64, p, 5, :], PS[0:64, 5, 128:256])
        return [rel[4], rel[5]]

    def down(i, nj, nh, hold, base, stride, t_h, bias):
        p = i % 2
        wait(pe, t_h, rel[6])
        for j in range(nj):
            r = min(128, nh - 128 * j)
            o = base + j * D
            m = put(pe, lambda r=r, o=o, j=j, p=p: pe.matmul(
                PS[:, 6, 0:D], HT[0:r, p, j, :], W[0:r, bass.ds(hold["v"] * stride + o, D)],
                start=(j == 0), stop=(j == nj - 1 and not bias)))
        if bias:
            m = put(pe, pe.matmul, PS[:, 6, 0:D], OHE[0:24, i, :], BS[:, F0:F0 + D], start=False, stop=True)
        tk = inc(m, own_sem(pe, "pe"))
        fl["ht"][p] = tk
        return tk

    def store_y(i, tk):
        wait(act, tk, fl["yo"][0])
        t = C(act.activation, YO, PS[:, 6, 0:D], ACT.Copy)
        rel[6] = t
        wait(sp, t)
        fl["yo"][0] = dma(sp, "yo", ys[i * 128:(i + 1) * 128, :], YO)
        return fl["yo"][0]

    def up0(i, hold, t_x_, t_w):
        p, bk = i % 2, i % 2
        wait(pe, t_x_, t_w, t_bs, rel[bk])
        put(pe, pe.matmul, PS[:, bk, :], OHE[0:24, i, :], BS[:, 0:F0], start=True, stop=False)
        for k in range(2):
            m = put(pe, lambda k=k, p=p, bk=bk: pe.matmul(
                PS[:, bk, :], XS[:, p, k, :], W[:, bass.ds(hold["v"] * EXP0 + k * F0, F0)], start=False, stop=(k == 1)))
        tk = inc(m, own_sem(pe, "pe"))
        fl["xs"][p] = tk
        wait(act, tk, fl["hb"][p])
        t = C(act.activation, HB[:, p, 0:F0], PS[:, bk, :], ACT.Gelu)
        rel[bk] = t
        return t

    def up1(i, which, hold, lhs, t_x_, t_w):
        p, b0 = i % 2, 2 * which
        wait(pe, t_x_, t_w, rel[b0], rel[b0 + 1])
        for half in range(2):
            for k in range(2):
                o = k * 2 * F1 + which * F1 + half * 352
                m = put(pe, lambda k=k, half=half, o=o: pe.matmul(
                    PS[:, b0 + half, 0:352], lhs[k], W[:, bass.ds(hold["v"] * SLOT + o, 352)],
                    start=(k == 0), stop=(k == 1)))
        tk = inc(m, own_sem(pe, "pe"))
        hb = HB[:, p, :].rearrange("p (a n) -> p a n", a=2)
        if which == 0:
            wait(act, tk, fl["hb"][p])
            t = C(act.activation, hb, PS[:, 0:2, 0:352], ACT.Silu)
            fl["silu"] = t
        else:
            fl["xs"][p] = tk
            wait(dve, tk, fl["silu"])
            t = V(dve.tensor_tensor, hb, hb, PS[:, 2:4, 0:352], ALU.mult)
        rel[b0] = rel[b0 + 1] = t
        return t

    def clear_flags():
        nw_free[0] = None
        fl.clear()
        fl.update(xl=[None] * 2, xs=[None] * 2, hb=[None] * 2, ht=[None] * 2, yo=[None], silu=None)

    def load0(e, after):
        wait(sp, after)
        o = e * EXP0
        wdma(f"wa{e}", W[:, o:o + 2 * F0].rearrange("p (k n) -> p k n", k=2), A["L0_ffn_W1"][e].rearrange("(k p) n -> p k n", p=128))
        return wdma(f"wa{e}", W[:, o + 2 * F0:o + EXP0].rearrange("p (k n) -> p k n", n=D),
                    A["L0_ffn_W2"][e].rearrange("(k p) n -> p k n", p=128))

    def load1(e, after):
        wait(sp, after)
        g, u, d = (A["sgT"], A["suT"], A["sdT"]) if e == 0 else (A["rgT"][e - 1], A["ruT"][e - 1], A["rdT"][e - 1])
        o = e * SLOT
        up = W[:, o:o + 4 * F1].rearrange("p (k w n) -> p k w n", k=2, w=2)
        dn = W[:, o + 4 * F1:o + SLOT].rearrange("p (k n) -> p k n", n=D)
        wdma(f"wb{e}", up[:, :, 0, :], g.rearrange("(k p) n -> p k n", p=128))
        wdma(f"wb{e}", up[:, :, 1, :], u.rearrange("(k p) n -> p k n", p=128))
        wdma(f"wb{e}", dn[:, 0:5, :], d[0:640, :].rearrange("(k p) n -> p k n", p=128))
        return wdma(f"wb{e}", dn[0:64, 5, :], d[640:704, :])

    t_w0, t_w1 = {}, {}

    def prefetch0(i):
        if i == 0:
            wait(sp, t_kb0)
        for e in ((0, 1, 2), (3, 4, 5), (6, 7))[i]:
            t_w0[e] = load0(e, None)
        if i == 2:
            t_w0["xz"] = wdma("xz", xs.rearrange("(t p) c -> p t c", p=128), zero[:, :].unsqueeze(1).to_broadcast([128, TILES1, D]))

    def prefetch1(i):
        for e in ((0,), (1, 2), (3,))[i]:
            t_w1[e] = load1(e, t_ffn0)

    def ffn0(t_in):
        clear_flags()
        for e in (sp, act, pool, dve, pe):
            wait(e, t_in)
        t_mu1 = None
        p, oh, made = R1[:, :, 0:E0], OH[:, 0, :, :], {}
        for step in (softmax_rows(E0), first_max(p, E0, oh, gw[:, 0, :], rs[:, 4, :]), routes(E0, [oh], oh, COUNTS0, made)):
            for _ in step:
                if t_mu1 is None:
                    wait(act, t_m1)
                    t_mu1 = C(act.activation, mu1, m1i, ACT.Copy)
        t_te, t_way = made["te"], made["way"]
        t_s = scatter(1, [t_in], made["p"], None)
        V(dve.tensor_tensor, OHE[0:24], bb(tef[0:24, 0:TILES0], 128),
          rowe[:, :].unsqueeze(1).to_broadcast([24, TILES0, 128]), ALU.is_equal)
        t_oh = seen_dve()
        t_nk = normed_keys1()

        t_g = [None] * NT

        def tiles(n):
            def body():
                clear_flags()
                wait(pe, t_oh, t_te)
                hold = [{} for _ in range(n)]
                t_l = {0: load_x(0, t_s), 1: load_x(1, t_s)}
                t_x_ = {0: turn_x(0, t_l[0])}
                th = None
                keys = {}
                steps = masks_keys1(t_nk, t_s, t_mu1, keys)
                for i in range(n):
                    if i:
                        t_ht = turn_h(i - 1, NJ0, F0, th)
                    if i + 1 < n:
                        t_x_[i + 1] = turn_x(i + 1, t_l[i + 1])
                    if i + 2 < n:
                        t_l[i + 2] = load_x(i + 2, t_s)
                    put(pe, lambda i=i: expert(i, hold[i], E0))
                    th = up0(i, hold[i], t_x_[i], [t_w0[e] for e in range(min(i + 1, E0))])
                    if i:
                        store_y(i - 1, down(i - 1, NJ0, F0, hold[i - 1], 2 * F0, EXP0, t_ht, True))
                    next(steps, None)
                t_ht = turn_h(n - 1, NJ0, F0, th)
                t_y = store_y(n - 1, down(n - 1, NJ0, F0, hold[n - 1], 2 * F0, EXP0, t_ht, True))
                for t in range(NT):
                    t_g[t] = gather(0, t, XN[:, t, :], t_y, n)
                return [t_y, keys["ks"], keys["kb"], keys["flag"]]
            return body

        t = branch(tei[0:1, TILES1:TILES1 + 1], [t_way, t_oh], [(w, tiles(n)) for w, n in enumerate(COUNTS0)])
        for i in range(NT):
            wait(dve, t_g[i])
            t = V(dve.scalar_tensor_tensor, X[:, i, :], XN[:, i, :], gw[:, 0, i:i + 1], X[:, i, :], ALU.mult, ALU.add)
        return t

    def ffn1(t_in):
        clear_flags()
        for e in (sp, act, pool, dve, pe):
            wait(e, t_in)
        for e in range(4, 6):
            t_w1[e] = load1(e, t_in)
        made = {}

        def routing():
            p = R1[:, :, 0:E1]
            o1, o2, oa = (OH[:, i, :, 0:E1] for i in range(3))
            g1, g2 = gw[:, 0, :], gw[:, 1, :]
            yield from softmax_rows(E1)
            yield from first_max(p, E1, o1, g1, rs[:, 5, :])
            VC(dve.scalar_tensor_tensor, LG[:, :, 0:E1], o1, -4.0, p, ALU.mult, ALU.add)
            yield from first_max(LG[:, :, 0:E1], E1, o2, g2, rs[:, 5, :])
            VC(dve.tensor_tensor, oa, o1, o2, ALU.add)
            yield from routes(E1, [o1, o2], oa, COUNTS1, made)
            made["s"] = scatter(2, [t_in], made["p"], None)
            for e in range(6, 8):
                t_w1[e] = load1(e, made["s"])
            yield
            VC(dve.tensor_tensor, rs[:, 0, :], g1, g2, ALU.add)
            VC(dve.reciprocal, rs[:, 0, :], rs[:, 0, :])
            VC(dve.tensor_tensor, g1, g1, rs[:, 0, :], ALU.mult)
            made["gw"] = VC(dve.tensor_tensor, g2, g2, rs[:, 0, :], ALU.mult)

        steps = routing()

        def advance(n):
            for _ in range(n):
                next(steps, None)

        def lhs(i):
            if i < NT:
                return [XT[:, k, i * 128:(i + 1) * 128] for k in range(2)]
            return [XS[:, i % 2, k, :] for k in range(2)]

        def finish(i, th, hold):
            tk = down(i, NJ1, F1, hold, 4 * F1, SLOT, th, False)
            if i < NT:
                wait(dve, tk)
                rel[6] = V(dve.tensor_tensor, X[:, i, :], X[:, i, :], PS[:, 6, 0:D], ALU.add)
                return None
            return store_y(i - NT, tk)

        def pull(i, n):
            if NT <= i < n:
                j = i - NT
                wait(sp, made["s"], fl["xl"][i % 2])
                return dma(sp, f"xl{i % 2}", XL[:, i % 2, :], xs[j * 128:(j + 1) * 128, :])

        shared = {"v": 0}
        last = None
        for i in range(NT):
            up1(i, 0, shared, lhs(i), t_in, t_w1[0])
            advance(1)
            if i:
                th = turn_h(i - 1, NJ1, F1, last)
                advance(1)
            last = up1(i, 1, shared, lhs(i), None, None)
            advance(1)
            if i:
                finish(i - 1, th, shared)
            advance(1)
        advance(100)
        left = {k: list(v) if isinstance(v, list) else v for k, v in fl.items()}

        def tiles(ntile):
            def body():
                fl.update({k: list(v) if isinstance(v, list) else v for k, v in left.items()})
                wait(pe, made["te"])
                n = NT + ntile
                hold = {i: {} for i in range(NT, n)}
                hold[NT - 1] = shared
                t_l = {i: pull(i, n) for i in (NT, NT + 1)}
                t_x_ = {}
                prev = last
                for i in range(NT, n):
                    if i == NT:
                        th = turn_h(i - 1, NJ1, F1, prev)
                        t_x_[i] = turn_x(i, t_l[i])
                        finish(i - 1, th, hold[i - 1])
                    put(pe, lambda i=i: expert1(i - NT, hold[i]))
                    up1(i, 0, hold[i], lhs(i), t_x_[i], [t_w1[e] for e in range(1, min(7, i - NT + 1) + 1)])
                    t_l[i + 2] = pull(i + 2, n)
                    if i > NT:
                        th = turn_h(i - 1, NJ1, F1, prev)
                    if i + 1 < n:
                        t_x_[i + 1] = turn_x(i + 1, t_l[i + 1])
                    new = up1(i, 1, hold[i], lhs(i), None, None)
                    if i > NT:
                        t_y = finish(i - 1, th, hold[i - 1])
                    prev = new
                t_y = finish(n - 1, turn_h(n - 1, NJ1, F1, prev), hold[n - 1])
                Y2 = XT[:, :, :].rearrange("p k n -> p (k n)").rearrange("p (t c) -> p t c", c=D)
                o_v = out.rearrange("(t p) c -> p t c", p=128)
                for t in range(NT):
                    ta = gather(0, t, XN[:, t, :], t_y, ntile)
                    tb = gather(1, t, Y2[:, t, :], t_y, ntile)
                    wait(dve, ta)
                    VC(dve.scalar_tensor_tensor, X[:, t, :], XN[:, t, :], gw[:, 0, t:t + 1], X[:, t, :], ALU.mult, ALU.add)
                    wait(dve, tb)
                    tf = V(dve.scalar_tensor_tensor, X[:, t, :], Y2[:, t, :], gw[:, 1, t:t + 1], X[:, t, :], ALU.mult, ALU.add)
                    wait(act, tf)
                    t_out = dma(act, "out", o_v[:, t, :], X[:, t, :])
                return t_out
            return body

        return branch(tei[0:1, TILES1:TILES1 + 1], [made["way"], made["gw"]], [(w, tiles(n)) for w, n in enumerate(COUNTS1)])

    def expert1(i, hold):
        hold["v"] = pe.value_load(tei[0:1, i:i + 1], min_val=0, max_val=E1 - 1) + 1

    wait(dve, t_id)
    t_idb = V(dve.tensor_copy, junk[:, :], ident[:, 0:1])
    t_wgT = expert_directions()
    t_ks0 = keys0()
    toks, t_xt0 = ln_turned([t_x[0]] * 4 + [t_x[1]] * 4)
    wait(dve, t_m0)
    t_mu0 = V(dve.tensor_scalar, mu0, m0i, 0.0, None, ALU.not_equal)
    t_q0 = [queries(0, b, t_xt0[b], 0, None) for b in range(NB)]
    key_counts(0, 0, mu0, t_mu0)
    t_kb0 = mask_row(0, 1, pool)
    t_flag0 = flag_of(0, 1)
    t_in0 = [t_flag0, t_x, t_ks0, t_q0, t_kb0, t_one0, t_wgT, t_idb, t_bs]
    t = branch(flags[0:1, 0:1], t_flag0,
               [(1, attention_fast(0, t_in0, [t_ks0, t_kb0, t_one0], t_q0, prefetch0)),
                (0, attention_general(0, t_in0, prefetch0))])
    wait(sp, t)
    t_m1 = dma(sp, "m1", m1i, A["mask1"].rearrange("b (q p) n -> p (b q) n", p=128))
    t_wp = load_proj(1, t)
    t_ffn0 = ffn0(t)
    t_in1 = [t_ffn0, t_wp]
    t = branch(flags[0:1, 1:2], t_ffn0,
               [(1, attention_fast(1, t_in1, None, None, prefetch1)), (0, attention_general(1, t_in1, prefetch1))])
    t = ffn1(t)
    wait(sp, t)
    segments.append((state["queue"], None))

    def choose(e, v, made):
        value, queue = made[0]
        if len(made) == 1:
            issue(queue[id(e)])
            return
        with e.If(v == value):
            issue(queue[id(e)])
        with e.Else():
            choose(e, v, made[1:])

    for what, made in segments:
        for e in engines:
            if made is None:
                issue(what[id(e)])
            else:
                choose(e, e.value_load(what, min_val=0, max_val=2), made)
    ctx.close()
def laid_out(i, np):
    c = np.ascontiguousarray
    a = {
        "x": c(i["x"]).reshape(NB * S, D),
        "ctxT": c(i["ctx_1024"].transpose(2, 0, 1)).reshape(D, NB * SK),
        "mask0": c(i["mask_1x1xSxS2_ik0"]).reshape(S, SK),
        "mask1": c(i["mask_BxSxS2_bk0"]),
    }
    for n in ("Wq", "Wk", "Wv", "Wo"):
        a[f"L0_xattn_{n}T"] = c(i[f"L0_xattn_{n}"].T)
    for n in ("L0_xattn_bq", "L0_xattn_bk", "L0_xattn_bv", "L0_xattn_bo", "L0_ffn_w_red", "L0_ffn_wg", "L0_ffn_W1",
              "L0_ffn_b1", "L0_ffn_W2", "L0_ffn_b2", "L1_xattn_Wq", "L1_xattn_Wk", "L1_xattn_Wv", "L1_xattn_gq",
              "L1_xattn_bq", "L1_xattn_gk", "L1_xattn_bk", "L1_xattn_gv", "L1_xattn_bv", "L1_ffn_rb"):
        a[n] = c(i[n])
    a["L1_ffn_wrT"] = c(i["L1_ffn_wr"].T)
    for n in ("sg", "su", "sd"):
        a[n + "T"] = c(i["L1_ffn_" + n].T)
    for n in ("rg", "ru", "rd"):
        a[n + "T"] = c(i["L1_ffn_" + n].transpose(0, 2, 1))
    a["ones"] = np.full((1, H * NB * S), 0x3F80, np.uint16)
    return a


def kernel(**inputs):
    import numpy as np
    import concourse.bacc as bacc
    from concourse.bass_utils import run_bass_kernel_spmd

    nc = bacc.Bacc("TRN2", target_bir_lowering=False, num_devices=1)
    arrays = laid_out({k: np.asarray(v) for k, v in inputs.items()}, np)
    aps = {n: nc.dram_tensor("in_" + n, v.shape, mybir.dt.from_np(v.dtype), kind="ExternalInput").ap()
           for n, v in arrays.items()}
    out = nc.dram_tensor("out", [NB * S, D], F32, kind="ExternalOutput").ap()
    build(nc, aps, out)
    r = run_bass_kernel_spmd(nc, [{"in_" + n: v for n, v in arrays.items()}], core_ids=[0])
    return r.results[0]["out"].reshape(NB, S, D)
```
